# Optimizing a Trainium2 kernel written in Bass

```python
import numpy as np
import jax
import jax.numpy as jnp

def _softmax(x, axis=-1):
    return jax.nn.softmax(x, axis=axis)

def _gelu(x):
    return jax.nn.gelu(x, approximate=True)

def _silu(x):
    return jax.nn.silu(x)

def _sigmoid(x):
    return jax.nn.sigmoid(x)

def _layernorm(x, axis=-1, eps=1e-05):
    m = jnp.mean(x, axis=axis, keepdims=True)
    v = jnp.var(x, axis=axis, keepdims=True)
    return (x - m) / jnp.sqrt(v + eps)

def _scatter_add(tgt, idx, src, axis=0):
    return tgt.at[idx].add(src)

def _segment_sum(src, seg, n):
    return jax.ops.segment_sum(src, seg, n)
kernel_name = 'mk_gps_d1_gnn_r8_20bd48'

def setup_inputs(seed: int=0):
    np.random.seed(seed)
    _w = jnp.asarray

    def _rec_inputs():
        import jax
        import jax.numpy as jnp
        _gk = jax.random.key(seed)
        x = -0.0001126 + 1 * jax.random.normal(jax.random.fold_in(_gk, 1), (1250, 768), jnp.float32)
        _s = jax.random.randint(jax.random.fold_in(_gk, 2), (20000,), 0, 1250, jnp.int32)
        _d = jax.random.randint(jax.random.fold_in(_gk, 3), (20000,), 0, 1250, jnp.int32)
        _loop = jnp.arange(1250, dtype=jnp.int32)
        src = jnp.concatenate([_s, _d, _loop])
        dst = jnp.concatenate([_d, _s, _loop])
        _o = jnp.argsort(dst, stable=True)
        src = src[_o]
        dst = dst[_o]
        edge_type_34 = jax.random.randint(jax.random.fold_in(_gk, 12), (41250,), 0, 34, jnp.int32)
        return (x, src, dst, edge_type_34)
    x, src, dst, edge_type_34 = _rec_inputs()

    def _L0_gnn_setup():
        import jax, jax.numpy as jnp
        import numpy as np
        N_NODES = 1250
        N_EDGES = 12500
        N_REL = 34
        DIM = 768

        def _graph_encoder(x, edge_index, edge_type, W_rel, W_root, b_rgcn, W_gcn, b_gcn):
            n = x.shape[0]
            src, dst = (edge_index[0], edge_index[1])
            ones = jnp.ones((src.shape[0],), dtype=x.dtype)
            seg = edge_type * n + dst
            agg = jax.ops.segment_sum(x[src], seg, num_segments=N_REL * n)
            cnt = jax.ops.segment_sum(ones, seg, num_segments=N_REL * n)
            mean = agg.reshape(N_REL, n, -1) / jnp.maximum(cnt, 1.0).reshape(N_REL, n, 1)
            h1 = jnp.einsum('rni,rio->no', mean, W_rel) + x @ W_root + b_rgcn
            xw = h1 @ W_gcn
            deg = jax.ops.segment_sum(ones, dst, num_segments=n) + 1.0
            dinv = jax.lax.rsqrt(deg)
            norm = dinv[src] * dinv[dst]
            out = jax.ops.segment_sum(xw[src] * norm[:, None], dst, num_segments=n)
            out = out + xw * (dinv * dinv)[:, None]
            return out + b_gcn
        key = jax.random.key(seed)
        ks = jax.random.split(key, 6)
        scale = 1.0 / np.sqrt(DIM)
        x = jax.random.normal(ks[0], (N_NODES, DIM), dtype=jnp.float32)
        edge_index = jax.random.randint(ks[1], (2, N_EDGES), 0, N_NODES, dtype=jnp.int32)
        edge_type = jax.random.randint(ks[2], (N_EDGES,), 0, N_REL, dtype=jnp.int32)
        W_rel = jax.random.normal(ks[3], (N_REL, DIM, DIM), dtype=jnp.float32) * scale
        W_root = jax.random.normal(ks[4], (DIM, DIM), dtype=jnp.float32) * scale
        b_rgcn = jnp.zeros((DIM,), dtype=jnp.float32)
        W_gcn = jax.random.normal(ks[5], (DIM, DIM), dtype=jnp.float32) * scale
        b_gcn = jnp.zeros((DIM,), dtype=jnp.float32)
        return {'x': x, 'edge_index': edge_index, 'edge_type': edge_type, 'W_rel': W_rel, 'W_root': W_root, 'b_rgcn': b_rgcn, 'W_gcn': W_gcn, 'b_gcn': b_gcn}
    _L0_gnn_all = _L0_gnn_setup()
    _L0_gnn_in = {k: v for k, v in _L0_gnn_all.items() if k in ('W_rel', 'W_root', 'b_rgcn', 'W_gcn', 'b_gcn')}
    del _L0_gnn_all

    def _L0_mix_setup():
        import jax, jax.numpy as jnp
        import numpy as np
        B, N, D = (4, 1024, 768)
        H, DH = (12, 64)
        INNER = H * DH
        key = jax.random.key(seed)
        k0, k1, k2 = jax.random.split(key, 3)
        return {'x': jax.random.normal(k0, (B, N, D), dtype=jnp.float32), 'w_qkv': jax.random.normal(k1, (D, INNER), dtype=jnp.float32) * 0.02, 'temp': jnp.ones((H, 1), dtype=jnp.float32), 'w_out': jax.random.normal(k2, (INNER, D), dtype=jnp.float32) * 0.02, 'b_out': jnp.zeros((D,), dtype=jnp.float32)}
    _L0_mix_all = _L0_mix_setup()
    _L0_mix_in = {k: v for k, v in _L0_mix_all.items() if k in ('w_qkv', 'temp', 'w_out', 'b_out')}
    del _L0_mix_all

    def _L0_ffn_setup():
        import jax, jax.numpy as jnp
        import numpy as np
        B, L, D, H, F = (4, 256, 768, 12, 384)
        ROUTE_FRAC = 0.15
        LN_EPS = 1e-05

        def _ln(x, g, b):
            m = jnp.mean(x, axis=-1, keepdims=True)
            v = jnp.mean((x - m) ** 2, axis=-1, keepdims=True)
            return (x - m) * jax.lax.rsqrt(v + LN_EPS) * g + b
        key = jax.random.key(seed)
        ks = jax.random.split(key, 20)
        s = 0.02
        return {'hidden_states': jax.random.normal(ks[0], (B, L, D), dtype=jnp.float32), 'g1': jnp.ones((D,), jnp.float32), 'b1': jnp.zeros((D,), jnp.float32), 'g2': jnp.ones((D,), jnp.float32), 'b2': jnp.zeros((D,), jnp.float32), 'Wr': jax.random.normal(ks[1], (D,), jnp.float32) * s, 'br': jnp.zeros((), jnp.float32), 'Wq': jax.random.normal(ks[2], (D, D), jnp.float32) * s, 'bq': jnp.zeros((D,), jnp.float32), 'Wk': jax.random.normal(ks[3], (D, D), jnp.float32) * s, 'bk': jnp.zeros((D,), jnp.float32), 'Wv': jax.random.normal(ks[4], (D, D), jnp.float32) * s, 'bv': jnp.zeros((D,), jnp.float32), 'Wo': jax.random.normal(ks[5], (D, D), jnp.float32) * s, 'bo': jnp.zeros((D,), jnp.float32), 'Wm': jax.random.normal(ks[6], (D, D), jnp.float32) * s, 'bm': jnp.zeros((D,), jnp.float32), 'W1': jax.random.normal(ks[7], (D, F), jnp.float32) * s, 'bf1': jnp.zeros((F,), jnp.float32), 'W2': jax.random.normal(ks[8], (F, D), jnp.float32) * s, 'bf2': jnp.zeros((D,), jnp.float32)}
    _L0_ffn_all = _L0_ffn_setup()
    _L0_ffn_in = {k: v for k, v in _L0_ffn_all.items() if k in ('g1', 'b1', 'g2', 'b2', 'Wr', 'br', 'Wq', 'bq', 'Wk', 'bk', 'Wv', 'bv', 'Wo', 'bo', 'Wm', 'bm', 'W1', 'bf1', 'W2', 'bf2')}
    del _L0_ffn_all
    return {'x': x, 'src': src, 'dst': dst, 'edge_type_34': edge_type_34, 'L0_gnn_W_rel': _L0_gnn_in['W_rel'], 'L0_gnn_W_root': _L0_gnn_in['W_root'], 'L0_gnn_b_rgcn': _L0_gnn_in['b_rgcn'], 'L0_gnn_W_gcn': _L0_gnn_in['W_gcn'], 'L0_gnn_b_gcn': _L0_gnn_in['b_gcn'], 'L0_mix_w_qkv': _L0_mix_in['w_qkv'], 'L0_mix_temp': _L0_mix_in['temp'], 'L0_mix_w_out': _L0_mix_in['w_out'], 'L0_mix_b_out': _L0_mix_in['b_out'], 'L0_ffn_g1': _L0_ffn_in['g1'], 'L0_ffn_b1': _L0_ffn_in['b1'], 'L0_ffn_g2': _L0_ffn_in['g2'], 'L0_ffn_b2': _L0_ffn_in['b2'], 'L0_ffn_Wr': _L0_ffn_in['Wr'], 'L0_ffn_br': _L0_ffn_in['br'], 'L0_ffn_Wq': _L0_ffn_in['Wq'], 'L0_ffn_bq': _L0_ffn_in['bq'], 'L0_ffn_Wk': _L0_ffn_in['Wk'], 'L0_ffn_bk': _L0_ffn_in['bk'], 'L0_ffn_Wv': _L0_ffn_in['Wv'], 'L0_ffn_bv': _L0_ffn_in['bv'], 'L0_ffn_Wo': _L0_ffn_in['Wo'], 'L0_ffn_bo': _L0_ffn_in['bo'], 'L0_ffn_Wm': _L0_ffn_in['Wm'], 'L0_ffn_bm': _L0_ffn_in['bm'], 'L0_ffn_W1': _L0_ffn_in['W1'], 'L0_ffn_bf1': _L0_ffn_in['bf1'], 'L0_ffn_W2': _L0_ffn_in['W2'], 'L0_ffn_bf2': _L0_ffn_in['bf2']}

def reference(x, src, dst, edge_type_34, L0_gnn_W_rel, L0_gnn_W_root, L0_gnn_b_rgcn, L0_gnn_W_gcn, L0_gnn_b_gcn, L0_mix_w_qkv, L0_mix_temp, L0_mix_w_out, L0_mix_b_out, L0_ffn_g1, L0_ffn_b1, L0_ffn_g2, L0_ffn_b2, L0_ffn_Wr, L0_ffn_br, L0_ffn_Wq, L0_ffn_bq, L0_ffn_Wk, L0_ffn_bk, L0_ffn_Wv, L0_ffn_bv, L0_ffn_Wo, L0_ffn_bo, L0_ffn_Wm, L0_ffn_bm, L0_ffn_W1, L0_ffn_bf1, L0_ffn_W2, L0_ffn_bf2):
    import jax
    import jax.numpy as jnp

    def _L0_gnn_ref(x, edge_index, edge_type, W_rel, W_root, b_rgcn, W_gcn, b_gcn):
        import jax, jax.numpy as jnp
        import numpy as np
        N_NODES = 1250
        N_EDGES = 12500
        N_REL = 34
        DIM = 768

        def _graph_encoder(x, edge_index, edge_type, W_rel, W_root, b_rgcn, W_gcn, b_gcn):
            n = x.shape[0]
            src, dst = (edge_index[0], edge_index[1])
            ones = jnp.ones((src.shape[0],), dtype=x.dtype)
            seg = edge_type * n + dst
            agg = jax.ops.segment_sum(x[src], seg, num_segments=N_REL * n)
            cnt = jax.ops.segment_sum(ones, seg, num_segments=N_REL * n)
            mean = agg.reshape(N_REL, n, -1) / jnp.maximum(cnt, 1.0).reshape(N_REL, n, 1)
            h1 = jnp.einsum('rni,rio->no', mean, W_rel) + x @ W_root + b_rgcn
            xw = h1 @ W_gcn
            deg = jax.ops.segment_sum(ones, dst, num_segments=n) + 1.0
            dinv = jax.lax.rsqrt(deg)
            norm = dinv[src] * dinv[dst]
            out = jax.ops.segment_sum(xw[src] * norm[:, None], dst, num_segments=n)
            out = out + xw * (dinv * dinv)[:, None]
            return out + b_gcn
        return _graph_encoder(x, edge_index, edge_type, W_rel, W_root, b_rgcn, W_gcn, b_gcn)

    def _L0_mix_ref(x, w_qkv, temp, w_out, b_out):
        import jax, jax.numpy as jnp
        import numpy as np
        B, N, D = (4, 1024, 768)
        H, DH = (12, 64)
        INNER = H * DH
        b, n, _ = x.shape
        h = temp.shape[0]
        w = (x @ w_qkv).reshape(b, n, h, -1).transpose(0, 2, 1, 3)
        norm = jnp.sqrt(jnp.sum(w * w, axis=2, keepdims=True))
        w_normed = w / jnp.maximum(norm, 1e-12)
        logits = jnp.sum(w_normed * w_normed, axis=-1) * temp
        Pi = jax.nn.softmax(logits, axis=-1)
        Pi_norm = Pi / (jnp.sum(Pi, axis=-1, keepdims=True) + 1e-08)
        dots = jnp.einsum('bhn,bhnd->bhd', Pi_norm, w * w)[:, :, None, :]
        attn = 1.0 / (1.0 + dots)
        out = -(w * Pi[..., None]) * attn
        out = out.transpose(0, 2, 1, 3).reshape(b, n, -1)
        return out @ w_out + b_out

    def _L0_ffn_ref(hidden_states, g1, b1, g2, b2, Wr, br, Wq, bq, Wk, bk, Wv, bv, Wo, bo, Wm, bm, W1, bf1, W2, bf2):
        import jax, jax.numpy as jnp
        import numpy as np
        B, L, D, H, F = (4, 256, 768, 12, 384)
        ROUTE_FRAC = 0.15
        LN_EPS = 1e-05

        def _ln(x, g, b):
            m = jnp.mean(x, axis=-1, keepdims=True)
            v = jnp.mean((x - m) ** 2, axis=-1, keepdims=True)
            return (x - m) * jax.lax.rsqrt(v + LN_EPS) * g + b
        b, l, d = hidden_states.shape
        dh = d // H
        normed = _ln(hidden_states, g1, b1)
        scores = jax.nn.sigmoid(jnp.einsum('bld,d->bl', normed, Wr) + br)
        k = max(1, int(round(ROUTE_FRAC * l)))
        _, idx = jax.lax.top_k(-scores, k)
        attn_mask = jnp.zeros((b, l), bool).at[jnp.arange(b)[:, None], idx].set(True)
        q = (normed @ Wq + bq).reshape(b, l, H, dh)
        kk = (normed @ Wk + bk).reshape(b, l, H, dh)
        v = (normed @ Wv + bv).reshape(b, l, H, dh)
        logits = jnp.einsum('blhd,bmhd->bhlm', q, kk) / jnp.sqrt(jnp.float32(dh))
        probs = jax.nn.softmax(logits, axis=-1)
        ctx = jnp.einsum('bhlm,bmhd->blhd', probs, v).reshape(b, l, d)
        attn_out = ctx @ Wo + bo
        w = scores / (jnp.sum(scores, axis=1, keepdims=True) + 1e-06)
        pooled = jnp.einsum('bl,bld->bd', w, normed)
        mix_out = (normed + scores[..., None] * pooled[:, None, :]) @ Wm + bm
        merged = jnp.where(attn_mask[..., None], attn_out, mix_out)
        h = hidden_states + merged
        n2 = _ln(h, g2, b2)
        ffn = jax.nn.gelu(n2 @ W1 + bf1, approximate=False) @ W2 + bf2
        return h + ffn
    edge_index = jnp.stack([src, dst])
    xn = _layernorm(x, axis=-1)
    x = x + _L0_gnn_ref(xn, edge_index, edge_type_34, L0_gnn_W_rel, L0_gnn_W_root, L0_gnn_b_rgcn, L0_gnn_W_gcn, L0_gnn_b_gcn) + _L0_mix_ref(xn[None], L0_mix_w_qkv, L0_mix_temp, L0_mix_w_out, L0_mix_b_out)[0]
    x = x + _L0_ffn_ref(_layernorm(x, axis=-1)[None], L0_ffn_g1, L0_ffn_b1, L0_ffn_g2, L0_ffn_b2, L0_ffn_Wr, L0_ffn_br, L0_ffn_Wq, L0_ffn_bq, L0_ffn_Wk, L0_ffn_bk, L0_ffn_Wv, L0_ffn_bv, L0_ffn_Wo, L0_ffn_bo, L0_ffn_Wm, L0_ffn_bm, L0_ffn_W1, L0_ffn_bf1, L0_ffn_W2, L0_ffn_bf2)[0]
    return x

_drawn_inputs = setup_inputs


def setup_inputs(seed=0):
    import zlib

    import numpy as np

    out = dict(_drawn_inputs(seed))
    spreads = {'L0_gnn_b_rgcn': (0.0, 0.1),
     'L0_gnn_b_gcn': (0.0, 0.1),
     'L0_mix_temp': (1.0, 0.6),
     'L0_mix_b_out': (0.0, 0.1),
     'L0_ffn_g1': (1.0, 0.2),
     'L0_ffn_b1': (0.0, 0.1),
     'L0_ffn_g2': (1.0, 0.6),
     'L0_ffn_b2': (0.0, 0.8),
     'L0_ffn_bq': (0.0, 0.8),
     'L0_ffn_bk': (0.0, 2.0),
     'L0_ffn_bv': (0.0, 0.8),
     'L0_ffn_bo': (0.0, 0.478),
     'L0_ffn_bm': (0.0, 0.303),
     'L0_ffn_bf1': (0.0, 0.734),
     'L0_ffn_bf2': (0.0, 0.278)}
    factors = {'L0_mix_w_qkv': 8.0,
     'L0_mix_w_out': 8.0,
     'L0_ffn_Wq': 8.0,
     'L0_ffn_Wk': 8.0,
     'L0_ffn_Wv': 5.288,
     'L0_ffn_Wo': 4.097}
    for name, (base, spread) in spreads.items():
        noise = np.random.default_rng([zlib.crc32(name.encode()), seed]).standard_normal(out[name].shape)
        drawn = base * np.exp(spread * noise) if base else spread * noise
        out[name] = jnp.asarray(drawn.astype(out[name].dtype))
    for name, factor in factors.items():
        out[name] = (out[name] * factor).astype(out[name].dtype)
    return out
```

```python
from contextlib import ExitStack
import math

import concourse.bass as bass
from concourse import mybir

ALU = mybir.AluOpType
ACT = mybir.ActivationFunctionType
AX = mybir.AxisListType
F32 = mybir.dt.float32
F32R = mybir.dt.float32r
F16 = mybir.dt.float16
I32 = mybir.dt.int32
U32 = mybir.dt.uint32
U16 = mybir.dt.uint16

N, D = 1250, 768
NT, T = 125, 10
KC = D // 128
HALF = D // 2
E = 41250
EC = E // NT
R = 34
NREL = R + 2
EB = 128
G = 2
SBE = EB * G
NSB = 2 * math.ceil((E // SBE + T) / 2)
NB = NSB * G
NBP = NB + 2 * G
H, DH = 12, 64
TOP = int(round(0.15 * N))
TH = TOP // 2
FF = 384
FK = FF // 128
EPS = 1e-5
MAGIC = 12582912.0
COLS = [(0, 416), (416, 416), (832, 418)]


SCRATCH = {
    "y": (NREL * N, D),
    "table": (EB * NBP, 4),
    "x1": (N, D),
    "hidden": (N, D),
    "mix": (N, D),
    "hf": (N, D),
    "score": (N,),
    "rank": (N,),
}


class Chain:

    def __init__(self, eng, sem):
        self.eng, self.sem, self.n, self.i, self.per = eng, sem, 0, None, 0

    def __call__(self, ins):
        self.n += 1
        ins.then_inc(self.sem, 1)
        self.wait()

    def wait(self):
        self.eng.wait_ge(self.sem, self.n if self.i is None else self.i * self.per + self.n)

    def enter(self, i, per):
        self.i, self.per, self.start = i, per, self.n

    def leave(self, times):
        assert self.n - self.start == self.per, (self.n - self.start, self.per)
        self.n = self.start + self.per * times
        self.i = None


def build(nc, a, out, scr):
    stack = ExitStack()
    with stack, nc.allow_non_contiguous_dma(reason="bias columns and 1250 scores, a few KB"):
        _build(nc, a, out, scr, stack)


def _build(nc, a, out, scr, top):
    def allocate(ctx, **where):
        def sb(name, shape, dt=F32):
            return ctx.enter_context(nc.sbuf_tensor(name, shape, dt, **where))
        return sb

    live = []

    def sem(name):
        live.append(nc.alloc_semaphore(name=name))
        return live[-1]

    def recycle():
        nc.clear_and_free_semaphores(live)
        live.clear()
        nc.all_engine_barrier()

    def sems(name, n):
        return [sem(f"{name}{i}") for i in range(n)]

    psum = top.enter_context(nc.psum_tensor("psum", [128, 8, 512], F32))

    def wide(slot, rows=NT, w=HALF):
        return psum[0:rows, 2 * slot:2 * slot + 2, 0:w]

    def halves(ap):
        return ap.rearrange("p (h n) -> p h n", h=2)

    tiled = lambda ap: ap.rearrange("(t p) d -> p t d", p=NT)
    chunked = lambda ap: ap.rearrange("(k p) n -> p k n", p=128)
    spread = lambda ap, rows: ap.partition_broadcast(rows)

    sb0 = allocate(top)
    ident = sb0("ident", [128, 128])
    identh = sb0("identh", [128, 128], F16)
    ones = sb0("ones", [128, 128])
    iota16 = sb0("iota16", [128, N], F16)
    dinv = sb0("dinv", [NT, T])
    prefix = sb0("prefix", [NT, NT])

    def stats(dve, link, src, tmp, mv, t):
        for h in range(2):
            ins = nc.vector.bn_stats(tmp[:, t, h * 6:h * 6 + 6], src[:, t, h * HALF:(h + 1) * HALF])
            link(ins)
        link(nc.vector.bn_aggr(mv[:, t, :], tmp[:, t, :]))

    def split_mm(o, lh, ll, rh, rl, start, stop):
        nc.tensor.matmul(o, lh, rh, start=start, stop=False)
        nc.tensor.matmul(o, lh, rl, start=False, stop=False)
        return nc.tensor.matmul(o, ll, rh, start=False, stop=stop)

    def rows_mm(slot, ah, al, wh, wl, cols, kc=KC):
        last = None
        for k in range(kc):
            for h in range(2):
                last = split_mm(psum[0:cols.stop - cols.start, 2 * slot + h, 0:HALF], ah[:, k, cols], al[:, k, cols],
                                wh[:, k, h * HALF:(h + 1) * HALF], wl[:, k, h * HALF:(h + 1) * HALF],
                                k == 0, k == kc - 1)
        return last

    def polish(link, r, v, tmp):
        link(nc.vector.tensor_tensor(tmp, r, r, ALU.mult))
        link(nc.vector.tensor_tensor(tmp, tmp, v, ALU.mult))
        link(nc.vector.tensor_scalar(tmp, tmp, -0.5, 1.5, ALU.mult, ALU.add))
        link(nc.vector.tensor_tensor(r, r, tmp, ALU.mult))

    def norm_block(tag, src_dram, xs, then, sink=None):
        with ExitStack() as ctx:
            sb = allocate(ctx)
            tmp, mv = sb(tag + "tmp", [NT, T, 12]), sb(tag + "mv", [NT, T, 2])
            std, rstd = sb(tag + "std", [NT, T]), sb(tag + "rstd", [NT, T])
            var = sb(tag + "var", [NT, T])
            ld, st, sq, ch, co = (sem(tag + n) for n in ("loaded", "stats", "sqrt", "chain", "const"))
            block = ctx.enter_context(nc.Block())

            @block.sync
            def _(sp):
                if src_dram is not None:
                    sp.dma_start(xs[:, :, :], tiled(src_dram)).then_inc(ld, 16)

            @block.gpsimd
            def _(pool):
                if tag == "ln_x":
                    nc.gpsimd.memset(ident[:, :], 0.0).then_inc(co, 1)
                    nc.gpsimd.memset(identh[:, :], 0.0).then_inc(co, 1)
                    nc.gpsimd.memset(ones[:, :], 1.0).then_inc(co, 1)
                    pool.iota(iota16[:, :], pattern=[[1, N]], base=0, channel_multiplier=0,
                              allow_small_or_imprecise_dtypes=True).then_inc(co, 1)
                    pool.wait_ge(co, 4)
                    for m in (ident, identh):
                        nc.gpsimd.affine_select(out=m[:, :], in_=m[:, :], compare_op=ALU.not_equal, fill=1.0, base=0,
                                                pattern=[[-1, 128]], channel_multiplier=1).then_inc(co, 1)
                    nc.gpsimd.affine_select(out=prefix[:, :], in_=ones[0:NT, 0:NT], compare_op=ALU.is_gt, fill=0.0,
                                            base=0, pattern=[[1, NT]], channel_multiplier=-1).then_inc(co, 1)

            @block.scalar
            def _(act):
                act.wait_ge(st, 1)
                nc.scalar.activation(std[:, :], var[:, :], ACT.Sqrt).then_inc(sq, 1)

            @block.vector
            def _(dve):
                link = Chain(dve, ch)
                if src_dram is not None:
                    dve.wait_ge(ld, 16)
                for t in range(T):
                    stats(dve, link, xs, tmp, mv, t)
                nc.vector.tensor_scalar(var[:, :], mv[:, :, 1], EPS, None, ALU.add).then_inc(st, 1)
                dve.wait_ge(sq, 1)
                link(nc.vector.reciprocal(rstd[:, :], std[:, :]))
                polish(link, rstd[:, :], var[:, :], std[:, :])
                for t in range(T):
                    then(dve, link, t, mv[:, t, 0:1], rstd[:, t:t + 1])

    def transpose_block(tag, xs, ah, al):
        with ExitStack() as ctx:
            tr, hi, lo = (sem(tag + n) for n in ("transposed", "high", "low"))
            block = ctx.enter_context(nc.Block())

            def part(m, t):
                return m[:, :, t * NT:(t + 1) * NT].rearrange("p (h k) n -> p h k n", h=2)

            def src(t):
                return psum[:, 2 * (t % 4):2 * (t % 4) + 2, 0:3 * NT].rearrange("p h (k n) -> p h k n", k=3)

            @block.tensor
            def _(pe):
                for t in range(T):
                    if t >= 4:
                        pe.wait_ge(lo, 2 * (t - 3))
                    for k in range(KC):
                        o = psum[:, 2 * (t % 4) + k // 3, (k % 3) * NT:(k % 3 + 1) * NT]
                        last = nc.tensor.transpose(o, xs[:, t, k * 128:(k + 1) * 128], ident[0:NT, 0:NT])
                    last.then_inc(tr, 1)

            @block.scalar
            def _(act):
                for t in range(T):
                    act.wait_ge(tr, t + 1)
                    for h in range(2):
                        nc.scalar.activation(part(ah, t)[:, h], src(t)[:, h], ACT.Copy).then_inc(hi, 1)

            @block.vector
            def _(dve):
                for t in range(T):
                    dve.wait_ge(hi, 2 * t + 2)
                    for h in range(2):
                        nc.vector.tensor_tensor(part(al, t)[:, h], src(t)[:, h], part(ah, t)[:, h].bitcast(F32),
                                                ALU.subtract).then_inc(lo, 1)

    def rows_block(tag, ah, al, weights, sink, kc=KC, loads=(), stores=()):
        with ExitStack() as ctx:
            sb = allocate(ctx)
            raw = sb(tag + "raw", [128, kc, D])
            wh, wl = sb(tag + "wh", [128, kc, D], F32R), sb(tag + "wl", [128, kc, D], F32R)
            ld, hi, lo, mm, ev, ch, xt = (sem(tag + n) for n in ("loaded", "high", "low", "product", "taken", "chain", "extra"))
            block = ctx.enter_context(nc.Block())
            J = len(weights)

            @block.sync
            def _(sp):
                for j, w in enumerate(weights):
                    if j:
                        sp.wait_ge(lo, j)
                    sp.dma_start(raw[:, :, :], chunked(w)).then_inc(ld, 16)
                for to, src in loads:
                    sp.dma_start(to, src).then_inc(xt, 16)
                for n, (to, src) in enumerate(stores):
                    sp.wait_ge(ev, T * (len(weights) - 1) + n + 1)
                    sp.dma_start(to, src).then_inc(xt, 16)
                sp.wait_ge(xt, 16 * (len(loads) + len(stores))) if stores else None

            @block.scalar
            def _(act):
                for j in range(J):
                    act.wait_ge(ld, 16 * (j + 1))
                    if j:
                        act.wait_ge(mm, T * j)
                    nc.scalar.activation(wh[:, :, :], raw[:, :, :], ACT.Copy).then_inc(hi, 1)

            @block.vector
            def _(dve):
                link = Chain(dve, ch)
                if loads:
                    dve.wait_ge(xt, 16 * len(loads))
                for j in range(J):
                    dve.wait_ge(hi, j + 1)
                    nc.vector.tensor_tensor(wl[:, :, :], raw[:, :, :], wh[:, :, :].bitcast(F32),
                                            ALU.subtract).then_inc(lo, 1)
                    for t in range(T):
                        dve.wait_ge(mm, T * j + t + 1)
                        sink(dve, link, j, t, wide(t % 4)).then_inc(ev, 1)

            @block.tensor
            def _(pe):
                for j in range(J):
                    pe.wait_ge(lo, j + 1)
                    for t in range(T):
                        n = T * j + t
                        if n >= 4:
                            pe.wait_ge(ev, n - 3)
                            if j and t < 4:
                                pe.wait_ge(ev, T * j)
                        rows_mm(t % 4, ah, al, wh, wl, slice(t * NT, (t + 1) * NT), kc).then_inc(mm, 1)

    tab, tab_rows = scr["table"], scr["table"].rearrange("(q b) f -> q b f", q=EB)
    y = scr["y"]
    yv = y.rearrange("(i p) d -> i p d", p=NT)

    graph = ExitStack()
    sbg = allocate(graph)
    tile_of = sbg("tile_of", [1, NSB + 2], I32)
    rec = sbg("rec", [NT, EC, 5])
    xform = ExitStack()
    sbx = allocate(xform)
    ath, atl = sbx("ath", [128, KC, N], F32R), sbx("atl", [128, KC, N], F32R)

    with ExitStack() as ctx:
        xs = allocate(ctx)("xs", [NT, T, D])
        norm_block("ln_x", a["x"], xs, lambda dve, link, t, m, r: link(
            nc.vector.tensor_scalar(xs[:, t, :], xs[:, t, :], m, r, ALU.subtract, ALU.mult)))
        transpose_block("tr_x", xs, ath, atl)

    def order_block():
        with ExitStack() as ctx:
            sb = allocate(ctx)
            raw = sb("raw_edges", [NT, 3, EC], I32)
            edge = sb("edge", [NT, 3, EC])
            tid, pos, tmp = sb("tid", [NT, EC]), sb("pos", [NT, EC]), sb("tmp", [NT, EC])
            hot, inc = sb("hot", [NT, T, EC]), sb("inc", [NT, T, EC])
            one = sb("one_row", [NT, EC])
            total, both, nb, cum = sb("total", [NT, T]), sb("both", [NT, 2, T]), sb("nb", [NT, T]), sb("cum", [NT, T])
            off, first = sb("off", [NT, T]), sb("first", [NT, T])
            sbi, sbt = sb("sbi", [1, NSB + 2]), sb("sbt", [1, NSB + 2])
            fill = sb("fill", [128, NBP, 4])
            ld, ch, co, tt, px, fl, pr = (sem("ord_" + n) for n in ("loaded", "chain", "const", "total", "prefix", "fill", "prepared"))
            block = ctx.enter_context(nc.Block())

            @block.sync
            def _(sp):
                for f, name in enumerate(("dst", "src", "edge_type_34")):
                    sp.dma_start(raw[:, f, :], a[name].rearrange("(p c) -> p c", p=NT)).then_inc(ld, 16)
                sp.wait_ge(pr, 1)
                sp.dma_start(tab_rows, fill[:, :, :]).then_inc(fl, 16)
                sp.wait_ge(fl, 16)

            @block.gpsimd
            def _(pool):
                pool.iota(sbi[:, :], pattern=[[1, NSB + 2]], base=0, channel_multiplier=0,
                          allow_small_or_imprecise_dtypes=True).then_inc(co, 1)

            @block.tensor
            def _(pe):
                pe.wait_ge(tt, 1)
                nc.tensor.matmul(psum[0:NT, 0, 0:T], prefix[:, :], total[:, :], start=True, stop=True)
                nc.tensor.matmul(psum[0:NT, 1, 0:T], ones[0:NT, 0:NT], total[:, :], start=True, stop=True).then_inc(px, 1)

            @block.vector
            def _(dve):
                link = Chain(dve, ch)
                link(nc.vector.memset(fill[:, :, :].bitcast(I32), 0))
                link(nc.vector.memset(fill[:, :, 2:3], -1.0))
                nc.vector.memset(one[:, :], 1.0).then_inc(pr, 1)
                dve.wait_ge(pr, 1)
                dve.wait_ge(ld, 48)
                dve.wait_ge(co, 1)
                link(nc.vector.tensor_copy(edge[:, :, :], raw[:, :, :]))
                dst, src, typ = edge[:, 0, :], edge[:, 1, :], edge[:, 2, :]
                link(nc.vector.tensor_scalar(tid[:, :], dst, float(NT), None, ALU.is_ge))
                for k in range(2, T):
                    link(nc.vector.scalar_tensor_tensor(tid[:, :], dst, float(NT * k), tid[:, :], ALU.is_ge, ALU.add))
                for k in range(T):
                    link(nc.vector.tensor_scalar(hot[:, k, :], tid[:, :], float(k), None, ALU.is_equal))
                    link(nc.vector.tensor_tensor_scan(inc[:, k, :], one[:, :], hot[:, k, :], 0.0, ALU.mult, ALU.add))
                nc.vector.tensor_copy(total[:, :], inc[:, :, EC - 1]).then_inc(tt, 1)
                link(nc.vector.scalar_tensor_tensor(rec[:, :, 0].bitcast(U32), typ, float(N), src, ALU.mult, ALU.add))
                link(nc.vector.tensor_copy(rec[:, :, 1], src))
                link(nc.vector.scalar_tensor_tensor(rec[:, :, 2], tid[:, :], -float(NT), dst, ALU.mult, ALU.add))
                link(nc.vector.tensor_copy(rec[:, :, 3], typ))
                dve.wait_ge(px, 1)
                link(nc.vector.tensor_copy(both[:, 0, :], psum[0:NT, 0, 0:T]))
                link(nc.vector.tensor_copy(both[:, 1, :], psum[0:NT, 1, 0:T]))
                link(nc.vector.tensor_scalar(nb[:, :], both[:, 1, :], 1.0 / SBE, (SBE - 1.0) / SBE - 0.5 + 0.5 / SBE,
                                             ALU.mult, ALU.add))
                link(nc.vector.tensor_scalar(nb[:, :], nb[:, :], MAGIC, None, ALU.add))
                link(nc.vector.tensor_scalar(nb[:, :], nb[:, :], MAGIC, None, ALU.subtract))
                link(nc.vector.tensor_tensor_scan(cum[:, :], one[:, 0:T], nb[:, :], 0.0, ALU.mult, ALU.add))
                link(nc.vector.tensor_tensor(first[:, :], cum[:, :], nb[:, :], ALU.subtract))
                link(nc.vector.tensor_scalar(off[:, :], first[:, :], float(SBE), -1.0, ALU.mult, ALU.add))
                link(nc.vector.tensor_tensor(off[:, :], off[:, :], both[:, 0, :], ALU.add))
                for k in range(T):
                    dest = pos if k == 0 else tmp
                    link(nc.vector.scalar_tensor_tensor(dest[:, :], inc[:, k, :], off[:, k:k + 1], hot[:, k, :], ALU.add, ALU.mult))
                    if k:
                        link(nc.vector.tensor_tensor(pos[:, :], pos[:, :], tmp[:, :], ALU.add))
                link(nc.vector.tensor_scalar(tmp[:, :], pos[:, :], 1.0 / EB, -0.5 + 0.5 / EB, ALU.mult, ALU.add))
                link(nc.vector.tensor_scalar(tmp[:, :], tmp[:, :], MAGIC, None, ALU.add))
                link(nc.vector.tensor_scalar(tmp[:, :], tmp[:, :], MAGIC, None, ALU.subtract))
                link(nc.vector.scalar_tensor_tensor(pos[:, :], tmp[:, :], -float(EB), pos[:, :], ALU.mult, ALU.add))
                link(nc.vector.scalar_tensor_tensor(rec[:, :, 4].bitcast(U32), pos[:, :], float(NBP), tmp[:, :], ALU.mult, ALU.add))
                link(nc.vector.tensor_scalar(sbt[:, :], sbi[:, :], first[0:1, 1:2], None, ALU.is_ge))
                for k in range(2, T):
                    link(nc.vector.scalar_tensor_tensor(sbt[:, :], sbi[:, :], first[0:1, k:k + 1], sbt[:, :], ALU.is_ge, ALU.add))
                link(nc.vector.tensor_copy(tile_of[:, :], sbt[:, :]))

    order_block()

    def relation_block():
        with ExitStack() as ctx:
            sb = allocate(ctx)
            raw = [sb(f"rraw{s}", [128, KC, D]) for s in range(2)]
            wh = [sb(f"rwh{s}", [128, KC, D], F32R) for s in range(2)]
            wl = [sb(f"rwl{s}", [128, KC, D], F32R) for s in range(2)]
            ys = [sb(f"ys{s}", [NT, D]) for s in range(4)]
            cur = [sb(f"cur{s}", [NT, 5]) for s in range(2)]
            ld, yst = sems("rel_loaded", 2), sems("y_stored", 4)
            hi, lo, mm, ev = (sem("rel_" + n) for n in ("high", "low", "product", "taken"))
            sct, cp = sems("scattered", 2), sem("record_copied")
            block = ctx.enter_context(nc.Block())
            weights = a["L0_gnn_W_rel"].rearrange("r (k p) n -> r p k n", p=128)
            PAIRS, PT = NREL // 2, 2 * T
            FREE = 4
            DONE = 1

            @block.sync
            def _(sp):
                for s in range(2):
                    sp.dma_start(raw[s][:, :, :], weights[s]).then_inc(ld[s], 16)

                def pair(p, row, following):
                    for s in range(2):
                        for t in range(T):
                            n = s * T + t
                            sp.wait_ge(ev, p * PT + n + 1 + FREE)
                            sp.dma_start(row(n), ys[n % 4][:, :]).then_inc(yst[n % 4], 16)
                        if following is not None:
                            sp.wait_ge(lo, p * 2 + s + 1)
                            sp.dma_start(raw[s][:, :, :], following(s)).then_inc(ld[s], 16)

                with sp.Fori(0, R // 2 - 1) as p:
                    pair(p, lambda n: yv[bass.ds(p * PT + n, 1)].rearrange("a p d -> (a p) d"),
                         lambda s: weights[bass.ds(p * 2 + s + 2, 1)].rearrange("a p k n -> (a p) k n"))
                pair(R // 2 - 1, lambda n: yv[(R // 2 - 1) * PT + n],
                     lambda s: chunked((a["L0_gnn_W_root"], a["L0_mix_w_qkv"])[s]))
                pair(R // 2, lambda n: yv[R // 2 * PT + n], None)
                for s in range(4):
                    sp.wait_ge(yst[s], 16 * (NREL * T // 4))

            @block.scalar
            def _(act):
                act.wait_ge(ld[0], 16)
                nc.scalar.activation(wh[0][:, :, :], raw[0][:, :, :], ACT.Copy).then_inc(hi, 1)

                def pair(p, more):
                    act.wait_ge(ld[1], p * 16 + 16)
                    act.wait_ge(mm, p * PT + DONE)
                    nc.scalar.activation(wh[1][:, :, :], raw[1][:, :, :], ACT.Copy).then_inc(hi, 1)
                    for n in range(PT):
                        act.wait_ge(mm, p * PT + n + 1 + DONE)
                        if n >= 4 or not isinstance(p, int) or p:
                            act.wait_ge(yst[n % 4], p * (PT // 4 * 16) + (n // 4) * 16)
                        nc.scalar.activation(halves(ys[n % 4][:, :]), wide(n % 4), ACT.Copy).then_inc(ev, 1)
                        if n == T and more:
                            act.wait_ge(ld[0], p * 16 + 32)
                            act.wait_ge(mm, p * PT + T + DONE)
                            nc.scalar.activation(wh[0][:, :, :], raw[0][:, :, :], ACT.Copy).then_inc(hi, 1)

                pair(0, True)
                with act.Fori(1, PAIRS - 1) as p:
                    pair(p, True)
                pair(PAIRS - 1, False)

            @block.vector
            def _(dve):
                with dve.Fori(0, PAIRS) as p:
                    for s in range(2):
                        dve.wait_ge(hi, p * 2 + s + 1)
                        nc.vector.tensor_tensor(wl[s][:, :, :], raw[s][:, :, :], wh[s][:, :, :].bitcast(F32),
                                                ALU.subtract).then_inc(lo, 1)

            @block.tensor
            def _(pe):
                pe.sem_inc(mm, DONE)
                pe.sem_inc(ev, FREE)
                with pe.Fori(0, PAIRS) as p:
                    for s in range(2):
                        pe.wait_ge(lo, p * 2 + s + 1)
                        for t in range(T):
                            n = s * T + t
                            pe.wait_ge(ev, p * PT + n - 3 + FREE)
                            rows_mm(n % 4, ath, atl, wh[s], wl[s], slice(t * NT, (t + 1) * NT)).then_inc(mm, 1)

            @block.gpsimd
            def _(pool):
                def scatter(c, s, first):
                    if not first:
                        pool.wait_ge(sct[s], c * 16)
                    nc.gpsimd.tensor_copy(cur[s][:, :].bitcast(U32),
                                          rec[:, bass.ds(c * 2 + s, 1), :].rearrange("p a f -> p (a f)").bitcast(U32)).then_inc(cp, 1)
                    pool.wait_ge(cp, c * 2 + s + 1)
                    pool.nop(nofuse=True)
                    pool.indirect_dma_start(out=tab, out_offset=bass.IndirectOffsetOnAxis(cur[s][:, 4:5].bitcast(U32), 0),
                                            in_=cur[s][:, 0:4], in_offset=None).then_inc(sct[s], 16)

                scatter(0, 0, True)
                scatter(0, 1, True)
                with pool.Fori(1, EC // 2) as c:
                    scatter(c, 0, False)
                    scatter(c, 1, False)
                for s in range(2):
                    pool.wait_ge(sct[s], 16 * (EC // 2))

    relation_block()
    xform.close()

    counts = ExitStack()
    sbc = allocate(counts)
    ct = sbc("ct", [NT, T, N], U16)
    gathered = ExitStack()
    sbq = allocate(gathered)
    cnt = sbq("cnt", [R, N])
    table = sbq("table", [EB, NBP, 4])

    def count_block():
        with ExitStack() as ctx:
            sb = allocate(ctx)
            cur = [sb(f"c_cur{s}", [EB, G, 4]) for s in range(2)]
            src = [sb(f"c_src{s}", [EB, G, N], F16) for s in range(2)]
            dst = [sb(f"c_dst{s}", [EB, G, NT], F16) for s in range(2)]
            rel = [sb(f"c_rel{s}", [EB, G, R], F16) for s in range(2)]
            deg, tmp = sb("deg", [NT, T]), sb("c_tmp", [NT, T])
            ld, ch, hot, mm, fl, dg, sq = (sem("cnt_" + n) for n in ("loaded", "chain", "onehot", "product", "added", "degree", "sqrt"))
            block = ctx.enter_context(nc.Block())
            AHEAD = 2

            @block.sync
            def _(sp):
                sp.dma_start(table[:, :, :], tab_rows).then_inc(ld, 16)

            @block.tensor
            def _(pe):
                pe.sem_inc(fl, AHEAD)

                with pe.Fori(0, NSB // 2) as p:
                    for s in range(2):
                        pe.wait_ge(hot, p * 2 + s + 1)
                        pe.wait_ge(fl, p * 2 + s + 1)
                        for g in range(G):
                            for i in range(T):
                                nc.tensor.matmul(psum[0:NT, 3 * s + i // 4, (i % 4) * NT:(i % 4 + 1) * NT],
                                                 src[s][:, g, i * NT:(i + 1) * NT], dst[s][:, g, :],
                                                 start=(g == 0 and i % 4 == 0), stop=(g == G - 1), skip_group_check=True)
                            last = nc.tensor.matmul(psum[0:R, 3 * s + 2, 2 * NT:3 * NT], rel[s][:, g, :], dst[s][:, g, :],
                                                    start=False, stop=(g == G - 1), skip_group_check=True)
                        last.then_inc(mm, 1)
                pe.wait_ge(fl, NSB + AHEAD)
                for t in range(T):
                    last = nc.tensor.matmul(psum[0:NT, 6, t:t + 1], cnt[:, t * NT:(t + 1) * NT], ones[0:R, 0:1], start=True, stop=True)
                last.then_inc(dg, 1)

            @block.scalar
            def _(act):
                act.wait_ge(ch, 2 + NSB + 1)
                nc.scalar.activation(dinv[:, :], deg[:, :], ACT.Sqrt).then_inc(sq, 1)

            @block.vector
            def _(dve):
                link = Chain(dve, ch)
                link(nc.vector.memset(ct[:, :, :].bitcast(U16), 0))
                link(nc.vector.memset(cnt[:, :], 0.0))
                dve.wait_ge(ld, 16)

                def onehots(i, s, n):
                    link(nc.vector.tensor_copy(cur[s][:, :, :], table[:, bass.ds(n * G, G), :]))
                    for g in range(G):
                        nc.vector.tensor_scalar(src[s][:, g, :], iota16[:, :], cur[s][:, g, 1:2], None, ALU.is_equal)
                        nc.vector.tensor_scalar(dst[s][:, g, :], iota16[:, 0:NT], cur[s][:, g, 2:3], None, ALU.is_equal)
                        ins = nc.vector.tensor_scalar(rel[s][:, g, :], iota16[:, 0:R], cur[s][:, g, 3:4], None, ALU.is_equal)
                    ins.then_inc(hot, 1)

                def add(s, n):
                    v = dve.value_load(tile_of[0:1, bass.ds(n, 1)], min_val=0, max_val=T - 1)
                    d = bass.ds(v * NT, NT)
                    dve.wait_ge(mm, n + 1)
                    a8 = ct[:, 0:8, d].rearrange("p (a b) n -> p a b n", a=2)
                    nc.vector.tensor_tensor(a8, a8, psum[0:NT, 3 * s:3 * s + 2, 0:4 * NT].rearrange("p a (b n) -> p a b n", b=4), ALU.add)
                    nc.vector.tensor_tensor(ct[:, 8:10, d], ct[:, 8:10, d],
                                            psum[0:NT, 3 * s + 2, 0:2 * NT].rearrange("p (b n) -> p b n", b=2), ALU.add)
                    nc.vector.tensor_tensor(cnt[:, d], cnt[:, d], psum[0:R, 3 * s + 2, 2 * NT:3 * NT], ALU.add).then_inc(fl, 1)
                    dve.wait_ge(fl, n + 1 + AHEAD)

                onehots(0, 0, 0)
                with dve.Fori(0, NSB // 2 - 1) as p:
                    link.enter(p, 2)
                    onehots(p, 1, p * 2 + 1)
                    add(0, p * 2)
                    onehots(p + 1, 0, p * 2 + 2)
                    add(1, p * 2 + 1)
                    link.leave(NSB // 2 - 1)
                onehots(0, 1, NSB - 1)
                add(0, NSB - 2)
                add(1, NSB - 1)
                dve.wait_ge(dg, 1)
                link(nc.vector.tensor_scalar(deg[:, :], psum[0:NT, 6, 0:T], 1.0, None, ALU.add))
                dve.wait_ge(sq, 1)
                link(nc.vector.reciprocal(dinv[:, :], dinv[:, :]))
                polish(link, dinv[:, :], deg[:, :], tmp[:, :])
                link(nc.vector.tensor_scalar(cnt[:, :], cnt[:, :], 1.0, None, ALU.max))
                link(nc.vector.reciprocal(cnt[:, :], cnt[:, :]))

    count_block()

    room = [allocate(top, side="right")(f"room{i}", [128, T * D]) for i in range(1)]
    acc = room[0][0:NT, :].rearrange("p (t d) -> p t d", t=T)

    def gather_block():
        with ExitStack() as ctx:
            sb = allocate(ctx)
            SL = 2 * G
            yg = [sb(f"yg{s}", [EB, D]) for s in range(SL)]
            row = [sb(f"row{s}", [EB, 1], U32) for s in range(SL)]
            cur = [sb(f"g_cur{s}", [EB, G, 4]) for s in range(2)]
            rel = [sb(f"g_rel{s}", [EB, G, R], F16) for s in range(2)]
            relt = [sb(f"g_relt{s}", [R, G, EB]) for s in range(2)]
            inv = [sb(f"g_inv{s}", [R, NT]) for s in range(2)]
            sel = [sb(f"g_sel{s}", [EB, G, NT]) for s in range(2)]
            bias = sb("g_bias", [NT, D])
            iota32 = sb("iota32", [EB, NT])
            gl = sems("rows_gathered", SL)
            cp, ld, ch, hot, trn, rt, vv, sl, mm, fl = (sem("gat_" + n) for n in (
                "row_copied", "loaded", "chain", "onehot", "transposed", "relation_rows", "weights", "selector", "product", "added"))
            block = ctx.enter_context(nc.Block())

            @block.sync
            def _(sp):
                sp.dma_start(acc[:, :, :], tiled(y[R * N:(R + 1) * N, :])).then_inc(ld, 16)
                sp.dma_start(bias[:, :], spread(a["L0_gnn_b_rgcn"], NT)).then_inc(ld, 16)

            @block.gpsimd
            def _(pool):
                def fetch(i, s, first):
                    if not first:
                        pool.wait_ge(mm, i * 2 - 1 + s // G)
                    nc.gpsimd.tensor_copy(row[s][:, :], table[:, bass.ds(i * SL + s, 1), 0:1].rearrange("p a f -> p (a f)").bitcast(U32)).then_inc(cp, 1)
                    pool.wait_ge(cp, i * SL + s + 1)
                    pool.nop(nofuse=True)
                    pool.indirect_dma_start(out=yg[s][:, :], out_offset=None, in_=y,
                                            in_offset=bass.IndirectOffsetOnAxis(row[s][:, :], 0)).then_inc(gl[s], 16)

                for s in range(SL):
                    fetch(0, s, True)
                with pool.Fori(1, NB // SL) as i:
                    for s in range(SL):
                        fetch(i, s, False)

            @block.scalar
            def _(act):
                with act.Fori(0, NSB // 2 + 1) as p:
                    for s in range(2):
                        act.wait_ge(trn, p * 2 + s + 1)
                        nc.scalar.activation(relt[s][:, :, :], psum[0:R, 4 + s, 0:G * EB].rearrange("p (g e) -> p g e", g=G),
                                             ACT.Copy).then_inc(rt, 1)

            @block.tensor
            def _(pe):
                pe.sem_inc(fl, 2)
                def transposes(s, n):
                    pe.wait_ge(hot, n + 1)
                    for g in range(G):
                        last = nc.tensor.matmul(psum[0:R, 4 + s, g * EB:(g + 1) * EB], rel[s][:, g, :], identh[:, :], start=True, stop=True)
                    last.then_inc(trn, 1)

                def weights(s, n):
                    pe.wait_ge(rt, n + 1)
                    for g in range(G):
                        last = nc.tensor.matmul(psum[:, 6 + s, g * NT:(g + 1) * NT], relt[s][:, g, :], inv[s][:, :], start=True, stop=True)
                    last.then_inc(vv, 1)

                def sums(p, s, n):
                    pe.wait_ge(sl, n + 1)
                    pe.wait_ge(fl, n + 1)
                    for g in range(G):
                        pe.wait_ge(gl[G * s + g], p * 16 + 16)
                        for h in range(2):
                            last = nc.tensor.matmul(psum[0:NT, 2 * s + h, 0:HALF], sel[s][:, g, :], yg[G * s + g][:, h * HALF:(h + 1) * HALF],
                                                    start=(g == 0), stop=(g == G - 1))
                    last.then_inc(mm, 1)

                transposes(0, 0)
                transposes(1, 1)
                weights(0, 0)
                with pe.Fori(0, NSB // 2) as p:
                    for s in range(2):
                        transposes(s, p * 2 + s + 2)
                        weights(1 - s, p * 2 + s + 1)
                        sums(p, s, p * 2 + s)

            @block.vector
            def _(dve):
                link = Chain(dve, ch)
                dve.wait_ge(ld, 32)
                link(nc.vector.tensor_copy(iota32[:, :], iota16[:, 0:NT]))
                for t in range(T):
                    link(nc.vector.tensor_tensor(acc[:, t, :], acc[:, t, :], bias[:, :], ALU.add))

                def tile_index(n):
                    return dve.value_load(tile_of[0:1, bass.ds(n, 1)], min_val=0, max_val=T - 1)

                def prepare(s, n, last_use):
                    if last_use is not None:
                        dve.wait_ge(vv, last_use)
                    link(nc.vector.tensor_copy(cur[s][:, :, :], table[:, bass.ds(n * G, G), :]))
                    nc.vector.tensor_copy(inv[s][:, :], cnt[:, bass.ds(tile_index(n) * NT, NT)])
                    for g in range(G):
                        ins = nc.vector.tensor_scalar(rel[s][:, g, :], iota16[:, 0:R], cur[s][:, g, 3:4], None, ALU.is_equal)
                    ins.then_inc(hot, 1)

                def select(s, n):
                    dve.wait_ge(vv, n + 1)
                    for g in range(G):
                        ins = nc.vector.scalar_tensor_tensor(sel[s][:, g, :], iota32[:, :], cur[s][:, g, 2:3],
                                                             psum[:, 6 + s, g * NT:(g + 1) * NT], ALU.is_equal, ALU.mult)
                    ins.then_inc(sl, 1)

                def add(s, n):
                    v = tile_index(n)
                    o = acc[:, bass.ds(v, 1), :].rearrange("p a (h n) -> p (a h) n", h=2)
                    dve.wait_ge(mm, n + 1)
                    nc.vector.tensor_tensor(o, o, wide(s), ALU.add).then_inc(fl, 1)
                    dve.wait_ge(fl, n + 3)

                prepare(0, 0, None)
                prepare(1, 1, None)
                select(0, 0)
                with dve.Fori(0, NSB // 2) as p:
                    link.enter(p, 2)
                    for s in range(2):
                        n = p * 2 + s
                        dve.wait_ge(sl, n + 1)
                        prepare(s, n + 2, n + 1)
                        select(1 - s, n + 1)
                        add(s, n)
                    link.leave(NSB // 2)

    gather_block()
    gathered.close()

    def bias_row(ctx, name, src):
        return allocate(ctx)(name, [NT, D]), spread(src, NT)

    with ExitStack() as ctx:
        sb = allocate(ctx)
        hh, hl = sb("h1_high", [128, KC, N], F32R), sb("h1_low", [128, KC, N], F32R)
        transpose_block("tr_h1", acc, hh, hl)
        rows_block("gcn_", hh, hl, [a["L0_gnn_W_gcn"]], lambda dve, link, j, t, rows: nc.vector.tensor_scalar(
            halves(acc[:, t, :]), rows, dinv[:, t:t + 1], None, ALU.mult))

    room.append(allocate(top, side="right")("room1", [128, T * D]))
    gn = room[1][0:NT, :].rearrange("p (t d) -> p t d", t=T)

    def propagate_block():
        with ExitStack() as ctx:
            sb = allocate(ctx)
            ctf = sb("ctf", [NT, T, N])
            bias = sb("p_bias", [NT, D])
            ld, ch, rd, mm, ev = (sem("prop_" + n) for n in ("loaded", "chain", "ready", "product", "taken"))
            block = ctx.enter_context(nc.Block())

            @block.sync
            def _(sp):
                sp.dma_start(bias[:, :], spread(a["L0_gnn_b_gcn"], NT)).then_inc(ld, 16)

            @block.tensor
            def _(pe):
                for t in range(T):
                    pe.wait_ge(rd, t + 1)
                    if t >= 4:
                        pe.wait_ge(ev, t - 3)
                    for i in range(T):
                        for h in range(2):
                            last = nc.tensor.matmul(psum[0:NT, 2 * (t % 4) + h, 0:HALF], ctf[:, i, t * NT:(t + 1) * NT],
                                                    acc[:, i, h * HALF:(h + 1) * HALF], start=(i == 0), stop=(i == T - 1))
                    last.then_inc(mm, 1)

            @block.vector
            def _(dve):
                link = Chain(dve, ch)
                for t in range(T):
                    cols = slice(t * NT, (t + 1) * NT)
                    link(nc.vector.tensor_copy(ctf[:, :, cols], ct[:, :, cols]))
                    nc.vector.tensor_tensor(ctf[:, t, cols], ctf[:, t, cols], ident[0:NT, 0:NT], ALU.add).then_inc(rd, 1)
                dve.wait_ge(ld, 16)
                for t in range(T):
                    dve.wait_ge(mm, t + 1)
                    nc.vector.scalar_tensor_tensor(halves(gn[:, t, :]), wide(t % 4), dinv[:, t:t + 1], halves(bias[:, :]),
                                                   ALU.mult, ALU.add).then_inc(ev, 1)

    propagate_block()
    recycle()
    counts.close()
    graph.close()

    w = acc

    def mix_block():
        with ExitStack() as ctx:
            sb = allocate(ctx)
            w2 = sb("w2", [NT, T, D])
            scale, tmp = sb("m_scale", [NT, D]), [sb(f"m_tmp{s}", [NT, D]) for s in range(2)]
            temp, lg = sb("m_temp", [NT, H]), sb("m_logits", [NT, T, H])
            lt, pt = sb("m_lt", [H, N]), sb("m_pt", [H, N])
            mx, sm, sp2 = sb("m_max", [H, 1]), sb("m_sum", [H, 1]), sb("m_sum2", [H, 1])
            pi, pn = sb("m_pi", [NT, T, H]), sb("m_pin", [NT, T, H])
            ld, ch, sq, cs, nr, tr, ex, bk, dt = (sem("mix_" + n) for n in (
                "loaded", "chain", "squared", "column_sums", "norms", "transposed", "exp", "back", "dots"))
            lc, pc, dd = sem("mix_logits_done"), sem("mix_pi_done"), sem("mix_dots_in")
            block = ctx.enter_context(nc.Block())

            def per_head(ap):
                return ap.unsqueeze(2).broadcast_to([NT, H, DH])

            def by_head(ap):
                return ap.rearrange("p (h d) -> p h d", h=H)

            @block.sync
            def _(sp):
                sp.dma_start(w[:, :, :], tiled(y[(R + 1) * N:(R + 2) * N, :])).then_inc(ld, 16)
                sp.dma_start(temp[:, :], spread(a["L0_mix_temp"].rearrange("h a -> (h a)"), NT)).then_inc(ld, 16)

            @block.tensor
            def _(pe):
                for t in range(T):
                    pe.wait_ge(sq, t + 1)
                    for h in range(2):
                        last = nc.tensor.matmul(psum[0:NT, h, 0:HALF], ones[0:NT, 0:NT], w2[:, t, h * HALF:(h + 1) * HALF],
                                                start=(t == 0), stop=(t == T - 1))
                last.then_inc(cs, 1)
                for t in range(T):
                    pe.wait_ge(lc, t + 1)
                    last = nc.tensor.transpose(psum[0:H, 2 + t // 4, (t % 4) * NT:(t % 4 + 1) * NT], lg[:, t, :], ident[0:NT, 0:NT])
                last.then_inc(tr, 1)
                pe.wait_ge(pc, 1)
                for n, m in enumerate((lt, pt)):
                    for t in range(T):
                        last = nc.tensor.transpose(psum[0:NT, 5 + n, t * H:(t + 1) * H], m[:, t * NT:(t + 1) * NT], ident[0:H, 0:H])
                last.then_inc(bk, 1)
                for t in range(T):
                    pe.wait_ge(dd, t + 1)
                    for h in range(2):
                        last = nc.tensor.matmul(psum[0:NT, h, 0:HALF], ones[0:NT, 0:NT], w2[:, t, h * HALF:(h + 1) * HALF],
                                                start=(t == 0), stop=(t == T - 1))
                last.then_inc(dt, 1)

            @block.scalar
            def _(act):
                act.wait_ge(cs, 1)
                nc.scalar.activation(halves(scale[:, :]), wide(0), ACT.Sqrt).then_inc(nr, 1)
                act.wait_ge(ex, 1)
                nc.scalar.activation(lt[:, :], lt[:, :], ACT.Exp, bias=mx[:, :], accum_out=sm[:, :]).then_inc(nr, 1)

            @block.vector
            def _(dve):
                link = Chain(dve, ch)
                dve.wait_ge(ld, 32)
                for t in range(T):
                    nc.vector.tensor_tensor(w2[:, t, :], w[:, t, :], w[:, t, :], ALU.mult).then_inc(sq, 1)
                dve.wait_ge(nr, 1)
                link(nc.vector.tensor_scalar(scale[:, :], scale[:, :], 1e-12, None, ALU.max))
                link(nc.vector.reciprocal(scale[:, :], scale[:, :]))
                dve.wait_ge(sq, T)
                for t in range(T):
                    x = tmp[t % 2]
                    link(nc.vector.tensor_tensor(x[:, :], w[:, t, :], scale[:, :], ALU.mult))
                    link(nc.vector.tensor_tensor(x[:, :], x[:, :], x[:, :], ALU.mult))
                    link(nc.vector.tensor_reduce(lg[:, t, :], by_head(x[:, :]), AX.X, ALU.add))
                    nc.vector.tensor_tensor(lg[:, t, :], lg[:, t, :], temp[:, :], ALU.mult).then_inc(lc, 1)
                dve.wait_ge(tr, 1)
                link(nc.vector.tensor_copy(lt[:, 0:8 * NT].rearrange("p (a n) -> p a n", a=2), psum[0:H, 2:4, 0:4 * NT]))
                link(nc.vector.tensor_copy(lt[:, 8 * NT:N], psum[0:H, 4, 0:2 * NT]))
                link(nc.vector.tensor_reduce(mx[:, :], lt[:, :], AX.X, ALU.max))
                nc.vector.tensor_scalar(mx[:, :], mx[:, :], -1.0, None, ALU.mult).then_inc(ex, 1)
                dve.wait_ge(nr, 2)
                link(nc.vector.reciprocal(sm[:, :], sm[:, :]))
                link(nc.vector.tensor_scalar(lt[:, :], lt[:, :], sm[:, :], None, ALU.mult))
                link(nc.vector.tensor_reduce(sp2[:, :], lt[:, :], AX.X, ALU.add))
                link(nc.vector.tensor_scalar(sp2[:, :], sp2[:, :], 1e-8, None, ALU.add))
                link(nc.vector.reciprocal(sp2[:, :], sp2[:, :]))
                nc.vector.tensor_scalar(pt[:, :], lt[:, :], sp2[:, :], None, ALU.mult).then_inc(pc, 1)
                dve.wait_ge(bk, 1)
                link(nc.vector.tensor_copy(pi[:, :, :], psum[0:NT, 5, 0:T * H].rearrange("p (t h) -> p t h", t=T)))
                link(nc.vector.tensor_copy(pn[:, :, :], psum[0:NT, 6, 0:T * H].rearrange("p (t h) -> p t h", t=T)))
                for t in range(T):
                    nc.vector.tensor_tensor(by_head(w2[:, t, :]), by_head(w2[:, t, :]), per_head(pn[:, t, :]), ALU.mult).then_inc(dd, 1)
                    link(nc.vector.tensor_tensor(by_head(w[:, t, :]), by_head(w[:, t, :]), per_head(pi[:, t, :]), ALU.mult))
                dve.wait_ge(dt, 1)
                link(nc.vector.tensor_scalar(halves(scale[:, :]), wide(0), 1.0, None, ALU.add))
                link(nc.vector.reciprocal(scale[:, :], scale[:, :]))
                link(nc.vector.tensor_scalar(scale[:, :], scale[:, :], -1.0, None, ALU.mult))
                for t in range(T):
                    link(nc.vector.tensor_tensor(w[:, t, :], w[:, t, :], scale[:, :], ALU.mult))

    mix_block()

    with ExitStack() as ctx:
        sb = allocate(ctx)
        hh, hl = sb("mix_high", [128, KC, N], F32R), sb("mix_low", [128, KC, N], F32R)
        transpose_block("tr_mix", w, hh, hl)
        bias = sb("o_bias", [NT, D])

        def sink(dve, link, j, t, rows):
            g = halves(gn[:, t, :])
            link(nc.vector.tensor_tensor(g, g, rows, ALU.add))
            link(nc.vector.tensor_tensor(gn[:, t, :], gn[:, t, :], bias[:, :], ALU.add))
            return nc.vector.tensor_tensor(gn[:, t, :], gn[:, t, :], w[:, t, :], ALU.add)

        rows_block("wout_", hh, hl, [a["L0_mix_w_out"]], sink,
                   loads=[(bias[:, :], spread(a["L0_mix_b_out"], NT)), (w[:, :, :], tiled(a["x"]))],
                   stores=[(scr["x1"][t * NT:(t + 1) * NT, :], gn[:, t, :]) for t in range(T)])

    nrm = gn
    norm_block("ln_h", None, nrm, lambda dve, link, t, m, r: link(
        nc.vector.tensor_scalar(nrm[:, t, :], nrm[:, t, :], m, r, ALU.subtract, ALU.mult)))

    def affine_norm(tag, xs, g, b, store):
        with ExitStack() as ctx:
            sb = allocate(ctx)
            gain, shift = sb(tag + "gain", [NT, D]), sb(tag + "shift", [NT, D])
            gl, st = sem(tag + "gain_loaded"), sem(tag + "stored")
            with ExitStack() as c2:
                block = c2.enter_context(nc.Block())

                @block.sync
                def _(sp):
                    sp.dma_start(gain[:, :], spread(g, NT)).then_inc(gl, 16)
                    sp.dma_start(shift[:, :], spread(b, NT)).then_inc(gl, 16)
                    sp.dma_start(tiled(store), xs[:, :, :]).then_inc(st, 16)
                    sp.wait_ge(gl, 32)
                    sp.wait_ge(st, 16)

            def then(dve, link, t, m, r):
                link(nc.vector.tensor_scalar(xs[:, t, :], xs[:, t, :], m, r, ALU.subtract, ALU.mult))
                link(nc.vector.tensor_tensor(xs[:, t, :], xs[:, t, :], gain[:, :], ALU.mult))
                link(nc.vector.tensor_tensor(xs[:, t, :], xs[:, t, :], shift[:, :], ALU.add))

            norm_block(tag, None, xs, then)

    affine_norm("ln_1", nrm, a["L0_ffn_g1"], a["L0_ffn_b1"], scr["hidden"])

    keep = ExitStack()
    sbk = allocate(keep)
    selt = sbk("selt", [TH, 2, N])
    unrouted = sbk("unrouted", [NT, T])
    score = sbk("score", [NT, T])
    pooled_w = sbk("pooled_w", [NT, D])
    qt = sbk("qt", [128, KC, TOP])

    def route_block():
        with ExitStack() as ctx:
            sb = allocate(ctx)
            wr, br = sb("wr", [NT, D]), sb("br", [NT, 1])
            wm, wq = sb("r_wm", [128, KC, D]), sb("r_wq", [128, KC, D])
            bq = sb("r_bq", [128, KC])
            junk, junk2 = sb("r_junk", [NT, N]), sb("r_junk2", [NT, N])
            z, e, idx, rank, ties = (sb("r_" + n, [NT, T]) for n in ("z", "e", "idx", "rank", "ties"))
            srow, rrow = sb("srow", [NT, N]), sb("rrow", [TH, N])
            iota, iotaj = sb("r_iota", [NT, N]), sb("r_iotaj", [TH, 2])
            sel = sb("sel", [NT, T, TOP])
            nselt = sb("nselt", [128, KC, TOP])
            total, pt, ptb = sb("r_total", [128, 1]), sb("r_pt", [128, KC]), sb("r_ptb", [128, KC, NT])
            ld, ldw, co, ch, zs, ex, sc, sd, rk, rd = (sem("rt_" + n) for n in (
                "loaded", "weights_loaded", "const", "chain", "z", "exp", "scores", "score_rows", "ranks", "rank_rows"))
            po, pd, sl, ns, nd, qd, pw = (sem("rt_" + n) for n in (
                "pooled", "pooled_ready", "selector", "selected", "selected_ready", "queries", "pooled_w"))
            qe = sem("rt_queries_taken")
            block = ctx.enter_context(nc.Block())
            by_tile = lambda ap: ap.rearrange("(t p) -> p t", p=NT)

            @block.sync
            def _(sp):
                sp.dma_start(wr[:, :], spread(a["L0_ffn_Wr"], NT)).then_inc(ld, 16)
                sp.dma_start(br[:, :], spread(a["L0_ffn_br"], NT)).then_inc(ld, 16)
                sp.dma_start(bq[:, :], a["L0_ffn_bq"].rearrange("(k p) -> p k", p=128)).then_inc(ld, 16)
                sp.dma_start(wm[:, :, :], chunked(a["L0_ffn_Wm"])).then_inc(ldw, 16)
                sp.dma_start(wq[:, :, :], chunked(a["L0_ffn_Wq"])).then_inc(ldw, 16)
                sp.wait_ge(sc, 1)
                sp.dma_start(by_tile(scr["score"]), score[:, :]).then_inc(sd, 16)
                sp.wait_ge(sd, 16)
                sp.dma_start(srow[:, :], spread(scr["score"], NT)).then_inc(sd, 16)
                sp.wait_ge(rk, 1)
                sp.dma_start(by_tile(scr["rank"]), rank[:, :]).then_inc(rd, 16)
                sp.wait_ge(rd, 16)
                sp.dma_start(rrow[:, :], spread(scr["rank"], TH)).then_inc(rd, 16)

            @block.gpsimd
            def _(pool):
                imprecise = dict(allow_small_or_imprecise_dtypes=True)
                pool.iota(iota[:, :], pattern=[[1, N]], base=0, channel_multiplier=0, **imprecise).then_inc(co, 1)
                pool.iota(idx[:, :], pattern=[[NT, T]], base=0, channel_multiplier=1, **imprecise).then_inc(co, 1)
                pool.iota(iotaj[:, :], pattern=[[TH, 2]], base=0, channel_multiplier=1, **imprecise).then_inc(co, 1)

            @block.scalar
            def _(act):
                act.wait_ge(zs, 1)
                nc.scalar.activation(e[:, :], z[:, :], ACT.Exp, scale=-1.0).then_inc(ex, 1)

            @block.tensor
            def _(pe):
                pe.wait_ge(sc, 1)
                for k in range(KC):
                    for t in range(T):
                        nc.tensor.matmul(psum[:, 0, k:k + 1], nrm[:, t, k * 128:(k + 1) * 128], score[:, t:t + 1],
                                         start=(t == 0), stop=(t == T - 1))
                for t in range(T):
                    last = nc.tensor.matmul(psum[:, 0, KC:KC + 1], ones[0:NT, :], score[:, t:t + 1], start=(t == 0), stop=(t == T - 1))
                last.then_inc(po, 1)
                pe.wait_ge(pd, 1)
                pe.wait_ge(ldw, 32)
                for k in range(KC):
                    for h in range(2):
                        last = nc.tensor.matmul(psum[0:NT, 2 + h, 0:HALF], ptb[:, k, :], wm[:, k, h * HALF:(h + 1) * HALF],
                                                start=(k == 0), stop=(k == KC - 1))
                last.then_inc(pw, 1)
                pe.wait_ge(sl, T)
                for k in range(KC):
                    if k >= 2:
                        pe.wait_ge(nd, k - 1)
                    for t in range(T):
                        last = nc.tensor.matmul(psum[:, 4 + k % 2, 0:TOP], nrm[:, t, k * 128:(k + 1) * 128], sel[:, t, :],
                                                start=(t == 0), stop=(t == T - 1))
                    last.then_inc(ns, 1)
                pe.wait_ge(nd, KC)
                for o in range(KC):
                    if o >= 2:
                        pe.wait_ge(qe, o - 1)
                    for k in range(KC):
                        last = nc.tensor.matmul(psum[:, 6 + o % 2, 0:TOP], wq[:, k, o * 128:(o + 1) * 128], nselt[:, k, :],
                                                start=(k == 0), stop=(k == KC - 1))
                    last.then_inc(qd, 1)

            @block.vector
            def _(dve):
                link = Chain(dve, ch)
                dve.wait_ge(ld, 48)
                dve.wait_ge(co, 3)
                for t in range(T):
                    link(nc.vector.scalar_tensor_tensor(junk[:, 0:D], nrm[:, t, :], 1.0, wr[:, :], ALU.mult, ALU.mult, accum_out=z[:, t:t + 1]))
                nc.vector.tensor_scalar(z[:, :], z[:, :], br[:, :], None, ALU.add).then_inc(zs, 1)
                dve.wait_ge(ex, 1)
                link(nc.vector.tensor_scalar(e[:, :], e[:, :], 1.0, None, ALU.add))
                nc.vector.reciprocal(score[:, :], e[:, :]).then_inc(sc, 1)
                dve.wait_ge(po, 1)
                link(nc.vector.tensor_scalar(total[:, :], psum[:, 0, KC:KC + 1], 1e-6, None, ALU.add))
                link(nc.vector.reciprocal(total[:, :], total[:, :]))
                link(nc.vector.tensor_scalar(pt[:, :], psum[:, 0, 0:KC], total[:, :], None, ALU.mult))
                nc.vector.tensor_copy(ptb[:, :, :], pt[:, :].unsqueeze(2).broadcast_to([128, KC, NT])).then_inc(pd, 1)
                dve.wait_ge(sd, 32)
                for t in range(T):
                    link(nc.vector.tensor_scalar(junk[:, :], srow[:, :], score[:, t:t + 1], None, ALU.is_lt, ALU.add, accum_out=rank[:, t:t + 1]))
                    link(nc.vector.tensor_scalar(junk2[:, :], iota[:, :], idx[:, t:t + 1], None, ALU.is_lt))
                    link(nc.vector.scalar_tensor_tensor(junk[:, :], srow[:, :], score[:, t:t + 1], junk2[:, :], ALU.is_equal, ALU.mult, accum_out=ties[:, t:t + 1]))
                nc.vector.tensor_tensor(rank[:, :], rank[:, :], ties[:, :], ALU.add).then_inc(rk, 1)
                dve.wait_ge(rk, 1)
                link(nc.vector.tensor_scalar(unrouted[:, :], rank[:, :], float(TOP), None, ALU.is_ge))
                for t in range(T):
                    nc.vector.tensor_scalar(sel[:, t, :], iota[:, 0:TOP], rank[:, t:t + 1], None, ALU.is_equal).then_inc(sl, 1)
                dve.wait_ge(pw, 1)
                link(nc.vector.tensor_copy(halves(pooled_w[:, :]), wide(1)))
                for k in range(KC):
                    dve.wait_ge(ns, k + 1)
                    nc.vector.tensor_copy(nselt[:, k, :], psum[:, 4 + k % 2, 0:TOP]).then_inc(nd, 1)
                dve.wait_ge(rd, 32)
                for i in range(2):
                    link(nc.vector.tensor_scalar(selt[:, i, :], rrow[:, :], iotaj[:, i:i + 1], None, ALU.is_equal))
                for o in range(KC):
                    dve.wait_ge(qd, o + 1)
                    nc.vector.tensor_scalar(qt[:, o, :], psum[:, 6 + o % 2, 0:TOP], bq[:, o:o + 1], None, ALU.add).then_inc(qe, 1)

    route_block()

    def cols_block(tag, ah, al, weight, oc, bias_dram, sink, kc=KC):
        with ExitStack() as ctx:
            sb = allocate(ctx)
            raw = sb(tag + "raw", [128, kc, oc * 128])
            wh, wl = sb(tag + "wh", [128, kc, oc * 128], F32R), sb(tag + "wl", [128, kc, oc * 128], F32R)
            bias = sb(tag + "bias", [128, oc])
            ld, hi, lo, mm, ev = (sem(tag + n) for n in ("loaded", "high", "low", "product", "taken"))
            block = ctx.enter_context(nc.Block())

            @block.sync
            def _(sp):
                sp.dma_start(raw[:, :, :], chunked(weight)).then_inc(ld, 16)
                sp.dma_start(bias[:, :], bias_dram.rearrange("(k p) -> p k", p=128)).then_inc(ld, 16)

            @block.scalar
            def _(act):
                act.wait_ge(ld, 32)
                nc.scalar.activation(wh[:, :, :], raw[:, :, :], ACT.Copy).then_inc(hi, 1)
                for n in range(oc * 3):
                    o, c = n // 3, n % 3
                    act.wait_ge(mm, n + 1)
                    sink(o, slice(COLS[c][0], COLS[c][0] + COLS[c][1]), psum[:, n % 8, 0:COLS[c][1]], bias[:, o:o + 1]).then_inc(ev, 1)

            @block.vector
            def _(dve):
                dve.wait_ge(hi, 1)
                nc.vector.tensor_tensor(wl[:, :, :], raw[:, :, :], wh[:, :, :].bitcast(F32), ALU.subtract).then_inc(lo, 1)

            @block.tensor
            def _(pe):
                pe.wait_ge(lo, 1)
                for n in range(oc * 3):
                    o, (c0, cn) = n // 3, COLS[n % 3]
                    if n >= 8:
                        pe.wait_ge(ev, n - 7)
                    for k in range(kc):
                        f = slice(o * 128, (o + 1) * 128)
                        last = split_mm(psum[:, n % 8, 0:cn], wh[:, k, f], wl[:, k, f],
                                        ah[:, k, c0:c0 + cn], al[:, k, c0:c0 + cn], k == 0, k == kc - 1)
                    last.then_inc(mm, 1)

    v = acc
    kt = room[1][:, 0:KC * N].rearrange("p (k n) -> p k n", k=KC)
    with ExitStack() as ctx:
        sb = allocate(ctx)
        hh, hl = sb("n_high", [128, KC, N], F32R), sb("n_low", [128, KC, N], F32R)
        transpose_block("tr_n", nrm, hh, hl)
        bias = sb("mv_bias", [NT, D])

        def mix_sink(dve, link, j, t, rows):
            link(nc.vector.tensor_tensor(halves(acc[:, t, :]), rows, halves(bias[:, :]), ALU.add))
            link(nc.vector.scalar_tensor_tensor(acc[:, t, :], pooled_w[:, :], score[:, t:t + 1], acc[:, t, :], ALU.mult, ALU.add))
            return nc.vector.tensor_scalar(acc[:, t, :], acc[:, t, :], unrouted[:, t:t + 1], None, ALU.mult)

        rows_block("wm_", hh, hl, [a["L0_ffn_Wm"]], mix_sink, loads=[(bias[:, :], spread(a["L0_ffn_bm"], NT))],
                   stores=[(scr["mix"][t * NT:(t + 1) * NT, :], acc[:, t, :]) for t in range(T)])
        rows_block("wv_", hh, hl, [a["L0_ffn_Wv"]],
                   lambda dve, link, j, t, rows: nc.vector.tensor_tensor(halves(v[:, t, :]), rows, halves(bias[:, :]), ALU.add),
                   loads=[(bias[:, :], spread(a["L0_ffn_bv"], NT))])
        cols_block("wk_", hh, hl, a["L0_ffn_Wk"], KC, a["L0_ffn_bk"],
                   lambda o, cols, got, b: nc.scalar.activation(kt[:, o, cols], got, ACT.Identity, bias=b))

    ctxs = sbk("ctxs", [TH, 2, D])

    def attention_block():
        with ExitStack() as ctx:
            sb = allocate(ctx)
            p = [sb(f"probs{s}", [TH, N]) for s in range(2)]
            pt = [sb(f"probst{s}", [NT, T, TH]) for s in range(2)]
            mx, nm, sm, rs = (sb("a_" + n, [TH, 2, 2]) for n in ("max", "negmax", "sum", "rsum"))
            qk, mxs, ex, tr, tc, pv, cx, ch = (sem("att_" + n) for n in (
                "scores", "max", "exp", "transposed", "copied", "context", "context_taken", "chain"))
            block = ctx.enter_context(nc.Block())
            U = 2 * H
            units = [(i, h) for i in range(2) for h in range(H)]

            @block.tensor
            def _(pe):
                def scores(u):
                    i, h = units[u]
                    s, rows = u % 2, slice((h % 2) * DH, (h % 2 + 1) * DH)
                    if u >= 2:
                        pe.wait_ge(cx, u - 1)
                        pe.wait_ge(ex, 2 * (u - 1))
                    for c, (c0, cn) in enumerate(COLS):
                        last = nc.tensor.matmul(psum[0:TH, 3 * s + c, 0:cn], qt[rows, h // 2, i * TH:(i + 1) * TH],
                                                kt[rows, h // 2, c0:c0 + cn], start=True, stop=True)
                    last.then_inc(qk, 1)

                scores(0)
                for u in range(U):
                    i, h = units[u]
                    s = u % 2
                    if u + 1 < U:
                        scores(u + 1)
                    pe.wait_ge(ex, 2 * (u + 1))
                    for b in range(2):
                        n = 2 * u + b
                        if n >= 2:
                            pe.wait_ge(tc, n - 1)
                        for j in range(5):
                            k = 5 * b + j
                            last = nc.tensor.transpose(psum[0:NT, 6 + b, j * TH:(j + 1) * TH], p[s][:, k * NT:(k + 1) * NT], ident[0:TH, 0:TH])
                        last.then_inc(tr, 1)
                    pe.wait_ge(tc, 2 * (u + 1))
                    for k in range(T):
                        last = nc.tensor.matmul(psum[0:TH, 3 * s + 2, 440:440 + DH], pt[s][:, k, :], v[:, k, h * DH:(h + 1) * DH],
                                                start=(k == 0), stop=(k == T - 1))
                    last.then_inc(pv, 1)

            @block.scalar
            def _(act):
                for u in range(U):
                    s = u % 2
                    act.wait_ge(mxs, u + 1)
                    if u >= 2:
                        act.wait_ge(tr, 2 * (u - 1))
                    nc.scalar.activation(p[s][:, 0:832].rearrange("p (a n) -> p a n", a=2), psum[0:TH, 3 * s:3 * s + 2, 0:416], ACT.Exp,
                                         bias=nm[:, s, 0:1], scale=0.125, accum_out=sm[:, s, 0:1]).then_inc(ex, 1)
                    nc.scalar.activation(p[s][:, 832:N], psum[0:TH, 3 * s + 2, 0:418], ACT.Exp,
                                         bias=nm[:, s, 0:1], scale=0.125, accum_out=sm[:, s, 1:2]).then_inc(ex, 1)

            @block.vector
            def _(dve):
                link = Chain(dve, ch)

                def maximum(u):
                    s = u % 2
                    dve.wait_ge(qk, u + 1)
                    link(nc.vector.tensor_reduce(mx[:, s, 0:1], psum[0:TH, 3 * s:3 * s + 2, 0:416], AX.XY, ALU.max))
                    link(nc.vector.tensor_reduce(mx[:, s, 1:2], psum[0:TH, 3 * s + 2, 0:418], AX.X, ALU.max))
                    link(nc.vector.tensor_tensor(mx[:, s, 0:1], mx[:, s, 0:1], mx[:, s, 1:2], ALU.max))
                    nc.vector.tensor_scalar(nm[:, s, 0:1], mx[:, s, 0:1], -0.125, None, ALU.mult).then_inc(mxs, 1)

                maximum(0)
                for u in range(U):
                    i, h = units[u]
                    s = u % 2
                    dve.wait_ge(ex, 2 * (u + 1))
                    link(nc.vector.tensor_tensor(rs[:, s, 0:1], sm[:, s, 0:1], sm[:, s, 1:2], ALU.add))
                    link(nc.vector.reciprocal(rs[:, s, 0:1], rs[:, s, 0:1]))
                    if u + 1 < U:
                        maximum(u + 1)
                    for b in range(2):
                        dve.wait_ge(tr, 2 * u + b + 1)
                        nc.vector.tensor_copy(pt[s][:, 5 * b:5 * b + 5, :],
                                              psum[0:NT, 6 + b, 0:5 * TH].rearrange("p (k n) -> p k n", k=5)).then_inc(tc, 1)
                    dve.wait_ge(pv, u + 1)
                    nc.vector.tensor_scalar(ctxs[:, i, h * DH:(h + 1) * DH], psum[0:TH, 3 * s + 2, 440:440 + DH], rs[:, s, 0:1],
                                            None, ALU.mult).then_inc(cx, 1)

    attention_block()

    hf, mixed = gn, acc

    def merge_block():
        with ExitStack() as ctx:
            sb = allocate(ctx)
            wo, bo = sb("wo", [128, KC, D]), sb("bo", [TH, D])
            ctxt, ao = sb("ctxt", [128, KC, TOP]), sb("ao", [TH, 2, D])
            ld, ldh, tr, tc, om, oe, mm, ev, ch, st = (sem("mg_" + n) for n in (
                "loaded", "rows_loaded", "transposed", "copied", "out_product", "out_taken", "merged", "taken", "chain", "stored"))
            block = ctx.enter_context(nc.Block())

            @block.sync
            def _(sp):
                sp.dma_start(wo[:, :, :], chunked(a["L0_ffn_Wo"])).then_inc(ld, 16)
                sp.dma_start(bo[:, :], spread(a["L0_ffn_bo"], TH)).then_inc(ld, 16)
                sp.dma_start(hf, tiled(scr["hidden"])).then_inc(ldh, 16)
                sp.dma_start(mixed, tiled(scr["mix"])).then_inc(ldh, 16)

            @block.tensor
            def _(pe):
                for i in range(2):
                    for k in range(KC):
                        last = nc.tensor.transpose(psum[:, 4 + k // 2, (k % 2) * TOP + i * TH:(k % 2) * TOP + (i + 1) * TH],
                                                   ctxs[:, i, k * 128:(k + 1) * 128], ident[0:TH, 0:TH])
                last.then_inc(tr, 1)
                pe.wait_ge(tc, 1)
                pe.wait_ge(ld, 32)
                for i in range(2):
                    for h in range(2):
                        for k in range(KC):
                            last = nc.tensor.matmul(psum[0:TH, 2 * i + h, 0:HALF], ctxt[:, k, i * TH:(i + 1) * TH],
                                                    wo[:, k, h * HALF:(h + 1) * HALF], start=(k == 0), stop=(k == KC - 1))
                last.then_inc(om, 1)
                pe.wait_ge(oe, 2)
                for t in range(T):
                    if t >= 4:
                        pe.wait_ge(ev, t - 3)
                    for h in range(2):
                        for i in range(2):
                            last = nc.tensor.matmul(psum[0:NT, 2 * (t % 4) + h, 0:HALF], selt[:, i, t * NT:(t + 1) * NT],
                                                    ao[:, i, h * HALF:(h + 1) * HALF], start=(i == 0), stop=(i == 1))
                    last.then_inc(mm, 1)

            @block.vector
            def _(dve):
                link = Chain(dve, ch)
                dve.wait_ge(tr, 1)
                nc.vector.tensor_copy(ctxt[:, :, :].rearrange("p (a b) n -> p a (b n)", a=3), psum[:, 4:7, 0:2 * TOP]).then_inc(tc, 1)
                dve.wait_ge(om, 1)
                dve.wait_ge(ld, 32)
                for i in range(2):
                    nc.vector.tensor_tensor(halves(ao[:, i, :]), wide(i, rows=TH), halves(bo[:, :]), ALU.add).then_inc(oe, 1)
                dve.wait_ge(ldh, 32)
                for t in range(T):
                    link(nc.vector.tensor_tensor(hf[:, t, :], hf[:, t, :], mixed[:, t, :], ALU.add))
                    dve.wait_ge(mm, t + 1)
                    nc.vector.tensor_tensor(halves(hf[:, t, :]), halves(hf[:, t, :]), wide(t % 4), ALU.add).then_inc(ev, 1)

    merge_block()
    keep.close()
    affine_norm("ln_2", hf, a["L0_ffn_g2"], a["L0_ffn_b2"], scr["hf"])

    with ExitStack() as ctx:
        sb = allocate(ctx)
        fh, fl2 = sb("f_high", [128, FK, N], F32R), sb("f_low", [128, FK, N], F32R)
        with ExitStack() as c2:
            sb2 = allocate(c2)
            hh, hl = sb2("n2_high", [128, KC, N], F32R), sb2("n2_low", [128, KC, N], F32R)
            transpose_block("tr_n2", hf, hh, hl)
            f = room[0][:, 0:FK * N].rearrange("p (k n) -> p k n", k=FK)
            cols_block("w1_", hh, hl, a["L0_ffn_W1"], FK, a["L0_ffn_bf1"],
                       lambda o, cols, got, b: nc.scalar.activation(f[:, o, cols], got, ACT.Gelu, bias=b))
        with ExitStack() as c2:
            hi = sem("f_hi")
            block = c2.enter_context(nc.Block())

            @block.scalar
            def _(act):
                for k in range(FK):
                    nc.scalar.activation(fh[:, k, :], f[:, k, :], ACT.Copy).then_inc(hi, 1)

            @block.vector
            def _(dve):
                for k in range(FK):
                    dve.wait_ge(hi, k + 1)
                    nc.vector.tensor_tensor(fl2[:, k, :], f[:, k, :], fh[:, k, :].bitcast(F32), ALU.subtract)

        bias = sb("f2_bias", [NT, D])
        x1 = sb("x1", [NT, T, D])

        def last_sink(dve, link, j, t, rows):
            link(nc.vector.tensor_tensor(halves(hf[:, t, :]), halves(hf[:, t, :]), rows, ALU.add))
            link(nc.vector.tensor_tensor(hf[:, t, :], hf[:, t, :], bias[:, :], ALU.add))
            return nc.vector.tensor_tensor(hf[:, t, :], hf[:, t, :], x1[:, t, :], ALU.add)

        rows_block("w2_", fh, fl2, [a["L0_ffn_W2"]], last_sink, kc=FK,
                   loads=[(bias[:, :], spread(a["L0_ffn_bf2"], NT)), (hf, tiled(scr["hf"])), (x1[:, :, :], tiled(scr["x1"]))],
                   stores=[(out[t * NT:(t + 1) * NT, :], hf[:, t, :]) for t in range(T)])


def kernel(**inputs):
    import numpy as np
    import concourse.bacc as bacc
    from concourse import mybir
    from concourse.bass_utils import run_bass_kernel_spmd as run

    nc = bacc.Bacc("TRN2", target_bir_lowering=False, num_devices=1)
    arrays, a = {}, {}
    for name, value in inputs.items():
        v = np.ascontiguousarray(value)
        v = v.reshape(v.shape or (1,))
        arrays["in_" + name] = v
        a[name] = nc.dram_tensor("in_" + name, v.shape, mybir.dt.from_np(v.dtype), kind="ExternalInput").ap()
    out = nc.dram_tensor("out", (N, D), F32, kind="ExternalOutput").ap()
    KIND = "Internal"
    scr = {name: nc.dram_tensor("scratch_" + name, shape, F32, kind=KIND).ap() for name, shape in SCRATCH.items()}
    build(nc, a, out, scr)
    r = run(nc, [arrays], core_ids=[0])
    if KIND != "Internal":
        for name in SCRATCH:
            np.save("/tmp/dbg_" + name + ".npy", r.results[0]["scratch_" + name])
    return r.results[0]["out"]
```

```python
from contextlib import ExitStack
import math

import concourse.bass as bass
from concourse import mybir

ALU = mybir.AluOpType
ACT = mybir.ActivationFunctionType
AX = mybir.AxisListType
F32 = mybir.dt.float32
F32R = mybir.dt.float32r
F16 = mybir.dt.float16
I32 = mybir.dt.int32
U32 = mybir.dt.uint32
U16 = mybir.dt.uint16

N, D = 1250, 768
NT, T = 125, 10
KC = D // 128
HALF = D // 2
E = 41250
EC = E // NT
R = 34
NREL = R + 2
EB = 128
G = 2
SBE = EB * G
NSB = 2 * math.ceil((E // SBE + T) / 2)
NSB = 4 * math.ceil(NSB / 4)
NB = NSB * G
PAIRS, PT = NREL // 2, 2 * T
COUNT_PAIRS = math.ceil(NSB / PT)
NSBP = COUNT_PAIRS * PT + 1
NBP = NSBP * G
COUNT_FROM = PAIRS - 1 - COUNT_PAIRS
assert NSBP >= NSB + 3
H, DH = 12, 64
TOP = int(round(0.15 * N))
TH = TOP // 2
FF = 384
FK = FF // 128
EPS = 1e-5
MAGIC = 12582912.0
COLS = [(0, 416), (416, 416), (832, 418)]


SCRATCH = {
    "y": (NREL * N, D),
    "table": (EB * NBP, 4),
    "x1": (N, D),
    "hidden": (N, D),
    "mix": (N, D),
    "hf": (N, D),
    "score": (N,),
    "rank": (N,),
}


class Chain:

    def __init__(self, eng, sem):
        self.eng, self.sem, self.n, self.i, self.per = eng, sem, 0, None, 0

    def __call__(self, ins):
        self.n += 1
        ins.then_inc(self.sem, 1)
        self.wait()

    def wait(self):
        self.eng.wait_ge(self.sem, self.n if self.i is None else self.i * self.per + self.n)

    def enter(self, i, per):
        self.i, self.per, self.start = i, per, self.n

    def leave(self, times):
        assert self.n - self.start == self.per, (self.n - self.start, self.per)
        self.n = self.start + self.per * times
        self.i = None


def build(nc, a, out, scr):
    stack = ExitStack()
    with stack, nc.allow_non_contiguous_dma(reason="bias columns and 1250 scores, a few KB"):
        _build(nc, a, out, scr, stack)


def _build(nc, a, out, scr, top):
    def allocate(ctx, **where):
        def sb(name, shape, dt=F32):
            return ctx.enter_context(nc.sbuf_tensor(name, shape, dt, **where))
        return sb

    live = []

    def sem(name):
        live.append(nc.alloc_semaphore(name=name))
        return live[-1]

    def recycle():
        nc.clear_and_free_semaphores(live)
        live.clear()
        nc.all_engine_barrier()

    def sems(name, n):
        return [sem(f"{name}{i}") for i in range(n)]

    psum = top.enter_context(nc.psum_tensor("psum", [128, 8, 512], F32))

    def wide(slot, rows=NT, w=HALF):
        return psum[0:rows, 2 * slot:2 * slot + 2, 0:w]

    def halves(ap):
        return ap.rearrange("p (h n) -> p h n", h=2)

    tiled = lambda ap: ap.rearrange("(t p) d -> p t d", p=NT)
    chunked = lambda ap: ap.rearrange("(k p) n -> p k n", p=128)
    spread = lambda ap, rows: ap.partition_broadcast(rows)

    sb0 = allocate(top)
    ident = sb0("ident", [128, 128])
    identh = sb0("identh", [128, 128], F16)
    ones = sb0("ones", [128, 128])
    iota16 = sb0("iota16", [128, N], F16)
    dinv = sb0("dinv", [NT, T])
    prefix = sb0("prefix", [NT, NT])

    def stats(dve, link, src, tmp, mv, t):
        for h in range(2):
            ins = nc.vector.bn_stats(tmp[:, t, h * 6:h * 6 + 6], src[:, t, h * HALF:(h + 1) * HALF])
            link(ins)
        link(nc.vector.bn_aggr(mv[:, t, :], tmp[:, t, :]))

    def split_mm(o, lh, ll, rh, rl, start, stop):
        nc.tensor.matmul(o, lh, rh, start=start, stop=False)
        nc.tensor.matmul(o, lh, rl, start=False, stop=False)
        return nc.tensor.matmul(o, ll, rh, start=False, stop=stop)

    def rows_mm(slot, ah, al, wh, wl, cols, kc=KC):
        last = None
        for k in range(kc):
            for h in range(2):
                last = split_mm(psum[0:cols.stop - cols.start, 2 * slot + h, 0:HALF], ah[:, k, cols], al[:, k, cols],
                                wh[:, k, h * HALF:(h + 1) * HALF], wl[:, k, h * HALF:(h + 1) * HALF],
                                k == 0, k == kc - 1)
        return last

    def polish(link, r, v, tmp):
        link(nc.vector.tensor_tensor(tmp, r, r, ALU.mult))
        link(nc.vector.tensor_tensor(tmp, tmp, v, ALU.mult))
        link(nc.vector.tensor_scalar(tmp, tmp, -0.5, 1.5, ALU.mult, ALU.add))
        link(nc.vector.tensor_tensor(r, r, tmp, ALU.mult))

    def norm_block(tag, src_dram, xs, then, sink=None):
        with ExitStack() as ctx:
            sb = allocate(ctx)
            tmp, mv = sb(tag + "tmp", [NT, T, 12]), sb(tag + "mv", [NT, T, 2])
            std, rstd = sb(tag + "std", [NT, T]), sb(tag + "rstd", [NT, T])
            var = sb(tag + "var", [NT, T])
            ld, st, sq, ch, co = (sem(tag + n) for n in ("loaded", "stats", "sqrt", "chain", "const"))
            block = ctx.enter_context(nc.Block())

            @block.sync
            def _(sp):
                if src_dram is not None:
                    sp.dma_start(xs[:, :, :], tiled(src_dram)).then_inc(ld, 16)

            @block.gpsimd
            def _(pool):
                if tag == "ln_x":
                    nc.gpsimd.memset(ident[:, :], 0.0).then_inc(co, 1)
                    nc.gpsimd.memset(identh[:, :], 0.0).then_inc(co, 1)
                    nc.gpsimd.memset(ones[:, :], 1.0).then_inc(co, 1)
                    pool.iota(iota16[:, :], pattern=[[1, N]], base=0, channel_multiplier=0,
                              allow_small_or_imprecise_dtypes=True).then_inc(co, 1)
                    pool.wait_ge(co, 4)
                    for m in (ident, identh):
                        nc.gpsimd.affine_select(out=m[:, :], in_=m[:, :], compare_op=ALU.not_equal, fill=1.0, base=0,
                                                pattern=[[-1, 128]], channel_multiplier=1).then_inc(co, 1)
                    nc.gpsimd.affine_select(out=prefix[:, :], in_=ones[0:NT, 0:NT], compare_op=ALU.is_gt, fill=0.0,
                                            base=0, pattern=[[1, NT]], channel_multiplier=-1).then_inc(co, 1)

            @block.scalar
            def _(act):
                act.wait_ge(st, 1)
                nc.scalar.activation(std[:, :], var[:, :], ACT.Sqrt).then_inc(sq, 1)

            @block.vector
            def _(dve):
                link = Chain(dve, ch)
                if src_dram is not None:
                    dve.wait_ge(ld, 16)
                for t in range(T):
                    stats(dve, link, xs, tmp, mv, t)
                nc.vector.tensor_scalar(var[:, :], mv[:, :, 1], EPS, None, ALU.add).then_inc(st, 1)
                dve.wait_ge(sq, 1)
                link(nc.vector.reciprocal(rstd[:, :], std[:, :]))
                polish(link, rstd[:, :], var[:, :], std[:, :])
                for t in range(T):
                    then(dve, link, t, mv[:, t, 0:1], rstd[:, t:t + 1])

    def transpose_block(tag, xs, ah, al):
        with ExitStack() as ctx:
            tr, hi, lo = (sem(tag + n) for n in ("transposed", "high", "low"))
            block = ctx.enter_context(nc.Block())

            def part(m, t):
                return m[:, :, t * NT:(t + 1) * NT].rearrange("p (h k) n -> p h k n", h=2)

            def src(t):
                return psum[:, 2 * (t % 4):2 * (t % 4) + 2, 0:3 * NT].rearrange("p h (k n) -> p h k n", k=3)

            @block.tensor
            def _(pe):
                for t in range(T):
                    if t >= 4:
                        pe.wait_ge(lo, 2 * (t - 3))
                    for k in range(KC):
                        o = psum[:, 2 * (t % 4) + k // 3, (k % 3) * NT:(k % 3 + 1) * NT]
                        last = nc.tensor.transpose(o, xs[:, t, k * 128:(k + 1) * 128], ident[0:NT, 0:NT])
                    last.then_inc(tr, 1)

            @block.scalar
            def _(act):
                for t in range(T):
                    act.wait_ge(tr, t + 1)
                    for h in range(2):
                        nc.scalar.activation(part(ah, t)[:, h], src(t)[:, h], ACT.Copy).then_inc(hi, 1)

            @block.vector
            def _(dve):
                for t in range(T):
                    dve.wait_ge(hi, 2 * t + 2)
                    for h in range(2):
                        nc.vector.tensor_tensor(part(al, t)[:, h], src(t)[:, h], part(ah, t)[:, h].bitcast(F32),
                                                ALU.subtract).then_inc(lo, 1)

    def rows_block(tag, ah, al, weights, sink, kc=KC, loads=(), stores=()):
        with ExitStack() as ctx:
            sb = allocate(ctx)
            raw = sb(tag + "raw", [128, kc, D])
            wh, wl = sb(tag + "wh", [128, kc, D], F32R), sb(tag + "wl", [128, kc, D], F32R)
            ld, hi, lo, mm, ev, ch, xt = (sem(tag + n) for n in ("loaded", "high", "low", "product", "taken", "chain", "extra"))
            block = ctx.enter_context(nc.Block())
            J = len(weights)

            @block.sync
            def _(sp):
                for j, w in enumerate(weights):
                    if j:
                        sp.wait_ge(lo, j)
                    sp.dma_start(raw[:, :, :], chunked(w)).then_inc(ld, 16)
                for to, src in loads:
                    sp.dma_start(to, src).then_inc(xt, 16)
                for n, (to, src) in enumerate(stores):
                    sp.wait_ge(ev, T * (len(weights) - 1) + n + 1)
                    sp.dma_start(to, src).then_inc(xt, 16)
                sp.wait_ge(xt, 16 * (len(loads) + len(stores))) if stores else None

            @block.scalar
            def _(act):
                for j in range(J):
                    act.wait_ge(ld, 16 * (j + 1))
                    if j:
                        act.wait_ge(mm, T * j)
                    nc.scalar.activation(wh[:, :, :], raw[:, :, :], ACT.Copy).then_inc(hi, 1)

            @block.vector
            def _(dve):
                link = Chain(dve, ch)
                if loads:
                    dve.wait_ge(xt, 16 * len(loads))
                for j in range(J):
                    dve.wait_ge(hi, j + 1)
                    nc.vector.tensor_tensor(wl[:, :, :], raw[:, :, :], wh[:, :, :].bitcast(F32),
                                            ALU.subtract).then_inc(lo, 1)
                    for t in range(T):
                        dve.wait_ge(mm, T * j + t + 1)
                        sink(dve, link, j, t, wide(t % 4)).then_inc(ev, 1)

            @block.tensor
            def _(pe):
                for j in range(J):
                    pe.wait_ge(lo, j + 1)
                    for t in range(T):
                        n = T * j + t
                        if n >= 4:
                            pe.wait_ge(ev, n - 3)
                            if j and t < 4:
                                pe.wait_ge(ev, T * j)
                        rows_mm(t % 4, ah, al, wh, wl, slice(t * NT, (t + 1) * NT), kc).then_inc(mm, 1)

    tab, tab_rows = scr["table"], scr["table"].rearrange("(q b) f -> q b f", q=EB)
    y = scr["y"]
    yv = y.rearrange("(i p) d -> i p d", p=NT)

    graph = ExitStack()
    sbg = allocate(graph)
    tile_of = sbg("tile_of", [1, NSBP], I32)
    records = sbg("records", [EB, max(EC * 5, NBP * 4)])
    rec = records[0:NT, 0:EC * 5].rearrange("p (c f) -> p c f", f=5)
    table = records[:, 0:NBP * 4].rearrange("p (b f) -> p b f", f=4)
    ct = sbg("ct", [NT, T, N], U16)
    cnt = sbg("cnt", [R, N + 2])
    xform = ExitStack()
    sbx = allocate(xform)
    ath, atl = sbx("ath", [128, KC, N], F32R), sbx("atl", [128, KC, N], F32R)

    with ExitStack() as ctx:
        xs = allocate(ctx)("xs", [NT, T, D])
        norm_block("ln_x", a["x"], xs, lambda dve, link, t, m, r: link(
            nc.vector.tensor_scalar(xs[:, t, :], xs[:, t, :], m, r, ALU.subtract, ALU.mult)))
        transpose_block("tr_x", xs, ath, atl)

    def order_block():
        with ExitStack() as ctx:
            sb = allocate(ctx)
            raw = sb("raw_edges", [NT, 3, EC], I32)
            edge = sb("edge", [NT, 3, EC])
            tid, pos, tmp = sb("tid", [NT, EC]), sb("pos", [NT, EC]), sb("tmp", [NT, EC])
            hot, inc = sb("hot", [NT, T, EC]), sb("inc", [NT, T, EC])
            one = sb("one_row", [NT, EC])
            total, both, nb, cum = sb("total", [NT, T]), sb("both", [NT, 2, T]), sb("nb", [NT, T]), sb("cum", [NT, T])
            off, first = sb("off", [NT, T]), sb("first", [NT, T])
            sbi, sbt = sb("sbi", [1, NSBP]), sb("sbt", [1, NSBP])
            fill = sb("fill", [128, NBP, 4])
            ld, ch, co, tt, px, fl, pr = (sem("ord_" + n) for n in ("loaded", "chain", "const", "total", "prefix", "fill", "prepared"))
            block = ctx.enter_context(nc.Block())

            @block.sync
            def _(sp):
                for f, name in enumerate(("dst", "src", "edge_type_34")):
                    sp.dma_start(raw[:, f, :], a[name].rearrange("(p c) -> p c", p=NT)).then_inc(ld, 16)
                sp.wait_ge(pr, 1)
                sp.dma_start(tab_rows, fill[:, :, :]).then_inc(fl, 16)
                sp.wait_ge(fl, 16)

            @block.gpsimd
            def _(pool):
                pool.iota(sbi[:, :], pattern=[[1, NSBP]], base=0, channel_multiplier=0,
                          allow_small_or_imprecise_dtypes=True).then_inc(co, 1)

            @block.tensor
            def _(pe):
                pe.wait_ge(tt, 1)
                nc.tensor.matmul(psum[0:NT, 0, 0:T], prefix[:, :], total[:, :], start=True, stop=True)
                nc.tensor.matmul(psum[0:NT, 1, 0:T], ones[0:NT, 0:NT], total[:, :], start=True, stop=True).then_inc(px, 1)

            @block.vector
            def _(dve):
                link = Chain(dve, ch)
                link(nc.vector.memset(fill[:, :, :].bitcast(I32), 0))
                link(nc.vector.memset(fill[:, :, 2:3], -1.0))
                nc.vector.memset(one[:, :], 1.0).then_inc(pr, 1)
                dve.wait_ge(pr, 1)
                dve.wait_ge(ld, 48)
                dve.wait_ge(co, 1)
                link(nc.vector.tensor_copy(edge[:, :, :], raw[:, :, :]))
                dst, src, typ = edge[:, 0, :], edge[:, 1, :], edge[:, 2, :]
                link(nc.vector.tensor_scalar(tid[:, :], dst, float(NT), None, ALU.is_ge))
                for k in range(2, T):
                    link(nc.vector.scalar_tensor_tensor(tid[:, :], dst, float(NT * k), tid[:, :], ALU.is_ge, ALU.add))
                for k in range(T):
                    link(nc.vector.tensor_scalar(hot[:, k, :], tid[:, :], float(k), None, ALU.is_equal))
                    link(nc.vector.tensor_tensor_scan(inc[:, k, :], one[:, :], hot[:, k, :], 0.0, ALU.mult, ALU.add))
                nc.vector.tensor_copy(total[:, :], inc[:, :, EC - 1]).then_inc(tt, 1)
                link(nc.vector.scalar_tensor_tensor(rec[:, :, 0].bitcast(U32), typ, float(N), src, ALU.mult, ALU.add))
                link(nc.vector.tensor_copy(rec[:, :, 1], src))
                link(nc.vector.scalar_tensor_tensor(rec[:, :, 2], tid[:, :], -float(NT), dst, ALU.mult, ALU.add))
                link(nc.vector.tensor_copy(rec[:, :, 3], typ))
                dve.wait_ge(px, 1)
                link(nc.vector.tensor_copy(both[:, 0, :], psum[0:NT, 0, 0:T]))
                link(nc.vector.tensor_copy(both[:, 1, :], psum[0:NT, 1, 0:T]))
                link(nc.vector.tensor_scalar(nb[:, :], both[:, 1, :], 1.0 / SBE, (SBE - 1.0) / SBE - 0.5 + 0.5 / SBE,
                                             ALU.mult, ALU.add))
                link(nc.vector.tensor_scalar(nb[:, :], nb[:, :], MAGIC, None, ALU.add))
                link(nc.vector.tensor_scalar(nb[:, :], nb[:, :], MAGIC, None, ALU.subtract))
                link(nc.vector.tensor_tensor_scan(cum[:, :], one[:, 0:T], nb[:, :], 0.0, ALU.mult, ALU.add))
                link(nc.vector.tensor_tensor(first[:, :], cum[:, :], nb[:, :], ALU.subtract))
                link(nc.vector.tensor_scalar(off[:, :], first[:, :], float(SBE), -1.0, ALU.mult, ALU.add))
                link(nc.vector.tensor_tensor(off[:, :], off[:, :], both[:, 0, :], ALU.add))
                for k in range(T):
                    dest = pos if k == 0 else tmp
                    link(nc.vector.scalar_tensor_tensor(dest[:, :], inc[:, k, :], off[:, k:k + 1], hot[:, k, :], ALU.add, ALU.mult))
                    if k:
                        link(nc.vector.tensor_tensor(pos[:, :], pos[:, :], tmp[:, :], ALU.add))
                link(nc.vector.tensor_scalar(tmp[:, :], pos[:, :], 1.0 / EB, -0.5 + 0.5 / EB, ALU.mult, ALU.add))
                link(nc.vector.tensor_scalar(tmp[:, :], tmp[:, :], MAGIC, None, ALU.add))
                link(nc.vector.tensor_scalar(tmp[:, :], tmp[:, :], MAGIC, None, ALU.subtract))
                link(nc.vector.scalar_tensor_tensor(pos[:, :], tmp[:, :], -float(EB), pos[:, :], ALU.mult, ALU.add))
                link(nc.vector.scalar_tensor_tensor(rec[:, :, 4].bitcast(U32), pos[:, :], float(NBP), tmp[:, :], ALU.mult, ALU.add))
                link(nc.vector.tensor_scalar(sbt[:, :], sbi[:, :], first[0:1, 1:2], None, ALU.is_ge))
                for k in range(2, T):
                    link(nc.vector.scalar_tensor_tensor(sbt[:, :], sbi[:, :], first[0:1, k:k + 1], sbt[:, :], ALU.is_ge, ALU.add))
                link(nc.vector.tensor_copy(tile_of[:, :], sbt[:, :]))

    order_block()

    def relation_block():
        with ExitStack() as ctx:
            sb = allocate(ctx)
            raw = sb("r_raw", [128, KC, D])
            wh = [sb(f"r_wh{s}", [128, KC, D], F32R) for s in range(2)]
            wl = [sb(f"r_wl{s}", [128, KC, D], F32R) for s in range(2)]
            ys = [sb(f"ys{s}", [NT, D]) for s in range(2)]
            rcur = [sb(f"rcur{s}", [NT, 5]) for s in range(2)]
            cur = [sb(f"c_cur{s}", [EB, G, 4]) for s in range(2)]
            src = [sb(f"c_src{s}", [EB, G, N], F16) for s in range(2)]
            dst = [sb(f"c_dst{s}", [EB, G, NT], F16) for s in range(2)]
            rel = [sb(f"c_rel{s}", [EB, G, R], F16) for s in range(2)]
            deg, tmp = sb("deg", [NT, T]), sb("c_tmp", [NT, T])
            ld, hi, lo, mm, ev = (sem("rel_" + n) for n in ("loaded", "high", "low", "product", "taken"))
            yst, sct, cp = sems("y_stored", 2), sems("scattered", 2), sem("record_copied")
            tl, ch, hot, cm, fl, dg, sq = (sem("cnt_" + n) for n in (
                "table_loaded", "chain", "onehot", "product", "added", "degree", "sqrt"))
            block = ctx.enter_context(nc.Block())
            weights = a["L0_gnn_W_rel"].rearrange("r (k p) n -> r p k n", p=128)
            FREE = 2
            DONE = 1
            DEGREES = 3

            @block.sync
            def _(sp):
                sp.dma_start(raw[:, :, :], weights[0]).then_inc(ld, 16)
                sp.wait_ge(lo, 1)
                sp.dma_start(raw[:, :, :], weights[1]).then_inc(ld, 16)

                def pair(p, row, following):
                    for s in range(2):
                        for t in range(T):
                            n = s * T + t
                            sp.wait_ge(ev, p * PT + n + 1 + FREE)
                            sp.dma_start(row(n), ys[n % 2][:, :]).then_inc(yst[n % 2], 16)
                        if following is not None:
                            sp.wait_ge(lo, p * 2 + s + 2)
                            sp.dma_start(raw[:, :, :], following(s)).then_inc(ld, 16)

                def pairs(p0, p1):
                    with sp.Fori(p0, p1) as p:
                        pair(p, lambda n: yv[bass.ds(p * PT + n, 1)].rearrange("a p d -> (a p) d"),
                             lambda s: weights[bass.ds(p * 2 + s + 2, 1)].rearrange("a p k n -> (a p) k n"))

                pairs(0, COUNT_FROM)
                for s in range(2):
                    sp.wait_ge(sct[s], 16 * (EC // 2))
                sp.dma_start(table[:, :, :], tab_rows).then_inc(tl, 16)
                pairs(COUNT_FROM, PAIRS - 2)
                pair(PAIRS - 2, lambda n: yv[(PAIRS - 2) * PT + n],
                     lambda s: chunked((a["L0_gnn_W_root"], a["L0_mix_w_qkv"])[s]))
                pair(PAIRS - 1, lambda n: yv[(PAIRS - 1) * PT + n], None)
                for s in range(2):
                    sp.wait_ge(yst[s], 16 * (NREL * T // 2))

            @block.scalar
            def _(act):
                act.wait_ge(ld, 16)
                nc.scalar.activation(wh[0][:, :, :], raw[:, :, :], ACT.Copy).then_inc(hi, 1)

                def pair(p, last):
                    for n in range(PT):
                        s, t = n // T, n % T
                        act.wait_ge(mm, p * PT + n + 1 + DONE)
                        if n >= 2 or not isinstance(p, int) or p:
                            act.wait_ge(yst[n % 2], p * (PT // 2 * 16) + (n // 2) * 16)
                        nc.scalar.activation(halves(ys[n % 2][:, :]), wide(n % 2), ACT.Copy).then_inc(ev, 1)
                        if t == 0 and not (last and s == 1):
                            act.wait_ge(ld, p * 32 + s * 16 + 32)
                            nc.scalar.activation(wh[1 - s][:, :, :], raw[:, :, :], ACT.Copy).then_inc(hi, 1)
                        if last and n == T:
                            act.wait_ge(ch, NSBP + DEGREES)
                            nc.scalar.activation(dinv[:, :], deg[:, :], ACT.Sqrt).then_inc(sq, 1)

                pair(0, False)
                with act.Fori(1, PAIRS - 1) as p:
                    pair(p, False)
                pair(PAIRS - 1, True)

            @block.vector
            def _(dve):
                def low(s):
                    return nc.vector.tensor_tensor(wl[s][:, :, :], raw[:, :, :], wh[s][:, :, :].bitcast(F32), ALU.subtract)

                link = Chain(dve, ch)
                dve.wait_ge(hi, 1)
                low(0).then_inc(lo, 1)
                link(nc.vector.memset(ct[:, :, :], 0))
                link(nc.vector.memset(cnt[:, :], 0.0))
                with dve.Fori(0, COUNT_FROM) as p:
                    for s in range(2):
                        dve.wait_ge(hi, p * 2 + s + 2)
                        low(1 - s).then_inc(lo, 1)

                def onehots(s, c):
                    link(nc.vector.tensor_copy(cur[s][:, :, :], table[:, bass.ds(c * G, G), :]))
                    for g in range(G):
                        nc.vector.tensor_scalar(src[s][:, g, :], iota16[:, :], cur[s][:, g, 1:2], None, ALU.is_equal)
                        nc.vector.tensor_scalar(dst[s][:, g, :], iota16[:, 0:NT], cur[s][:, g, 2:3], None, ALU.is_equal)
                        ins = nc.vector.tensor_scalar(rel[s][:, g, :], iota16[:, 0:R], cur[s][:, g, 3:4], None, ALU.is_equal)
                    ins.then_inc(hot, 1)

                def add(c):
                    v = dve.value_load(tile_of[0:1, bass.ds(c, 1)], min_val=0, max_val=T - 1)
                    d = bass.ds(v * NT, NT)
                    dve.wait_ge(cm, c + 1)
                    a8 = ct[:, 0:8, d].rearrange("p (a b) n -> p a b n", a=2)
                    nc.vector.tensor_tensor(a8, a8, psum[0:NT, 4:6, 0:4 * NT].rearrange("p a (b n) -> p a b n", b=4), ALU.add)
                    nc.vector.tensor_tensor(ct[:, 8:10, d], ct[:, 8:10, d],
                                            psum[0:NT, 6, 0:2 * NT].rearrange("p (b n) -> p b n", b=2), ALU.add)
                    nc.vector.tensor_tensor(cnt[:, d], cnt[:, d], psum[0:R, 6, 2 * NT:3 * NT], ALU.add).then_inc(fl, 1)
                    dve.wait_ge(fl, c + 2)

                dve.wait_ge(tl, 16)
                onehots(0, 0)
                with dve.Fori(0, COUNT_PAIRS) as q:
                    link.enter(q, PT)
                    for n in range(PT):
                        onehots((n + 1) % 2, q * PT + n + 1)
                        add(q * PT + n)
                        if n % T == 3:
                            dve.wait_ge(hi, q * 2 + (COUNT_FROM * 2 + n // T + 2))
                            low(1 - n // T).then_inc(lo, 1)
                    link.leave(COUNT_PAIRS)
                dve.wait_ge(hi, (PAIRS - 1) * 2 + 2)
                low(1).then_inc(lo, 1)
                dve.wait_ge(dg, 1)
                link(nc.vector.tensor_scalar(deg[:, :], psum[0:NT, 7, 0:T], 1.0, None, ALU.add))
                dve.wait_ge(sq, 1)
                link(nc.vector.reciprocal(dinv[:, :], dinv[:, :]))
                polish(link, dinv[:, :], deg[:, :], tmp[:, :])
                link(nc.vector.tensor_scalar(cnt[:, :], cnt[:, :], 1.0, None, ALU.max))
                link(nc.vector.reciprocal(cnt[:, :], cnt[:, :]))

            @block.tensor
            def _(pe):
                pe.sem_inc(mm, DONE)
                pe.sem_inc(ev, FREE)
                pe.sem_inc(fl, 1)

                def count(s, c):
                    pe.wait_ge(hot, c + 1)
                    pe.wait_ge(fl, c + 1)
                    for g in range(G):
                        for i in range(T):
                            nc.tensor.matmul(psum[0:NT, 4 + i // 4, (i % 4) * NT:(i % 4 + 1) * NT],
                                             src[s][:, g, i * NT:(i + 1) * NT], dst[s][:, g, :],
                                             start=(g == 0 and i % 4 == 0), stop=(g == G - 1), skip_group_check=True)
                        last = nc.tensor.matmul(psum[0:R, 6, 2 * NT:3 * NT], rel[s][:, g, :], dst[s][:, g, :],
                                                start=False, stop=(g == G - 1), skip_group_check=True)
                    last.then_inc(cm, 1)

                def pair(p, c=None, degrees=False):
                    for n in range(PT):
                        s, t = n // T, n % T
                        if t == 0:
                            pe.wait_ge(lo, p * 2 + s + 1)
                        pe.wait_ge(ev, p * PT + n - 1 + FREE)
                        rows_mm(n % 2, ath, atl, wh[s], wl[s], slice(t * NT, (t + 1) * NT)).then_inc(mm, 1)
                        if c is not None:
                            count(n % 2, c * PT + n)
                        if degrees and n == 1:
                            pe.wait_ge(fl, COUNT_PAIRS * PT + 1)
                            for i in range(T):
                                last = nc.tensor.matmul(psum[0:NT, 7, i:i + 1], cnt[:, i * NT:(i + 1) * NT], ones[0:R, 0:1],
                                                        start=True, stop=True)
                            last.then_inc(dg, 1)

                with pe.Fori(0, COUNT_FROM) as p:
                    pair(p)
                with pe.Fori(0, COUNT_PAIRS) as q:
                    pair(q + COUNT_FROM, q)
                pair(PAIRS - 1, degrees=True)

            @block.gpsimd
            def _(pool):
                def scatter(c, s, first):
                    if not first:
                        pool.wait_ge(sct[s], c * 16)
                    nc.gpsimd.tensor_copy(rcur[s][:, :].bitcast(U32),
                                          rec[:, bass.ds(c * 2 + s, 1), :].rearrange("p a f -> p (a f)").bitcast(U32)).then_inc(cp, 1)
                    pool.wait_ge(cp, c * 2 + s + 1)
                    pool.nop(nofuse=True)
                    pool.indirect_dma_start(out=tab, out_offset=bass.IndirectOffsetOnAxis(rcur[s][:, 4:5].bitcast(U32), 0),
                                            in_=rcur[s][:, 0:4], in_offset=None).then_inc(sct[s], 16)

                scatter(0, 0, True)
                scatter(0, 1, True)
                with pool.Fori(1, EC // 2) as c:
                    scatter(c, 0, False)
                    scatter(c, 1, False)
                for s in range(2):
                    pool.wait_ge(sct[s], 16 * (EC // 2))

    relation_block()
    xform.close()

    room = [allocate(top, side="right")(f"room{i}", [128, T * D]) for i in range(1)]
    acc = room[0][0:NT, :].rearrange("p (t d) -> p t d", t=T)

    def gather_block():
        with ExitStack() as ctx:
            sb = allocate(ctx)
            SL = 4 * G
            PIECES = 8
            yg = [sb(f"yg{s}", [EB, D]) for s in range(SL)]
            row = [sb(f"row{s}", [EB, 1], U32) for s in range(SL)]
            cur = [sb(f"g_cur{s}", [EB, G, 4]) for s in range(4)]
            rel = sb("g_rel", [EB, NBP, R], F16)
            relt = [sb(f"g_relt{s}", [R, G, EB], F32R) for s in range(2)]
            parts = sb("inv_parts", [R, 2, N + 2], F32R)
            inv = [sb(f"g_inv{s}", [R, 2, NT + 1], F32R) for s in range(2)]
            sel = [sb(f"g_sel{s}", [EB, G, NT]) for s in range(4)]
            bias = sb("g_bias", [NT, D])
            iota32 = sb("iota32", [EB, NT])
            gl = sems("rows_gathered", SL)
            cp, ld, ch, hot, ip, trn, rt, vv, sl, mm, fl = (sem("gat_" + n) for n in (
                "row_copied", "loaded", "chain", "onehot", "inverse_parts", "transposed", "relation_rows", "weights",
                "selector", "product", "added"))
            block = ctx.enter_context(nc.Block())
            LAST = NSB + 2
            cuts = [min(NBP, round(NBP * i / PIECES)) for i in range(PIECES + 1)]

            @block.sync
            def _(sp):
                sp.dma_start(acc[:, :, :], tiled(y[R * N:(R + 1) * N, :])).then_inc(ld, 16)
                sp.dma_start(bias[:, :], spread(a["L0_gnn_b_rgcn"], NT)).then_inc(ld, 16)

            @block.gpsimd
            def _(pool):
                def fetch(i, s, first):
                    if not first:
                        pool.wait_ge(mm, (i - 1) * (SL // G) + s // G + 1)
                    nc.gpsimd.tensor_copy(row[s][:, :], table[:, bass.ds(i * SL + s, 1), 0:1].rearrange("p a f -> p (a f)").bitcast(U32)).then_inc(cp, 1)
                    pool.wait_ge(cp, i * SL + s + 1)
                    pool.nop(nofuse=True)
                    pool.indirect_dma_start(out=yg[s][:, :], out_offset=None, in_=y,
                                            in_offset=bass.IndirectOffsetOnAxis(row[s][:, :], 0)).then_inc(gl[s], 16)

                for s in range(SL):
                    fetch(0, s, True)
                with pool.Fori(1, NB // SL) as i:
                    for s in range(SL):
                        fetch(i, s, False)

            @block.scalar
            def _(act):
                act.wait_ge(ip, 1)
                with act.Fori(0, LAST // 2) as p:
                    for s in range(2):
                        n = p * 2 + s
                        v = act.value_load(tile_of[0:1, bass.ds(n, 1)], min_val=0, max_val=T - 1)
                        act.wait_ge(trn, n + 1)
                        nc.scalar.activation(inv[s][:, :, :], parts[:, :, bass.ds(v * NT, NT + 1)].bitcast(F32), ACT.Copy)
                        nc.scalar.activation(relt[s][:, :, :], psum[0:R, 4 + s, 0:G * EB].rearrange("p (g e) -> p g e", g=G),
                                             ACT.Copy).then_inc(rt, 1)

            @block.tensor
            def _(pe):
                pe.sem_inc(fl, 2)

                def transposes(s, n):
                    for g in range(G):
                        last = nc.tensor.matmul(psum[0:R, 4 + s, g * EB:(g + 1) * EB], rel[:, bass.ds(n * G + g, 1), :].rearrange("p a r -> p (a r)"),
                                                identh[:, :], start=True, stop=True)
                    last.then_inc(trn, 1)

                def weights(s, n):
                    pe.wait_ge(rt, n + 1)
                    for g in range(G):
                        for part in range(2):
                            last = nc.tensor.matmul(psum[:, 6 + s, g * EB:g * EB + NT + 1], relt[s][:, g, :], inv[s][:, part, :],
                                                    start=(part == 0), stop=(part == 1))
                    last.then_inc(vv, 1)

                def sums(p, q, n):
                    s = q % 2
                    pe.wait_ge(sl, n + 1)
                    pe.wait_ge(fl, n + 1)
                    for g in range(G):
                        slot = G * q + g
                        pe.wait_ge(gl[slot], p * 16 + 16)
                        for h in range(2):
                            last = nc.tensor.matmul(psum[0:NT, 2 * s + h, 0:HALF], sel[q][:, g, :], yg[slot][:, h * HALF:(h + 1) * HALF],
                                                    start=(g == 0), stop=(g == G - 1))
                    last.then_inc(mm, 1)

                pe.wait_ge(hot, 1)
                transposes(0, 0)
                transposes(1, 1)
                weights(0, 0)
                transposes(0, 2)
                weights(1, 1)
                pe.wait_ge(hot, PIECES)
                with pe.Fori(0, NSB // 4) as p:
                    for q in range(4):
                        n = p * 4 + q
                        transposes((q + 1) % 2, n + 3)
                        pe.wait_ge(sl, n + 1)
                        weights(q % 2, n + 2)
                        sums(p, q, n)

            @block.vector
            def _(dve):
                link = Chain(dve, ch)
                link(nc.vector.tensor_copy(parts[:, 0, :], cnt[:, :]))
                nc.vector.tensor_tensor(parts[:, 1, :], cnt[:, :], parts[:, 0, :].bitcast(F32), ALU.subtract).then_inc(ip, 1)
                for c0, c1 in zip(cuts, cuts[1:]):
                    nc.vector.tensor_tensor(rel[:, c0:c1, :], table[:, c0:c1, 3:4].broadcast_to([EB, c1 - c0, R]),
                                            iota16[:, 0:R].unsqueeze(1).broadcast_to([EB, c1 - c0, R]), ALU.is_equal).then_inc(hot, 1)
                link(nc.vector.tensor_copy(iota32[:, :], iota16[:, 0:NT]))

                def select(q, n):
                    link(nc.vector.tensor_copy(cur[q][:, :, :], table[:, bass.ds(n * G, G), :]))
                    dve.wait_ge(vv, n + 1)
                    for g in range(G):
                        ins = nc.vector.scalar_tensor_tensor(sel[q][:, g, :], iota32[:, :], cur[q][:, g, 2:3],
                                                             psum[:, 6 + q % 2, g * EB:g * EB + NT], ALU.is_equal, ALU.mult)
                    ins.then_inc(sl, 1)

                def add(s, n):
                    v = dve.value_load(tile_of[0:1, bass.ds(n, 1)], min_val=0, max_val=T - 1)
                    o = acc[:, bass.ds(v, 1), :].rearrange("p a (h n) -> p (a h) n", h=2)
                    dve.wait_ge(mm, n + 1)
                    nc.vector.tensor_tensor(o, o, wide(s), ALU.add).then_inc(fl, 1)

                select(0, 0)
                select(1, 1)
                dve.wait_ge(ld, 32)
                with dve.Fori(0, NSB // 4) as p:
                    link.enter(p, 4)
                    for q in range(4):
                        n = p * 4 + q
                        select((q + 2) % 4, n + 2)
                        dve.wait_ge(fl, n + 2)
                        add(q % 2, n)
                    link.leave(NSB // 4)
                dve.wait_ge(fl, NSB + 2)
                for t in range(T):
                    nc.vector.tensor_tensor(acc[:, t, :], acc[:, t, :], bias[:, :], ALU.add)

    gather_block()

    def bias_row(ctx, name, src):
        return allocate(ctx)(name, [NT, D]), spread(src, NT)

    with ExitStack() as ctx:
        sb = allocate(ctx)
        hh, hl = sb("h1_high", [128, KC, N], F32R), sb("h1_low", [128, KC, N], F32R)
        transpose_block("tr_h1", acc, hh, hl)
        rows_block("gcn_", hh, hl, [a["L0_gnn_W_gcn"]], lambda dve, link, j, t, rows: nc.vector.tensor_scalar(
            halves(acc[:, t, :]), rows, dinv[:, t:t + 1], None, ALU.mult))

    room.append(allocate(top, side="right")("room1", [128, T * D]))
    gn = room[1][0:NT, :].rearrange("p (t d) -> p t d", t=T)

    def propagate_block():
        with ExitStack() as ctx:
            sb = allocate(ctx)
            ctf = sb("ctf", [NT, T, N])
            bias = sb("p_bias", [NT, D])
            ld, ch, rd, mm, ev = (sem("prop_" + n) for n in ("loaded", "chain", "ready", "product", "taken"))
            block = ctx.enter_context(nc.Block())

            @block.sync
            def _(sp):
                sp.dma_start(bias[:, :], spread(a["L0_gnn_b_gcn"], NT)).then_inc(ld, 16)

            @block.tensor
            def _(pe):
                for t in range(T):
                    pe.wait_ge(rd, t + 1)
                    if t >= 4:
                        pe.wait_ge(ev, t - 3)
                    for i in range(T):
                        for h in range(2):
                            last = nc.tensor.matmul(psum[0:NT, 2 * (t % 4) + h, 0:HALF], ctf[:, i, t * NT:(t + 1) * NT],
                                                    acc[:, i, h * HALF:(h + 1) * HALF], start=(i == 0), stop=(i == T - 1))
                    last.then_inc(mm, 1)

            @block.vector
            def _(dve):
                link = Chain(dve, ch)
                for t in range(T):
                    cols = slice(t * NT, (t + 1) * NT)
                    link(nc.vector.tensor_copy(ctf[:, :, cols], ct[:, :, cols]))
                    nc.vector.tensor_tensor(ctf[:, t, cols], ctf[:, t, cols], ident[0:NT, 0:NT], ALU.add).then_inc(rd, 1)
                dve.wait_ge(ld, 16)
                for t in range(T):
                    dve.wait_ge(mm, t + 1)
                    nc.vector.scalar_tensor_tensor(halves(gn[:, t, :]), wide(t % 4), dinv[:, t:t + 1], halves(bias[:, :]),
                                                   ALU.mult, ALU.add).then_inc(ev, 1)

    propagate_block()
    recycle()
    graph.close()

    w = acc

    def mix_block():
        with ExitStack() as ctx:
            sb = allocate(ctx)
            w2 = sb("w2", [NT, T, D])
            scale, tmp = sb("m_scale", [NT, D]), [sb(f"m_tmp{s}", [NT, D]) for s in range(2)]
            temp, lg = sb("m_temp", [NT, H]), sb("m_logits", [NT, T, H])
            lt, pt = sb("m_lt", [H, N]), sb("m_pt", [H, N])
            mx, sm, sp2 = sb("m_max", [H, 1]), sb("m_sum", [H, 1]), sb("m_sum2", [H, 1])
            pi, pn = sb("m_pi", [NT, T, H]), sb("m_pin", [NT, T, H])
            ld, ch, sq, cs, nr, tr, ex, bk, dt = (sem("mix_" + n) for n in (
                "loaded", "chain", "squared", "column_sums", "norms", "transposed", "exp", "back", "dots"))
            lc, pc, dd = sem("mix_logits_done"), sem("mix_pi_done"), sem("mix_dots_in")
            block = ctx.enter_context(nc.Block())

            def per_head(ap):
                return ap.unsqueeze(2).broadcast_to([NT, H, DH])

            def by_head(ap):
                return ap.rearrange("p (h d) -> p h d", h=H)

            @block.sync
            def _(sp):
                sp.dma_start(w[:, :, :], tiled(y[(R + 1) * N:(R + 2) * N, :])).then_inc(ld, 16)
                sp.dma_start(temp[:, :], spread(a["L0_mix_temp"].rearrange("h a -> (h a)"), NT)).then_inc(ld, 16)

            @block.tensor
            def _(pe):
                for t in range(T):
                    pe.wait_ge(sq, t + 1)
                    for h in range(2):
                        last = nc.tensor.matmul(psum[0:NT, h, 0:HALF], ones[0:NT, 0:NT], w2[:, t, h * HALF:(h + 1) * HALF],
                                                start=(t == 0), stop=(t == T - 1))
                last.then_inc(cs, 1)
                for t in range(T):
                    pe.wait_ge(lc, t + 1)
                    last = nc.tensor.transpose(psum[0:H, 2 + t // 4, (t % 4) * NT:(t % 4 + 1) * NT], lg[:, t, :], ident[0:NT, 0:NT])
                last.then_inc(tr, 1)
                pe.wait_ge(pc, 1)
                for n, m in enumerate((lt, pt)):
                    for t in range(T):
                        last = nc.tensor.transpose(psum[0:NT, 5 + n, t * H:(t + 1) * H], m[:, t * NT:(t + 1) * NT], ident[0:H, 0:H])
                last.then_inc(bk, 1)
                for t in range(T):
                    pe.wait_ge(dd, t + 1)
                    for h in range(2):
                        last = nc.tensor.matmul(psum[0:NT, h, 0:HALF], ones[0:NT, 0:NT], w2[:, t, h * HALF:(h + 1) * HALF],
                                                start=(t == 0), stop=(t == T - 1))
                last.then_inc(dt, 1)

            @block.scalar
            def _(act):
                act.wait_ge(cs, 1)
                nc.scalar.activation(halves(scale[:, :]), wide(0), ACT.Sqrt).then_inc(nr, 1)
                act.wait_ge(ex, 1)
                nc.scalar.activation(lt[:, :], lt[:, :], ACT.Exp, bias=mx[:, :], accum_out=sm[:, :]).then_inc(nr, 1)

            @block.vector
            def _(dve):
                link = Chain(dve, ch)
                dve.wait_ge(ld, 32)
                for t in range(T):
                    nc.vector.tensor_tensor(w2[:, t, :], w[:, t, :], w[:, t, :], ALU.mult).then_inc(sq, 1)
                dve.wait_ge(nr, 1)
                link(nc.vector.tensor_scalar(scale[:, :], scale[:, :], 1e-12, None, ALU.max))
                link(nc.vector.reciprocal(scale[:, :], scale[:, :]))
                dve.wait_ge(sq, T)
                for t in range(T):
                    x = tmp[t % 2]
                    link(nc.vector.tensor_tensor(x[:, :], w[:, t, :], scale[:, :], ALU.mult))
                    link(nc.vector.tensor_tensor(x[:, :], x[:, :], x[:, :], ALU.mult))
                    link(nc.vector.tensor_reduce(lg[:, t, :], by_head(x[:, :]), AX.X, ALU.add))
                    nc.vector.tensor_tensor(lg[:, t, :], lg[:, t, :], temp[:, :], ALU.mult).then_inc(lc, 1)
                dve.wait_ge(tr, 1)
                link(nc.vector.tensor_copy(lt[:, 0:8 * NT].rearrange("p (a n) -> p a n", a=2), psum[0:H, 2:4, 0:4 * NT]))
                link(nc.vector.tensor_copy(lt[:, 8 * NT:N], psum[0:H, 4, 0:2 * NT]))
                link(nc.vector.tensor_reduce(mx[:, :], lt[:, :], AX.X, ALU.max))
                nc.vector.tensor_scalar(mx[:, :], mx[:, :], -1.0, None, ALU.mult).then_inc(ex, 1)
                dve.wait_ge(nr, 2)
                link(nc.vector.reciprocal(sm[:, :], sm[:, :]))
                link(nc.vector.tensor_scalar(lt[:, :], lt[:, :], sm[:, :], None, ALU.mult))
                link(nc.vector.tensor_reduce(sp2[:, :], lt[:, :], AX.X, ALU.add))
                link(nc.vector.tensor_scalar(sp2[:, :], sp2[:, :], 1e-8, None, ALU.add))
                link(nc.vector.reciprocal(sp2[:, :], sp2[:, :]))
                nc.vector.tensor_scalar(pt[:, :], lt[:, :], sp2[:, :], None, ALU.mult).then_inc(pc, 1)
                dve.wait_ge(bk, 1)
                link(nc.vector.tensor_copy(pi[:, :, :], psum[0:NT, 5, 0:T * H].rearrange("p (t h) -> p t h", t=T)))
                link(nc.vector.tensor_copy(pn[:, :, :], psum[0:NT, 6, 0:T * H].rearrange("p (t h) -> p t h", t=T)))
                for t in range(T):
                    nc.vector.tensor_tensor(by_head(w2[:, t, :]), by_head(w2[:, t, :]), per_head(pn[:, t, :]), ALU.mult).then_inc(dd, 1)
                    link(nc.vector.tensor_tensor(by_head(w[:, t, :]), by_head(w[:, t, :]), per_head(pi[:, t, :]), ALU.mult))
                dve.wait_ge(dt, 1)
                link(nc.vector.tensor_scalar(halves(scale[:, :]), wide(0), 1.0, None, ALU.add))
                link(nc.vector.reciprocal(scale[:, :], scale[:, :]))
                link(nc.vector.tensor_scalar(scale[:, :], scale[:, :], -1.0, None, ALU.mult))
                for t in range(T):
                    link(nc.vector.tensor_tensor(w[:, t, :], w[:, t, :], scale[:, :], ALU.mult))

    mix_block()

    with ExitStack() as ctx:
        sb = allocate(ctx)
        hh, hl = sb("mix_high", [128, KC, N], F32R), sb("mix_low", [128, KC, N], F32R)
        transpose_block("tr_mix", w, hh, hl)
        bias = sb("o_bias", [NT, D])

        def sink(dve, link, j, t, rows):
            g = halves(gn[:, t, :])
            link(nc.vector.tensor_tensor(g, g, rows, ALU.add))
            link(nc.vector.tensor_tensor(gn[:, t, :], gn[:, t, :], bias[:, :], ALU.add))
            return nc.vector.tensor_tensor(gn[:, t, :], gn[:, t, :], w[:, t, :], ALU.add)

        rows_block("wout_", hh, hl, [a["L0_mix_w_out"]], sink,
                   loads=[(bias[:, :], spread(a["L0_mix_b_out"], NT)), (w[:, :, :], tiled(a["x"]))],
                   stores=[(scr["x1"][t * NT:(t + 1) * NT, :], gn[:, t, :]) for t in range(T)])

    nrm = gn
    norm_block("ln_h", None, nrm, lambda dve, link, t, m, r: link(
        nc.vector.tensor_scalar(nrm[:, t, :], nrm[:, t, :], m, r, ALU.subtract, ALU.mult)))

    def affine_norm(tag, xs, g, b, store):
        with ExitStack() as ctx:
            sb = allocate(ctx)
            gain, shift = sb(tag + "gain", [NT, D]), sb(tag + "shift", [NT, D])
            gl, st = sem(tag + "gain_loaded"), sem(tag + "stored")
            with ExitStack() as c2:
                block = c2.enter_context(nc.Block())

                @block.sync
                def _(sp):
                    sp.dma_start(gain[:, :], spread(g, NT)).then_inc(gl, 16)
                    sp.dma_start(shift[:, :], spread(b, NT)).then_inc(gl, 16)
                    sp.dma_start(tiled(store), xs[:, :, :]).then_inc(st, 16)
                    sp.wait_ge(gl, 32)
                    sp.wait_ge(st, 16)

            def then(dve, link, t, m, r):
                link(nc.vector.tensor_scalar(xs[:, t, :], xs[:, t, :], m, r, ALU.subtract, ALU.mult))
                link(nc.vector.tensor_tensor(xs[:, t, :], xs[:, t, :], gain[:, :], ALU.mult))
                link(nc.vector.tensor_tensor(xs[:, t, :], xs[:, t, :], shift[:, :], ALU.add))

            norm_block(tag, None, xs, then)

    affine_norm("ln_1", nrm, a["L0_ffn_g1"], a["L0_ffn_b1"], scr["hidden"])

    keep = ExitStack()
    sbk = allocate(keep)
    selt = sbk("selt", [TH, 2, N])
    unrouted = sbk("unrouted", [NT, T])
    score = sbk("score", [NT, T])
    pooled_w = sbk("pooled_w", [NT, D])
    qt = sbk("qt", [128, KC, TOP])

    def route_block():
        with ExitStack() as ctx:
            sb = allocate(ctx)
            wr, br = sb("wr", [NT, D]), sb("br", [NT, 1])
            wm, wq = sb("r_wm", [128, KC, D]), sb("r_wq", [128, KC, D])
            bq = sb("r_bq", [128, KC])
            junk, junk2 = sb("r_junk", [NT, N]), sb("r_junk2", [NT, N])
            z, e, idx, rank, ties = (sb("r_" + n, [NT, T]) for n in ("z", "e", "idx", "rank", "ties"))
            srow, rrow = sb("srow", [NT, N]), sb("rrow", [TH, N])
            iota, iotaj = sb("r_iota", [NT, N]), sb("r_iotaj", [TH, 2])
            sel = sb("sel", [NT, T, TOP])
            nselt = sb("nselt", [128, KC, TOP])
            total, pt, ptb = sb("r_total", [128, 1]), sb("r_pt", [128, KC]), sb("r_ptb", [128, KC, NT])
            ld, ldw, co, ch, zs, ex, sc, sd, rk, rd = (sem("rt_" + n) for n in (
                "loaded", "weights_loaded", "const", "chain", "z", "exp", "scores", "score_rows", "ranks", "rank_rows"))
            po, pd, sl, ns, nd, qd, pw = (sem("rt_" + n) for n in (
                "pooled", "pooled_ready", "selector", "selected", "selected_ready", "queries", "pooled_w"))
            qe = sem("rt_queries_taken")
            block = ctx.enter_context(nc.Block())
            by_tile = lambda ap: ap.rearrange("(t p) -> p t", p=NT)

            @block.sync
            def _(sp):
                sp.dma_start(wr[:, :], spread(a["L0_ffn_Wr"], NT)).then_inc(ld, 16)
                sp.dma_start(br[:, :], spread(a["L0_ffn_br"], NT)).then_inc(ld, 16)
                sp.dma_start(bq[:, :], a["L0_ffn_bq"].rearrange("(k p) -> p k", p=128)).then_inc(ld, 16)
                sp.dma_start(wm[:, :, :], chunked(a["L0_ffn_Wm"])).then_inc(ldw, 16)
                sp.dma_start(wq[:, :, :], chunked(a["L0_ffn_Wq"])).then_inc(ldw, 16)
                sp.wait_ge(sc, 1)
                sp.dma_start(by_tile(scr["score"]), score[:, :]).then_inc(sd, 16)
                sp.wait_ge(sd, 16)
                sp.dma_start(srow[:, :], spread(scr["score"], NT)).then_inc(sd, 16)
                sp.wait_ge(rk, 1)
                sp.dma_start(by_tile(scr["rank"]), rank[:, :]).then_inc(rd, 16)
                sp.wait_ge(rd, 16)
                sp.dma_start(rrow[:, :], spread(scr["rank"], TH)).then_inc(rd, 16)

            @block.gpsimd
            def _(pool):
                imprecise = dict(allow_small_or_imprecise_dtypes=True)
                pool.iota(iota[:, :], pattern=[[1, N]], base=0, channel_multiplier=0, **imprecise).then_inc(co, 1)
                pool.iota(idx[:, :], pattern=[[NT, T]], base=0, channel_multiplier=1, **imprecise).then_inc(co, 1)
                pool.iota(iotaj[:, :], pattern=[[TH, 2]], base=0, channel_multiplier=1, **imprecise).then_inc(co, 1)

            @block.scalar
            def _(act):
                act.wait_ge(zs, 1)
                nc.scalar.activation(e[:, :], z[:, :], ACT.Exp, scale=-1.0).then_inc(ex, 1)

            @block.tensor
            def _(pe):
                pe.wait_ge(sc, 1)
                for k in range(KC):
                    for t in range(T):
                        nc.tensor.matmul(psum[:, 0, k:k + 1], nrm[:, t, k * 128:(k + 1) * 128], score[:, t:t + 1],
                                         start=(t == 0), stop=(t == T - 1))
                for t in range(T):
                    last = nc.tensor.matmul(psum[:, 0, KC:KC + 1], ones[0:NT, :], score[:, t:t + 1], start=(t == 0), stop=(t == T - 1))
                last.then_inc(po, 1)
                pe.wait_ge(pd, 1)
                pe.wait_ge(ldw, 32)
                for k in range(KC):
                    for h in range(2):
                        last = nc.tensor.matmul(psum[0:NT, 2 + h, 0:HALF], ptb[:, k, :], wm[:, k, h * HALF:(h + 1) * HALF],
                                                start=(k == 0), stop=(k == KC - 1))
                last.then_inc(pw, 1)
                pe.wait_ge(sl, T)
                for k in range(KC):
                    if k >= 2:
                        pe.wait_ge(nd, k - 1)
                    for t in range(T):
                        last = nc.tensor.matmul(psum[:, 4 + k % 2, 0:TOP], nrm[:, t, k * 128:(k + 1) * 128], sel[:, t, :],
                                                start=(t == 0), stop=(t == T - 1))
                    last.then_inc(ns, 1)
                pe.wait_ge(nd, KC)
                for o in range(KC):
                    if o >= 2:
                        pe.wait_ge(qe, o - 1)
                    for k in range(KC):
                        last = nc.tensor.matmul(psum[:, 6 + o % 2, 0:TOP], wq[:, k, o * 128:(o + 1) * 128], nselt[:, k, :],
                                                start=(k == 0), stop=(k == KC - 1))
                    last.then_inc(qd, 1)

            @block.vector
            def _(dve):
                link = Chain(dve, ch)
                dve.wait_ge(ld, 48)
                dve.wait_ge(co, 3)
                for t in range(T):
                    link(nc.vector.scalar_tensor_tensor(junk[:, 0:D], nrm[:, t, :], 1.0, wr[:, :], ALU.mult, ALU.mult, accum_out=z[:, t:t + 1]))
                nc.vector.tensor_scalar(z[:, :], z[:, :], br[:, :], None, ALU.add).then_inc(zs, 1)
                dve.wait_ge(ex, 1)
                link(nc.vector.tensor_scalar(e[:, :], e[:, :], 1.0, None, ALU.add))
                nc.vector.reciprocal(score[:, :], e[:, :]).then_inc(sc, 1)
                dve.wait_ge(po, 1)
                link(nc.vector.tensor_scalar(total[:, :], psum[:, 0, KC:KC + 1], 1e-6, None, ALU.add))
                link(nc.vector.reciprocal(total[:, :], total[:, :]))
                link(nc.vector.tensor_scalar(pt[:, :], psum[:, 0, 0:KC], total[:, :], None, ALU.mult))
                nc.vector.tensor_copy(ptb[:, :, :], pt[:, :].unsqueeze(2).broadcast_to([128, KC, NT])).then_inc(pd, 1)
                dve.wait_ge(sd, 32)
                for t in range(T):
                    link(nc.vector.tensor_scalar(junk[:, :], srow[:, :], score[:, t:t + 1], None, ALU.is_lt, ALU.add, accum_out=rank[:, t:t + 1]))
                    link(nc.vector.tensor_scalar(junk2[:, :], iota[:, :], idx[:, t:t + 1], None, ALU.is_lt))
                    link(nc.vector.scalar_tensor_tensor(junk[:, :], srow[:, :], score[:, t:t + 1], junk2[:, :], ALU.is_equal, ALU.mult, accum_out=ties[:, t:t + 1]))
                nc.vector.tensor_tensor(rank[:, :], rank[:, :], ties[:, :], ALU.add).then_inc(rk, 1)
                dve.wait_ge(rk, 1)
                link(nc.vector.tensor_scalar(unrouted[:, :], rank[:, :], float(TOP), None, ALU.is_ge))
                for t in range(T):
                    nc.vector.tensor_scalar(sel[:, t, :], iota[:, 0:TOP], rank[:, t:t + 1], None, ALU.is_equal).then_inc(sl, 1)
                dve.wait_ge(pw, 1)
                link(nc.vector.tensor_copy(halves(pooled_w[:, :]), wide(1)))
                for k in range(KC):
                    dve.wait_ge(ns, k + 1)
                    nc.vector.tensor_copy(nselt[:, k, :], psum[:, 4 + k % 2, 0:TOP]).then_inc(nd, 1)
                dve.wait_ge(rd, 32)
                for i in range(2):
                    link(nc.vector.tensor_scalar(selt[:, i, :], rrow[:, :], iotaj[:, i:i + 1], None, ALU.is_equal))
                for o in range(KC):
                    dve.wait_ge(qd, o + 1)
                    nc.vector.tensor_scalar(qt[:, o, :], psum[:, 6 + o % 2, 0:TOP], bq[:, o:o + 1], None, ALU.add).then_inc(qe, 1)

    route_block()

    def cols_block(tag, ah, al, weight, oc, bias_dram, sink, kc=KC):
        with ExitStack() as ctx:
            sb = allocate(ctx)
            raw = sb(tag + "raw", [128, kc, oc * 128])
            wh, wl = sb(tag + "wh", [128, kc, oc * 128], F32R), sb(tag + "wl", [128, kc, oc * 128], F32R)
            bias = sb(tag + "bias", [128, oc])
            ld, hi, lo, mm, ev = (sem(tag + n) for n in ("loaded", "high", "low", "product", "taken"))
            block = ctx.enter_context(nc.Block())

            @block.sync
            def _(sp):
                sp.dma_start(raw[:, :, :], chunked(weight)).then_inc(ld, 16)
                sp.dma_start(bias[:, :], bias_dram.rearrange("(k p) -> p k", p=128)).then_inc(ld, 16)

            @block.scalar
            def _(act):
                act.wait_ge(ld, 32)
                nc.scalar.activation(wh[:, :, :], raw[:, :, :], ACT.Copy).then_inc(hi, 1)
                for n in range(oc * 3):
                    o, c = n // 3, n % 3
                    act.wait_ge(mm, n + 1)
                    sink(o, slice(COLS[c][0], COLS[c][0] + COLS[c][1]), psum[:, n % 8, 0:COLS[c][1]], bias[:, o:o + 1]).then_inc(ev, 1)

            @block.vector
            def _(dve):
                dve.wait_ge(hi, 1)
                nc.vector.tensor_tensor(wl[:, :, :], raw[:, :, :], wh[:, :, :].bitcast(F32), ALU.subtract).then_inc(lo, 1)

            @block.tensor
            def _(pe):
                pe.wait_ge(lo, 1)
                for n in range(oc * 3):
                    o, (c0, cn) = n // 3, COLS[n % 3]
                    if n >= 8:
                        pe.wait_ge(ev, n - 7)
                    for k in range(kc):
                        f = slice(o * 128, (o + 1) * 128)
                        last = split_mm(psum[:, n % 8, 0:cn], wh[:, k, f], wl[:, k, f],
                                        ah[:, k, c0:c0 + cn], al[:, k, c0:c0 + cn], k == 0, k == kc - 1)
                    last.then_inc(mm, 1)

    v = acc
    kt = room[1][:, 0:KC * N].rearrange("p (k n) -> p k n", k=KC)
    with ExitStack() as ctx:
        sb = allocate(ctx)
        hh, hl = sb("n_high", [128, KC, N], F32R), sb("n_low", [128, KC, N], F32R)
        transpose_block("tr_n", nrm, hh, hl)
        bias = sb("mv_bias", [NT, D])

        def mix_sink(dve, link, j, t, rows):
            link(nc.vector.tensor_tensor(halves(acc[:, t, :]), rows, halves(bias[:, :]), ALU.add))
            link(nc.vector.scalar_tensor_tensor(acc[:, t, :], pooled_w[:, :], score[:, t:t + 1], acc[:, t, :], ALU.mult, ALU.add))
            return nc.vector.tensor_scalar(acc[:, t, :], acc[:, t, :], unrouted[:, t:t + 1], None, ALU.mult)

        rows_block("wm_", hh, hl, [a["L0_ffn_Wm"]], mix_sink, loads=[(bias[:, :], spread(a["L0_ffn_bm"], NT))],
                   stores=[(scr["mix"][t * NT:(t + 1) * NT, :], acc[:, t, :]) for t in range(T)])
        rows_block("wv_", hh, hl, [a["L0_ffn_Wv"]],
                   lambda dve, link, j, t, rows: nc.vector.tensor_tensor(halves(v[:, t, :]), rows, halves(bias[:, :]), ALU.add),
                   loads=[(bias[:, :], spread(a["L0_ffn_bv"], NT))])
        cols_block("wk_", hh, hl, a["L0_ffn_Wk"], KC, a["L0_ffn_bk"],
                   lambda o, cols, got, b: nc.scalar.activation(kt[:, o, cols], got, ACT.Identity, bias=b))

    ctxs = sbk("ctxs", [TH, 2, D])

    def attention_block():
        with ExitStack() as ctx:
            sb = allocate(ctx)
            p = [sb(f"probs{s}", [TH, N]) for s in range(2)]
            pt = [sb(f"probst{s}", [NT, T, TH]) for s in range(2)]
            mx, nm, sm, rs = (sb("a_" + n, [TH, 2, 2]) for n in ("max", "negmax", "sum", "rsum"))
            qk, mxs, ex, tr, tc, pv, cx, ch = (sem("att_" + n) for n in (
                "scores", "max", "exp", "transposed", "copied", "context", "context_taken", "chain"))
            block = ctx.enter_context(nc.Block())
            U = 2 * H
            units = [(i, h) for i in range(2) for h in range(H)]

            @block.tensor
            def _(pe):
                def scores(u):
                    i, h = units[u]
                    s, rows = u % 2, slice((h % 2) * DH, (h % 2 + 1) * DH)
                    if u >= 2:
                        pe.wait_ge(cx, u - 1)
                        pe.wait_ge(ex, 2 * (u - 1))
                    for c, (c0, cn) in enumerate(COLS):
                        last = nc.tensor.matmul(psum[0:TH, 3 * s + c, 0:cn], qt[rows, h // 2, i * TH:(i + 1) * TH],
                                                kt[rows, h // 2, c0:c0 + cn], start=True, stop=True)
                    last.then_inc(qk, 1)

                scores(0)
                for u in range(U):
                    i, h = units[u]
                    s = u % 2
                    if u + 1 < U:
                        scores(u + 1)
                    pe.wait_ge(ex, 2 * (u + 1))
                    for b in range(2):
                        n = 2 * u + b
                        if n >= 2:
                            pe.wait_ge(tc, n - 1)
                        for j in range(5):
                            k = 5 * b + j
                            last = nc.tensor.transpose(psum[0:NT, 6 + b, j * TH:(j + 1) * TH], p[s][:, k * NT:(k + 1) * NT], ident[0:TH, 0:TH])
                        last.then_inc(tr, 1)
                    pe.wait_ge(tc, 2 * (u + 1))
                    for k in range(T):
                        last = nc.tensor.matmul(psum[0:TH, 3 * s + 2, 440:440 + DH], pt[s][:, k, :], v[:, k, h * DH:(h + 1) * DH],
                                                start=(k == 0), stop=(k == T - 1))
                    last.then_inc(pv, 1)

            @block.scalar
            def _(act):
                for u in range(U):
                    s = u % 2
                    act.wait_ge(mxs, u + 1)
                    if u >= 2:
                        act.wait_ge(tr, 2 * (u - 1))
                    nc.scalar.activation(p[s][:, 0:832].rearrange("p (a n) -> p a n", a=2), psum[0:TH, 3 * s:3 * s + 2, 0:416], ACT.Exp,
                                         bias=nm[:, s, 0:1], scale=0.125, accum_out=sm[:, s, 0:1]).then_inc(ex, 1)
                    nc.scalar.activation(p[s][:, 832:N], psum[0:TH, 3 * s + 2, 0:418], ACT.Exp,
                                         bias=nm[:, s, 0:1], scale=0.125, accum_out=sm[:, s, 1:2]).then_inc(ex, 1)

            @block.vector
            def _(dve):
                link = Chain(dve, ch)

                def maximum(u):
                    s = u % 2
                    dve.wait_ge(qk, u + 1)
                    link(nc.vector.tensor_reduce(mx[:, s, 0:1], psum[0:TH, 3 * s:3 * s + 2, 0:416], AX.XY, ALU.max))
                    link(nc.vector.tensor_reduce(mx[:, s, 1:2], psum[0:TH, 3 * s + 2, 0:418], AX.X, ALU.max))
                    link(nc.vector.tensor_tensor(mx[:, s, 0:1], mx[:, s, 0:1], mx[:, s, 1:2], ALU.max))
                    nc.vector.tensor_scalar(nm[:, s, 0:1], mx[:, s, 0:1], -0.125, None, ALU.mult).then_inc(mxs, 1)

                maximum(0)
                for u in range(U):
                    i, h = units[u]
                    s = u % 2
                    dve.wait_ge(ex, 2 * (u + 1))
                    link(nc.vector.tensor_tensor(rs[:, s, 0:1], sm[:, s, 0:1], sm[:, s, 1:2], ALU.add))
                    link(nc.vector.reciprocal(rs[:, s, 0:1], rs[:, s, 0:1]))
                    if u + 1 < U:
                        maximum(u + 1)
                    for b in range(2):
                        dve.wait_ge(tr, 2 * u + b + 1)
                        nc.vector.tensor_copy(pt[s][:, 5 * b:5 * b + 5, :],
                                              psum[0:NT, 6 + b, 0:5 * TH].rearrange("p (k n) -> p k n", k=5)).then_inc(tc, 1)
                    dve.wait_ge(pv, u + 1)
                    nc.vector.tensor_scalar(ctxs[:, i, h * DH:(h + 1) * DH], psum[0:TH, 3 * s + 2, 440:440 + DH], rs[:, s, 0:1],
                                            None, ALU.mult).then_inc(cx, 1)

    attention_block()

    hf, mixed = gn, acc

    def merge_block():
        with ExitStack() as ctx:
            sb = allocate(ctx)
            wo, bo = sb("wo", [128, KC, D]), sb("bo", [TH, D])
            ctxt, ao = sb("ctxt", [128, KC, TOP]), sb("ao", [TH, 2, D])
            ld, ldh, tr, tc, om, oe, mm, ev, ch, st = (sem("mg_" + n) for n in (
                "loaded", "rows_loaded", "transposed", "copied", "out_product", "out_taken", "merged", "taken", "chain", "stored"))
            block = ctx.enter_context(nc.Block())

            @block.sync
            def _(sp):
                sp.dma_start(wo[:, :, :], chunked(a["L0_ffn_Wo"])).then_inc(ld, 16)
                sp.dma_start(bo[:, :], spread(a["L0_ffn_bo"], TH)).then_inc(ld, 16)
                sp.dma_start(hf, tiled(scr["hidden"])).then_inc(ldh, 16)
                sp.dma_start(mixed, tiled(scr["mix"])).then_inc(ldh, 16)

            @block.tensor
            def _(pe):
                for i in range(2):
                    for k in range(KC):
                        last = nc.tensor.transpose(psum[:, 4 + k // 2, (k % 2) * TOP + i * TH:(k % 2) * TOP + (i + 1) * TH],
                                                   ctxs[:, i, k * 128:(k + 1) * 128], ident[0:TH, 0:TH])
                last.then_inc(tr, 1)
                pe.wait_ge(tc, 1)
                pe.wait_ge(ld, 32)
                for i in range(2):
                    for h in range(2):
                        for k in range(KC):
                            last = nc.tensor.matmul(psum[0:TH, 2 * i + h, 0:HALF], ctxt[:, k, i * TH:(i + 1) * TH],
                                                    wo[:, k, h * HALF:(h + 1) * HALF], start=(k == 0), stop=(k == KC - 1))
                last.then_inc(om, 1)
                pe.wait_ge(oe, 2)
                for t in range(T):
                    if t >= 4:
                        pe.wait_ge(ev, t - 3)
                    for h in range(2):
                        for i in range(2):
                            last = nc.tensor.matmul(psum[0:NT, 2 * (t % 4) + h, 0:HALF], selt[:, i, t * NT:(t + 1) * NT],
                                                    ao[:, i, h * HALF:(h + 1) * HALF], start=(i == 0), stop=(i == 1))
                    last.then_inc(mm, 1)

            @block.vector
            def _(dve):
                link = Chain(dve, ch)
                dve.wait_ge(tr, 1)
                nc.vector.tensor_copy(ctxt[:, :, :].rearrange("p (a b) n -> p a (b n)", a=3), psum[:, 4:7, 0:2 * TOP]).then_inc(tc, 1)
                dve.wait_ge(om, 1)
                dve.wait_ge(ld, 32)
                for i in range(2):
                    nc.vector.tensor_tensor(halves(ao[:, i, :]), wide(i, rows=TH), halves(bo[:, :]), ALU.add).then_inc(oe, 1)
                dve.wait_ge(ldh, 32)
                for t in range(T):
                    link(nc.vector.tensor_tensor(hf[:, t, :], hf[:, t, :], mixed[:, t, :], ALU.add))
                    dve.wait_ge(mm, t + 1)
                    nc.vector.tensor_tensor(halves(hf[:, t, :]), halves(hf[:, t, :]), wide(t % 4), ALU.add).then_inc(ev, 1)

    merge_block()
    keep.close()
    affine_norm("ln_2", hf, a["L0_ffn_g2"], a["L0_ffn_b2"], scr["hf"])

    with ExitStack() as ctx:
        sb = allocate(ctx)
        fh, fl2 = sb("f_high", [128, FK, N], F32R), sb("f_low", [128, FK, N], F32R)
        with ExitStack() as c2:
            sb2 = allocate(c2)
            hh, hl = sb2("n2_high", [128, KC, N], F32R), sb2("n2_low", [128, KC, N], F32R)
            transpose_block("tr_n2", hf, hh, hl)
            f = room[0][:, 0:FK * N].rearrange("p (k n) -> p k n", k=FK)
            cols_block("w1_", hh, hl, a["L0_ffn_W1"], FK, a["L0_ffn_bf1"],
                       lambda o, cols, got, b: nc.scalar.activation(f[:, o, cols], got, ACT.Gelu, bias=b))
        with ExitStack() as c2:
            hi = sem("f_hi")
            block = c2.enter_context(nc.Block())

            @block.scalar
            def _(act):
                for k in range(FK):
                    nc.scalar.activation(fh[:, k, :], f[:, k, :], ACT.Copy).then_inc(hi, 1)

            @block.vector
            def _(dve):
                for k in range(FK):
                    dve.wait_ge(hi, k + 1)
                    nc.vector.tensor_tensor(fl2[:, k, :], f[:, k, :], fh[:, k, :].bitcast(F32), ALU.subtract)

        bias = sb("f2_bias", [NT, D])
        x1 = sb("x1", [NT, T, D])

        def last_sink(dve, link, j, t, rows):
            link(nc.vector.tensor_tensor(halves(hf[:, t, :]), halves(hf[:, t, :]), rows, ALU.add))
            link(nc.vector.tensor_tensor(hf[:, t, :], hf[:, t, :], bias[:, :], ALU.add))
            return nc.vector.tensor_tensor(hf[:, t, :], hf[:, t, :], x1[:, t, :], ALU.add)

        rows_block("w2_", fh, fl2, [a["L0_ffn_W2"]], last_sink, kc=FK,
                   loads=[(bias[:, :], spread(a["L0_ffn_bf2"], NT)), (hf, tiled(scr["hf"])), (x1[:, :, :], tiled(scr["x1"]))],
                   stores=[(out[t * NT:(t + 1) * NT, :], hf[:, t, :]) for t in range(T)])


def kernel(**inputs):
    import numpy as np
    import concourse.bacc as bacc
    from concourse import mybir
    from concourse.bass_utils import run_bass_kernel_spmd as run

    nc = bacc.Bacc("TRN2", target_bir_lowering=False, num_devices=1)
    arrays, a = {}, {}
    for name, value in inputs.items():
        v = np.ascontiguousarray(value)
        v = v.reshape(v.shape or (1,))
        arrays["in_" + name] = v
        a[name] = nc.dram_tensor("in_" + name, v.shape, mybir.dt.from_np(v.dtype), kind="ExternalInput").ap()
    out = nc.dram_tensor("out", (N, D), F32, kind="ExternalOutput").ap()
    KIND = "Internal"
    scr = {name: nc.dram_tensor("scratch_" + name, shape, F32, kind=KIND).ap() for name, shape in SCRATCH.items()}
    build(nc, a, out, scr)
    r = run(nc, [arrays], core_ids=[0])
    if KIND != "Internal":
        for name in SCRATCH:
            np.save("/tmp/dbg_" + name + ".npy", r.results[0]["scratch_" + name])
    return r.results[0]["out"]
```

```python
from contextlib import ExitStack
import math

import concourse.bass as bass
from concourse import mybir

ALU = mybir.AluOpType
ACT = mybir.ActivationFunctionType
AX = mybir.AxisListType
F32 = mybir.dt.float32
F32R = mybir.dt.float32r
F16 = mybir.dt.float16
I32 = mybir.dt.int32
U32 = mybir.dt.uint32
U16 = mybir.dt.uint16

N, D = 1250, 768
NT, T = 125, 10
KC = D // 128
HALF = D // 2
E = 41250
EC = E // NT
R = 34
NREL = R + 2
EB = 128
G = 2
SBE = EB * G
NSB = 2 * math.ceil((E // SBE + T) / 2)
NSB = 4 * math.ceil(NSB / 4)
NB = NSB * G
PAIRS, PT = NREL // 2, 2 * T
COUNT_PAIRS = math.ceil(NSB / PT)
NSBP = COUNT_PAIRS * PT + 1
NBP = NSBP * G
COUNT_FROM = PAIRS - 1 - COUNT_PAIRS
assert NSBP >= NSB + 3
H, DH = 12, 64
TOP = int(round(0.15 * N))
TH = TOP // 2
FF = 384
FK = FF // 128
EPS = 1e-5
MAGIC = 12582912.0
COLS = [(0, 416), (416, 416), (832, 418)]


SCRATCH = {
    "y": (NREL * N, D),
    "table": (EB * NBP, 4),
    "x1": (N, D),
    "hidden": (N, D),
    "mix": (N, D),
    "score": (N,),
    "rank": (N,),
}


class Chain:

    def __init__(self, eng, sem):
        self.eng, self.sem, self.n, self.i, self.per = eng, sem, 0, None, 0

    def __call__(self, ins):
        self.n += 1
        ins.then_inc(self.sem, 1)
        self.wait()

    def wait(self):
        self.eng.wait_ge(self.sem, self.n if self.i is None else self.i * self.per + self.n)

    def enter(self, i, per):
        self.i, self.per, self.start = i, per, self.n

    def leave(self, times):
        assert self.n - self.start == self.per, (self.n - self.start, self.per)
        self.n = self.start + self.per * times
        self.i = None


def build(nc, a, out, scr):
    stack = ExitStack()
    with stack, nc.allow_non_contiguous_dma(reason="bias columns and 1250 scores, a few KB"):
        _build(nc, a, out, scr, stack)


def _build(nc, a, out, scr, top):
    def allocate(ctx, **where):
        def sb(name, shape, dt=F32):
            return ctx.enter_context(nc.sbuf_tensor(name, shape, dt, **where))
        return sb

    live = []

    def sem(name):
        live.append(nc.alloc_semaphore(name=name))
        return live[-1]

    def recycle():
        nc.clear_and_free_semaphores(live)
        live.clear()
        nc.all_engine_barrier()

    def sems(name, n):
        return [sem(f"{name}{i}") for i in range(n)]

    psum = top.enter_context(nc.psum_tensor("psum", [128, 8, 512], F32))

    def wide(slot, rows=NT, w=HALF):
        return psum[0:rows, 2 * slot:2 * slot + 2, 0:w]

    def halves(ap):
        return ap.rearrange("p (h n) -> p h n", h=2)

    tiled = lambda ap: ap.rearrange("(t p) d -> p t d", p=NT)
    chunked = lambda ap: ap.rearrange("(k p) n -> p k n", p=128)
    spread = lambda ap, rows: ap.partition_broadcast(rows)

    sb0 = allocate(top)
    ident = sb0("ident", [128, 128])
    identh = sb0("identh", [128, 128], F16)
    ones = sb0("ones", [128, 128])
    iota16 = sb0("iota16", [128, N], F16)
    dinv = sb0("dinv", [NT, T])
    prefix = sb0("prefix", [NT, NT])

    def stats(link, src, tmp, mv, t):
        for h in range(2):
            ins = nc.vector.bn_stats(tmp[:, t, h * 6:h * 6 + 6], src[:, t, h * HALF:(h + 1) * HALF])
            link(ins)
        return nc.vector.bn_aggr(mv[:, t, :], tmp[:, t, :])

    def split_mm(outs, lh, ll, rights, start, stop):
        last = None
        for o, (rh, rl) in zip(outs, rights):
            nc.tensor.matmul(o, lh, rh, start=start, stop=False)
            nc.tensor.matmul(o, lh, rl, start=False, stop=False)
        for o, (rh, _) in zip(outs, rights):
            last = nc.tensor.matmul(o, ll, rh, start=False, stop=stop)
        return last

    def rows_mm(slot, ah, al, wh, wl, cols, kc=KC, before=None):
        last = None
        outs = [psum[0:cols.stop - cols.start, 2 * slot + h, 0:HALF] for h in range(2)]
        for k in range(kc):
            if before:
                before(k)
            last = split_mm(outs, ah[:, k, cols], al[:, k, cols],
                            [(wh[:, k, h * HALF:(h + 1) * HALF], wl[:, k, h * HALF:(h + 1) * HALF]) for h in range(2)],
                            k == 0, k == kc - 1)
        return last

    def polish(link, r, v, tmp):
        link(nc.vector.tensor_tensor(tmp, r, r, ALU.mult))
        link(nc.vector.tensor_tensor(tmp, tmp, v, ALU.mult))
        link(nc.vector.tensor_scalar(tmp, tmp, -0.5, 1.5, ALU.mult, ALU.add))
        link(nc.vector.tensor_tensor(r, r, tmp, ALU.mult))

    def norm_block(tag, xs, then, loads=(), taken=None, ready=None):
        with ExitStack() as ctx:
            sb = allocate(ctx)
            if ready is None:
                tmp, mv = sb(tag + "tmp", [NT, T, 12]), sb(tag + "mv", [NT, T, 2])
            else:
                mv = ready
            std, rstd = sb(tag + "std", [NT, T]), sb(tag + "rstd", [NT, T])
            var = sb(tag + "var", [NT, T])
            st, sq, ch = (sem(tag + n) for n in ("stats", "sqrt", "chain"))
            block = ctx.enter_context(nc.Block())

            @block.sync
            def _(sp):
                for to, src in loads:
                    sp.dma_start(to, src).then_inc(taken, 16)

            @block.scalar
            def _(act):
                act.wait_ge(st, 1)
                nc.scalar.activation(std[:, :], var[:, :], ACT.Sqrt).then_inc(sq, 1)

            @block.vector
            def _(dve):
                link = Chain(dve, ch)
                for t in range(T if ready is None else 0):
                    link(stats(link, xs, tmp, mv, t))
                nc.vector.tensor_scalar(var[:, :], mv[:, :, 1], EPS, None, ALU.add).then_inc(st, 1)
                dve.wait_ge(sq, 1)
                link(nc.vector.reciprocal(rstd[:, :], std[:, :]))
                polish(link, rstd[:, :], var[:, :], std[:, :])
                for t in range(T):
                    then(dve, link, t, mv[:, t, 0:1], rstd[:, t:t + 1])

    def transpose_block(tag, xs, ah, al):
        with ExitStack() as ctx:
            tr, hi, lo = (sem(tag + n) for n in ("transposed", "high", "low"))
            block = ctx.enter_context(nc.Block())

            def part(m, t):
                return m[:, :, t * NT:(t + 1) * NT].rearrange("p (h k) n -> p h k n", h=2)

            def src(t):
                return psum[:, 2 * (t % 4):2 * (t % 4) + 2, 0:3 * NT].rearrange("p h (k n) -> p h k n", k=3)

            @block.tensor
            def _(pe):
                for t in range(T):
                    if t >= 4:
                        pe.wait_ge(lo, 2 * (t - 3))
                    for k in range(KC):
                        o = psum[:, 2 * (t % 4) + k // 3, (k % 3) * NT:(k % 3 + 1) * NT]
                        last = nc.tensor.transpose(o, xs[:, t, k * 128:(k + 1) * 128], ident[0:NT, 0:NT])
                    last.then_inc(tr, 1)

            @block.scalar
            def _(act):
                for t in range(T):
                    act.wait_ge(tr, t + 1)
                    for h in range(2):
                        nc.scalar.activation(part(ah, t)[:, h], src(t)[:, h], ACT.Copy).then_inc(hi, 1)

            @block.vector
            def _(dve):
                for t in range(T):
                    dve.wait_ge(hi, 2 * t + 2)
                    for h in range(2):
                        nc.vector.tensor_tensor(part(al, t)[:, h], src(t)[:, h], part(ah, t)[:, h].bitcast(F32),
                                                ALU.subtract).then_inc(lo, 1)

    def rows_block(tag, xs, ah, al, weight, sink, kc=KC, loads=(), tile_load=None, store=None, prepare=None):
        with ExitStack() as ctx:
            sb = allocate(ctx)
            raw = [sb(f"{tag}raw{s}", [128, D]) for s in range(3)]
            wh, wl = sb(tag + "wh", [128, kc, D], F32R), sb(tag + "wl", [128, kc, D], F32R)
            wld, tld = sems(tag + "weights_loaded", 3), sems(tag + "tile_loaded", 3)
            bl, whi, wlo, mm, ev, ch, st = (sem(tag + n) for n in (
                "bias_loaded", "weights_high", "weights_low", "product", "taken", "chain", "stored"))
            rdy, tr, hi, lo = (sem(tag + n) for n in ("prepared", "transposed", "high", "low"))
            block = ctx.enter_context(nc.Block())
            slots = 4 if xs is None else 2

            def part(m, t):
                return m[:, :, t * NT:(t + 1) * NT].rearrange("p (h k) n -> p h k n", h=2)

            def turned(t):
                s = 2 + t % 2
                return psum[:, 2 * s:2 * s + 2, 0:3 * NT].rearrange("p h (k n) -> p h k n", k=3)

            @block.sync
            def _(sp):
                for k in range(kc):
                    if k >= 3:
                        sp.wait_ge(wlo, k - 2)
                    sp.dma_start(raw[k % 3][:, :], chunked(weight)[:, k, :]).then_inc(wld[k % 3], 16)
                    if k == 0:
                        for to, src in loads:
                            sp.dma_start(to, src).then_inc(bl, 16)
                for t in range(T + 3):
                    if t >= 3:
                        sp.wait_ge(ev, t - 2)
                    if t < T and tile_load:
                        if xs is not None:
                            sp.wait_ge(tr, t + 1)
                        to, src = tile_load(t)
                        sp.dma_start(to, src).then_inc(tld[t % 3], 16)
                    if t >= 3 and store:
                        to, src = store(t - 3)
                        sp.dma_start(to, src).then_inc(st, 16)
                if store:
                    sp.wait_ge(st, 16 * T)

            @block.tensor
            def _(pe):
                def transposes(t):
                    if prepare:
                        pe.wait_ge(rdy, t + 1)
                    if t >= 2:
                        pe.wait_ge(lo, t - 1)
                    for k in range(KC):
                        o = psum[:, 2 * (2 + t % 2) + k // 3, (k % 3) * NT:(k % 3 + 1) * NT]
                        last = nc.tensor.transpose(o, xs[:, t, k * 128:(k + 1) * 128], ident[0:NT, 0:NT])
                    last.then_inc(tr, 1)

                if xs is not None:
                    transposes(0)
                    transposes(1)
                for t in range(T):
                    if xs is not None:
                        pe.wait_ge(lo, t + 1)
                    if t >= slots:
                        pe.wait_ge(ev, t - slots + 1)
                    rows_mm(t % slots, ah, al, wh, wl, slice(t * NT, (t + 1) * NT), kc,
                            before=(lambda k: pe.wait_ge(wlo, k + 1)) if t == 0 else None).then_inc(mm, 1)
                    if xs is not None and t + 2 < T:
                        transposes(t + 2)

            @block.scalar
            def _(act):
                def high(t):
                    act.wait_ge(tr, t + 1)
                    nc.scalar.activation(part(ah, t), turned(t), ACT.Copy).then_inc(hi, 1)

                def weights_high(k):
                    act.wait_ge(wld[k % 3], 16 * (k // 3 + 1))
                    nc.scalar.activation(wh[:, k, :], raw[k % 3][:, :], ACT.Copy).then_inc(whi, 1)

                if xs is not None:
                    high(0)
                    high(1)
                for k in range(kc):
                    weights_high(k)
                if xs is not None:
                    for t in range(2, T):
                        high(t)

            @block.vector
            def _(dve):
                link = Chain(dve, ch)

                def low(t):
                    dve.wait_ge(hi, t + 1)
                    nc.vector.tensor_tensor(part(al, t), turned(t), part(ah, t).bitcast(F32), ALU.subtract).then_inc(lo, 1)

                for t in range(3 if prepare else 0):
                    prepare(link, t).then_inc(rdy, 1)
                if xs is not None:
                    low(0)
                    low(1)
                for k in range(kc):
                    dve.wait_ge(whi, k + 1)
                    nc.vector.tensor_tensor(wl[:, k, :], raw[k % 3][:, :], wh[:, k, :].bitcast(F32), ALU.subtract).then_inc(wlo, 1)
                if loads:
                    dve.wait_ge(bl, 16 * len(loads))
                for t in range(T):
                    if prepare and t + 3 < T:
                        prepare(link, t + 3).then_inc(rdy, 1)
                    if xs is not None and t + 2 < T:
                        low(t + 2)
                    if tile_load:
                        dve.wait_ge(tld[t % 3], 16 * (t // 3 + 1))
                    dve.wait_ge(mm, t + 1)
                    sink(dve, link, t, wide(t % slots)).then_inc(ev, 1)

    tab, tab_rows = scr["table"], scr["table"].rearrange("(q b) f -> q b f", q=EB)
    y = scr["y"]
    yv = y.rearrange("(i p) d -> i p d", p=NT)

    graph = ExitStack()
    sbg = allocate(graph)
    tile_of = sbg("tile_of", [1, NSBP], I32)
    records = sbg("records", [EB, max(EC * 5, NBP * 4)])
    rec = records[0:NT, 0:EC * 5].rearrange("p (c f) -> p c f", f=5)
    table = records[:, 0:NBP * 4].rearrange("p (b f) -> p b f", f=4)
    count = sbg("count", [NT, T, N + R], U16)
    inv_count = sbg("inv_count", [NT, T, R])
    xform = ExitStack()
    sbx = allocate(xform)
    rel_weights = a["L0_gnn_W_rel"].rearrange("r (k p) n -> r p k n", p=128)
    raw = sbx("r_raw", [128, KC, D])
    wh, wl = [sbx("r_wh0", [128, KC, D], F32R)], [sbx("r_wl0", [128, KC, D], F32R)]
    x_stack = ExitStack()
    xs = allocate(x_stack, side="right")("xs", [NT, T, D])
    x_mv = allocate(x_stack, side="right")("x_mean_var", [NT, T, 2])

    def order_block():
        with ExitStack() as ctx:
            sb = allocate(ctx)
            given = sb("given_edges", [NT, 3, EC], I32)
            edge = sb("edge", [NT, 3, EC])
            tid, pos, tmp = sb("tid", [NT, EC]), sb("pos", [NT, EC]), sb("tmp", [NT, EC])
            hot, inc = sb("hot", [NT, T, EC]), sb("inc", [NT, T, EC])
            one = sb("one_row", [NT, EC])
            total, both, nb, cum = sb("total", [NT, T]), sb("both", [NT, 2, T]), sb("nb", [NT, T]), sb("cum", [NT, T])
            off, first = sb("off", [NT, T]), sb("first", [NT, T])
            sbi, sbt = sb("sbi", [1, NSBP]), sb("sbt", [1, NSBP])
            fill = sb("fill", [128, NBP, 4])
            junk, negmean, sums = sb("x_junk", [NT, D]), sb("x_negmean", [NT, T]), sb("x_sums", [NT, 2, T])
            x_loaded, xw = sems("x_loaded", T // 2), sem("x_row_sums")
            ld, ch, co, tt, px, fl, pr = (sem("ord_" + n) for n in ("loaded", "chain", "const", "total", "prefix", "fill", "prepared"))
            w0, w0h = sem("first_weight_loaded"), sem("first_weight_high")
            block = ctx.enter_context(nc.Block())

            @block.sync
            def _(sp):
                for f, name in enumerate(("dst", "src", "edge_type_34")):
                    sp.dma_start(given[:, f, :], a[name].rearrange("(p c) -> p c", p=NT)).then_inc(ld, 16)
                for i in range(T // 2):
                    sp.dma_start(xs[:, 2 * i:2 * i + 2, :], tiled(a["x"])[:, 2 * i:2 * i + 2, :]).then_inc(x_loaded[i], 16)
                sp.dma_start(raw[:, :, :], rel_weights[0]).then_inc(w0, 16)
                sp.wait_ge(pr, 1)
                sp.dma_start(tab_rows, fill[:, :, :]).then_inc(fl, 16)
                sp.wait_ge(fl, 16)

            @block.gpsimd
            def _(pool):
                imprecise = dict(allow_small_or_imprecise_dtypes=True)
                pool.iota(sbi[:, :], pattern=[[1, NSBP]], base=0, channel_multiplier=0, **imprecise).then_inc(co, 1)
                nc.gpsimd.memset(ones[:, :], 1.0).then_inc(co, 1)
                nc.gpsimd.memset(ident[:, :], 0.0).then_inc(co, 1)
                nc.gpsimd.memset(identh[:, :], 0.0).then_inc(co, 1)
                pool.wait_ge(co, 4)
                nc.gpsimd.affine_select(out=prefix[:, :], in_=ones[0:NT, 0:NT], compare_op=ALU.is_gt, fill=0.0,
                                        base=0, pattern=[[1, NT]], channel_multiplier=-1).then_inc(co, 1)
                for m in (ident, identh):
                    nc.gpsimd.affine_select(out=m[:, :], in_=m[:, :], compare_op=ALU.not_equal, fill=1.0, base=0,
                                            pattern=[[-1, 128]], channel_multiplier=1).then_inc(co, 1)
                pool.iota(iota16[:, :], pattern=[[1, N]], base=0, channel_multiplier=0, **imprecise).then_inc(co, 1)

            @block.scalar
            def _(act):
                for t in range(T):
                    if t % 2 == 0:
                        act.wait_ge(x_loaded[t // 2], 16)
                    if t:
                        act.wait_ge(xw, t)
                    nc.scalar.activation(junk[:, :], xs[:, t, :], ACT.Identity, accum_out=sums[:, 0, t:t + 1]).then_inc(xw, 1)
                act.wait_ge(xw, T)
                nc.scalar.activation(negmean[:, :], sums[:, 0, :], ACT.Copy, scale=-1.0 / D).then_inc(xw, 1)
                for t in range(T):
                    act.wait_ge(xw, T + 1 + t)
                    nc.scalar.activation(junk[:, :], xs[:, t, :], ACT.Square, bias=negmean[:, t:t + 1],
                                         accum_out=sums[:, 1, t:t + 1]).then_inc(xw, 1)
                act.wait_ge(w0, 16)
                nc.scalar.activation(wh[0][:, :, :], raw[:, :, :], ACT.Copy).then_inc(w0h, 1)

            @block.tensor
            def _(pe):
                pe.wait_ge(co, 5)
                pe.wait_ge(tt, 1)
                nc.tensor.matmul(psum[0:NT, 0, 0:T], prefix[:, :], total[:, :], start=True, stop=True)
                nc.tensor.matmul(psum[0:NT, 1, 0:T], ones[0:NT, 0:NT], total[:, :], start=True, stop=True).then_inc(px, 1)

            @block.vector
            def _(dve):
                link = Chain(dve, ch)
                link(nc.vector.memset(fill[:, :, :].bitcast(I32), 0))
                link(nc.vector.memset(fill[:, :, 2:3], -1.0))
                nc.vector.memset(one[:, :], 1.0).then_inc(pr, 1)
                dve.wait_ge(pr, 1)
                dve.wait_ge(ld, 48)
                dve.wait_ge(co, 1)
                link(nc.vector.tensor_copy(edge[:, :, :], given[:, :, :]))
                dst, src, typ = edge[:, 0, :], edge[:, 1, :], edge[:, 2, :]
                link(nc.vector.tensor_scalar(tid[:, :], dst, float(NT), None, ALU.is_ge))
                for k in range(2, T):
                    link(nc.vector.scalar_tensor_tensor(tid[:, :], dst, float(NT * k), tid[:, :], ALU.is_ge, ALU.add))
                for k in range(T):
                    link(nc.vector.tensor_scalar(hot[:, k, :], tid[:, :], float(k), None, ALU.is_equal))
                    link(nc.vector.tensor_tensor_scan(inc[:, k, :], one[:, :], hot[:, k, :], 0.0, ALU.mult, ALU.add))
                nc.vector.tensor_copy(total[:, :], inc[:, :, EC - 1]).then_inc(tt, 1)
                link(nc.vector.scalar_tensor_tensor(rec[:, :, 0].bitcast(U32), typ, float(N), src, ALU.mult, ALU.add))
                link(nc.vector.tensor_copy(rec[:, :, 1], src))
                link(nc.vector.scalar_tensor_tensor(rec[:, :, 2], tid[:, :], -float(NT), dst, ALU.mult, ALU.add))
                link(nc.vector.tensor_copy(rec[:, :, 3], typ))
                dve.wait_ge(px, 1)
                link(nc.vector.tensor_copy(both[:, 0, :], psum[0:NT, 0, 0:T]))
                link(nc.vector.tensor_copy(both[:, 1, :], psum[0:NT, 1, 0:T]))
                link(nc.vector.tensor_scalar(nb[:, :], both[:, 1, :], 1.0 / SBE, (SBE - 1.0) / SBE - 0.5 + 0.5 / SBE,
                                             ALU.mult, ALU.add))
                link(nc.vector.tensor_scalar(nb[:, :], nb[:, :], MAGIC, None, ALU.add))
                link(nc.vector.tensor_scalar(nb[:, :], nb[:, :], MAGIC, None, ALU.subtract))
                link(nc.vector.tensor_tensor_scan(cum[:, :], one[:, 0:T], nb[:, :], 0.0, ALU.mult, ALU.add))
                link(nc.vector.tensor_tensor(first[:, :], cum[:, :], nb[:, :], ALU.subtract))
                link(nc.vector.tensor_scalar(off[:, :], first[:, :], float(SBE), -1.0, ALU.mult, ALU.add))
                link(nc.vector.tensor_tensor(off[:, :], off[:, :], both[:, 0, :], ALU.add))
                for k in range(T):
                    dest = pos if k == 0 else tmp
                    link(nc.vector.scalar_tensor_tensor(dest[:, :], inc[:, k, :], off[:, k:k + 1], hot[:, k, :], ALU.add, ALU.mult))
                    if k:
                        link(nc.vector.tensor_tensor(pos[:, :], pos[:, :], tmp[:, :], ALU.add))
                link(nc.vector.tensor_scalar(tmp[:, :], pos[:, :], 1.0 / EB, -0.5 + 0.5 / EB, ALU.mult, ALU.add))
                link(nc.vector.tensor_scalar(tmp[:, :], tmp[:, :], MAGIC, None, ALU.add))
                link(nc.vector.tensor_scalar(tmp[:, :], tmp[:, :], MAGIC, None, ALU.subtract))
                link(nc.vector.scalar_tensor_tensor(pos[:, :], tmp[:, :], -float(EB), pos[:, :], ALU.mult, ALU.add))
                link(nc.vector.scalar_tensor_tensor(rec[:, :, 4].bitcast(U32), pos[:, :], float(NBP), tmp[:, :], ALU.mult, ALU.add))
                link(nc.vector.tensor_scalar(sbt[:, :], sbi[:, :], first[0:1, 1:2], None, ALU.is_ge))
                for k in range(2, T):
                    link(nc.vector.scalar_tensor_tensor(sbt[:, :], sbi[:, :], first[0:1, k:k + 1], sbt[:, :], ALU.is_ge, ALU.add))
                link(nc.vector.tensor_copy(tile_of[:, :], sbt[:, :]))
                dve.wait_ge(xw, 2 * T + 1)
                nc.vector.tensor_scalar(x_mv[:, :, 0], negmean[:, :], -1.0, None, ALU.mult)
                nc.vector.tensor_scalar(x_mv[:, :, 1], sums[:, 1, :], 1.0 / D, None, ALU.mult)
                dve.wait_ge(w0h, 1)
                nc.vector.tensor_tensor(wl[0][:, :, :], raw[:, :, :], wh[0][:, :, :].bitcast(F32), ALU.subtract)

    order_block()
    ath, atl = sbx("ath", [128, KC, N], F32R), sbx("atl", [128, KC, N], F32R)
    norm_block("ln_x", xs, lambda dve, link, t, m, r: link(
        nc.vector.tensor_scalar(xs[:, t, :], xs[:, t, :], m, r, ALU.subtract, ALU.mult)), ready=x_mv)
    transpose_block("tr_x", xs, ath, atl)
    x_stack.close()
    wh.append(sbx("r_wh1", [128, KC, D], F32R))
    wl.append(sbx("r_wl1", [128, KC, D], F32R))

    def relation_block():
        with ExitStack() as ctx:
            sb = allocate(ctx)
            ys = [sb(f"ys{s}", [NT, D]) for s in range(2)]
            rcur = [sb(f"rcur{s}", [NT, 5]) for s in range(2)]
            cur = [sb(f"c_cur{s}", [EB, G, 4]) for s in range(2)]
            src = [sb(f"c_src{s}", [EB, G, N + R], F16) for s in range(2)]
            dst = [sb(f"c_dst{s}", [EB, G, NT], F16) for s in range(2)]
            deg, tmp = sb("deg", [NT, T]), sb("c_tmp", [NT, T])
            ld, hi, lo, mm, ev = (sem("rel_" + n) for n in ("loaded", "high", "low", "product", "taken"))
            yst, sct, cp = sems("y_stored", 2), sems("scattered", 2), sem("record_copied")
            tl, ch, hot, cm, fl, sq = (sem("cnt_" + n) for n in ("table_loaded", "chain", "onehot", "product", "added", "sqrt"))
            block = ctx.enter_context(nc.Block())
            weights = rel_weights
            FREE = 2
            DONE = 1
            DEGREES = 3
            CB = (N + R) // 3
            assert 3 * CB == N + R

            @block.sync
            def _(sp):
                sp.dma_start(raw[:, :, :], weights[1]).then_inc(ld, 16)

                def pair(p, row, following):
                    for s in range(2):
                        for t in range(T):
                            n = s * T + t
                            sp.wait_ge(ev, p * PT + n + 1 + FREE)
                            sp.dma_start(row(n), ys[n % 2][:, :]).then_inc(yst[n % 2], 16)
                        if following is not None:
                            sp.wait_ge(lo, p * 2 + s + 1)
                            sp.dma_start(raw[:, :, :], following(s)).then_inc(ld, 16)

                def pairs(p0, p1):
                    with sp.Fori(p0, p1) as p:
                        pair(p, lambda n: yv[bass.ds(p * PT + n, 1)].rearrange("a p d -> (a p) d"),
                             lambda s: weights[bass.ds(p * 2 + s + 2, 1)].rearrange("a p k n -> (a p) k n"))

                pairs(0, COUNT_FROM)
                for s in range(2):
                    sp.wait_ge(sct[s], 16 * (EC // 2))
                sp.dma_start(table[:, :, :], tab_rows).then_inc(tl, 16)
                pairs(COUNT_FROM, PAIRS - 2)
                pair(PAIRS - 2, lambda n: yv[(PAIRS - 2) * PT + n],
                     lambda s: chunked((a["L0_gnn_W_root"], a["L0_mix_w_qkv"])[s]))
                pair(PAIRS - 1, lambda n: yv[(PAIRS - 1) * PT + n], None)
                for s in range(2):
                    sp.wait_ge(yst[s], 16 * (NREL * T // 2))

            @block.scalar
            def _(act):
                def pair(p, last):
                    for n in range(PT):
                        s, t = n // T, n % T
                        act.wait_ge(mm, p * PT + n + 1 + DONE)
                        if n >= 2 or not isinstance(p, int) or p:
                            act.wait_ge(yst[n % 2], p * (PT // 2 * 16) + (n // 2) * 16)
                        nc.scalar.activation(halves(ys[n % 2][:, :]), wide(n % 2), ACT.Copy).then_inc(ev, 1)
                        if t == 0 and not (last and s == 1):
                            act.wait_ge(ld, p * 32 + s * 16 + 16)
                            nc.scalar.activation(wh[1 - s][:, :, :], raw[:, :, :], ACT.Copy).then_inc(hi, 1)
                        if last and n == T:
                            act.wait_ge(ch, NSBP + DEGREES)
                            nc.scalar.activation(dinv[:, :], deg[:, :], ACT.Sqrt).then_inc(sq, 1)

                pair(0, False)
                with act.Fori(1, PAIRS - 1) as p:
                    pair(p, False)
                pair(PAIRS - 1, True)

            @block.vector
            def _(dve):
                def low(s):
                    return nc.vector.tensor_tensor(wl[s][:, :, :], raw[:, :, :], wh[s][:, :, :].bitcast(F32), ALU.subtract)

                link = Chain(dve, ch)
                link(nc.vector.memset(count[:, :, :], 0))
                with dve.Fori(0, COUNT_FROM) as p:
                    for s in range(2):
                        dve.wait_ge(hi, p * 2 + s + 1)
                        low(1 - s).then_inc(lo, 1)

                def onehots(s, c):
                    link(nc.vector.tensor_copy(cur[s][:, :, :], table[:, bass.ds(c * G, G), :]))
                    for g in range(G):
                        nc.vector.tensor_scalar(src[s][:, g, 0:N], iota16[:, :], cur[s][:, g, 1:2], None, ALU.is_equal)
                        nc.vector.tensor_scalar(dst[s][:, g, :], iota16[:, 0:NT], cur[s][:, g, 2:3], None, ALU.is_equal)
                        ins = nc.vector.tensor_scalar(src[s][:, g, N:N + R], iota16[:, 0:R], cur[s][:, g, 3:4], None, ALU.is_equal)
                    ins.then_inc(hot, 1)

                def add(c):
                    v = dve.value_load(tile_of[0:1, bass.ds(c, 1)], min_val=0, max_val=T - 1)
                    o = count[:, bass.ds(v, 1), :].rearrange("p a (b n) -> p (a b) n", b=3)
                    dve.wait_ge(cm, c + 1)
                    nc.vector.tensor_tensor(o, o, psum[0:NT, 4:7, 0:CB], ALU.add).then_inc(fl, 1)
                    dve.wait_ge(fl, c + 2)

                dve.wait_ge(tl, 16)
                onehots(0, 0)
                with dve.Fori(0, COUNT_PAIRS) as q:
                    link.enter(q, PT)
                    for n in range(PT):
                        onehots((n + 1) % 2, q * PT + n + 1)
                        add(q * PT + n)
                        if n % T == 3:
                            dve.wait_ge(hi, q * 2 + (COUNT_FROM * 2 + n // T + 1))
                            low(1 - n // T).then_inc(lo, 1)
                    link.leave(COUNT_PAIRS)
                dve.wait_ge(hi, (PAIRS - 1) * 2 + 1)
                low(1).then_inc(lo, 1)
                link(nc.vector.tensor_reduce(deg[:, :], count[:, :, N:N + R], AX.X, ALU.add))
                link(nc.vector.tensor_scalar(deg[:, :], deg[:, :], 1.0, None, ALU.add))
                dve.wait_ge(sq, 1)
                link(nc.vector.reciprocal(dinv[:, :], dinv[:, :]))
                polish(link, dinv[:, :], deg[:, :], tmp[:, :])
                link(nc.vector.tensor_scalar(inv_count[:, :, :], count[:, :, N:N + R], 1.0, None, ALU.max))
                link(nc.vector.reciprocal(inv_count[:, :, :], inv_count[:, :, :]))

            @block.tensor
            def _(pe):
                pe.sem_inc(mm, DONE)
                pe.sem_inc(ev, FREE)
                pe.sem_inc(fl, 1)

                def count_edges(s, c):
                    pe.wait_ge(hot, c + 1)
                    pe.wait_ge(fl, c + 1)
                    for g in range(G):
                        for i in range(3):
                            last = nc.tensor.matmul(psum[0:NT, 4 + i, 0:CB], dst[s][:, g, :], src[s][:, g, i * CB:(i + 1) * CB],
                                                    start=(g == 0), stop=(g == G - 1))
                    last.then_inc(cm, 1)

                def pair(p, c=None):
                    for n in range(PT):
                        s, t = n // T, n % T
                        if t == 0 and (s == 1 or not isinstance(p, int) or p):
                            pe.wait_ge(lo, p * 2 + s)
                        pe.wait_ge(ev, p * PT + n - 1 + FREE)
                        rows_mm(n % 2, ath, atl, wh[s], wl[s], slice(t * NT, (t + 1) * NT)).then_inc(mm, 1)
                        if c is not None:
                            count_edges(n % 2, c * PT + n)

                pair(0)
                with pe.Fori(1, COUNT_FROM) as p:
                    pair(p)
                with pe.Fori(0, COUNT_PAIRS) as q:
                    pair(q + COUNT_FROM, q)
                pair(PAIRS - 1)

            @block.gpsimd
            def _(pool):
                def scatter(c, s, first):
                    if not first:
                        pool.wait_ge(sct[s], c * 16)
                    nc.gpsimd.tensor_copy(rcur[s][:, :].bitcast(U32),
                                          rec[:, bass.ds(c * 2 + s, 1), :].rearrange("p a f -> p (a f)").bitcast(U32)).then_inc(cp, 1)
                    pool.wait_ge(cp, c * 2 + s + 1)
                    pool.nop(nofuse=True)
                    pool.indirect_dma_start(out=tab, out_offset=bass.IndirectOffsetOnAxis(rcur[s][:, 4:5].bitcast(U32), 0),
                                            in_=rcur[s][:, 0:4], in_offset=None).then_inc(sct[s], 16)

                scatter(0, 0, True)
                scatter(0, 1, True)
                with pool.Fori(1, EC // 2) as c:
                    scatter(c, 0, False)
                    scatter(c, 1, False)
                for s in range(2):
                    pool.wait_ge(sct[s], 16 * (EC // 2))

    relation_block()
    xform.close()

    room = [allocate(top, side="right")(f"room{i}", [128, T * D]) for i in range(1)]
    acc = room[0][0:NT, :].rearrange("p (t d) -> p t d", t=T)

    def gather_block():
        with ExitStack() as ctx:
            sb = allocate(ctx)
            SL = 4 * G
            PIECES = 8
            yg = [sb(f"yg{s}", [EB, D]) for s in range(SL)]
            row = [sb(f"row{s}", [EB, 1], U32) for s in range(SL)]
            cur = [sb(f"g_cur{s}", [EB, G, 4]) for s in range(4)]
            rel = sb("g_rel", [EB, NBP, R], F16)
            relt = [sb(f"g_relt{s}", [R, G, EB], F32R) for s in range(2)]
            parts = sb("inv_parts", [R, 2, N + 2], F32R)
            inv = [sb(f"g_inv{s}", [R, 2, NT + 1], F32R) for s in range(2)]
            sel = [sb(f"g_sel{s}", [EB, G, NT]) for s in range(4)]
            bias = sb("g_bias", [NT, D])
            iota32 = sb("iota32", [EB, NT])
            gl = sems("rows_gathered", SL)
            it = sem("gat_inverse_transposed")
            cp, ld, ch, hot, ip, trn, rt, vv, sl, mm, fl = (sem("gat_" + n) for n in (
                "row_copied", "loaded", "chain", "onehot", "inverse_parts", "transposed", "relation_rows", "weights",
                "selector", "product", "added"))
            block = ctx.enter_context(nc.Block())
            LAST = NSB + 2
            cuts = [min(NBP, round(NBP * i / PIECES)) for i in range(PIECES + 1)]

            @block.sync
            def _(sp):
                sp.dma_start(acc[:, :, :], tiled(y[R * N:(R + 1) * N, :])).then_inc(ld, 16)
                sp.dma_start(bias[:, :], spread(a["L0_gnn_b_rgcn"], NT)).then_inc(ld, 16)

            @block.gpsimd
            def _(pool):
                def fetch(i, s, first):
                    if not first:
                        pool.wait_ge(mm, (i - 1) * (SL // G) + s // G + 1)
                    nc.gpsimd.tensor_copy(row[s][:, :], table[:, bass.ds(i * SL + s, 1), 0:1].rearrange("p a f -> p (a f)").bitcast(U32)).then_inc(cp, 1)
                    pool.wait_ge(cp, i * SL + s + 1)
                    pool.nop(nofuse=True)
                    pool.indirect_dma_start(out=yg[s][:, :], out_offset=None, in_=y,
                                            in_offset=bass.IndirectOffsetOnAxis(row[s][:, :], 0)).then_inc(gl[s], 16)

                for s in range(SL):
                    fetch(0, s, True)
                with pool.Fori(1, NB // SL) as i:
                    for s in range(SL):
                        fetch(i, s, False)

            @block.scalar
            def _(act):
                act.wait_ge(ip, 1)
                with act.Fori(0, LAST // 2) as p:
                    for s in range(2):
                        n = p * 2 + s
                        v = act.value_load(tile_of[0:1, bass.ds(n, 1)], min_val=0, max_val=T - 1)
                        act.wait_ge(trn, n + 1)
                        nc.scalar.activation(inv[s][:, :, :], parts[:, :, bass.ds(v * NT, NT + 1)].bitcast(F32), ACT.Copy)
                        nc.scalar.activation(relt[s][:, :, :], psum[0:R, 4 + s, 0:G * EB].rearrange("p (g e) -> p g e", g=G),
                                             ACT.Copy).then_inc(rt, 1)

            @block.tensor
            def _(pe):
                pe.sem_inc(fl, 2)

                def transposes(s, n):
                    for g in range(G):
                        last = nc.tensor.matmul(psum[0:R, 4 + s, g * EB:(g + 1) * EB], rel[:, bass.ds(n * G + g, 1), :].rearrange("p a r -> p (a r)"),
                                                identh[:, :], start=True, stop=True)
                    last.then_inc(trn, 1)

                def weights(s, n):
                    pe.wait_ge(rt, n + 1)
                    for g in range(G):
                        for part in range(2):
                            last = nc.tensor.matmul(psum[:, 6 + s, g * EB:g * EB + NT + 1], relt[s][:, g, :], inv[s][:, part, :],
                                                    start=(part == 0), stop=(part == 1))
                    last.then_inc(vv, 1)

                def sums(p, q, n):
                    s = q % 2
                    pe.wait_ge(sl, n + 1)
                    pe.wait_ge(fl, n + 1)
                    for g in range(G):
                        slot = G * q + g
                        pe.wait_ge(gl[slot], p * 16 + 16)
                        for h in range(2):
                            last = nc.tensor.matmul(psum[0:NT, 2 * s + h, 0:HALF], sel[q][:, g, :], yg[slot][:, h * HALF:(h + 1) * HALF],
                                                    start=(g == 0), stop=(g == G - 1))
                    last.then_inc(mm, 1)

                for t in range(T):
                    last = nc.tensor.transpose(psum[0:R, t // 4, (t % 4) * NT:(t % 4 + 1) * NT], inv_count[:, t, :], ident[0:NT, 0:NT])
                last.then_inc(it, 1)
                pe.wait_ge(hot, 1)
                transposes(0, 0)
                transposes(1, 1)
                weights(0, 0)
                transposes(0, 2)
                weights(1, 1)
                pe.wait_ge(hot, PIECES)
                with pe.Fori(0, NSB // 4) as p:
                    for q in range(4):
                        n = p * 4 + q
                        transposes((q + 1) % 2, n + 3)
                        pe.wait_ge(sl, n + 1)
                        weights(q % 2, n + 2)
                        sums(p, q, n)

            @block.vector
            def _(dve):
                link = Chain(dve, ch)
                link(nc.vector.memset(parts[:, :, N:N + 2].bitcast(F32), 0.0))
                dve.wait_ge(it, 1)
                for to, got in ((slice(0, 8 * NT), psum[0:R, 0:2, 0:4 * NT]), (slice(8 * NT, N), psum[0:R, 2:3, 0:2 * NT])):
                    banks = got.shape[1]
                    high, low = (parts[:, i, to].rearrange("r (b n) -> r b n", b=banks) for i in range(2))
                    link(nc.vector.tensor_copy(high, got))
                    ins = nc.vector.tensor_tensor(low, got, high.bitcast(F32), ALU.subtract)
                ins.then_inc(ip, 1)
                for c0, c1 in zip(cuts, cuts[1:]):
                    nc.vector.tensor_tensor(rel[:, c0:c1, :], table[:, c0:c1, 3:4].broadcast_to([EB, c1 - c0, R]),
                                            iota16[:, 0:R].unsqueeze(1).broadcast_to([EB, c1 - c0, R]), ALU.is_equal).then_inc(hot, 1)
                link(nc.vector.tensor_copy(iota32[:, :], iota16[:, 0:NT]))

                def select(q, n):
                    link(nc.vector.tensor_copy(cur[q][:, :, :], table[:, bass.ds(n * G, G), :]))
                    dve.wait_ge(vv, n + 1)
                    for g in range(G):
                        ins = nc.vector.scalar_tensor_tensor(sel[q][:, g, :], iota32[:, :], cur[q][:, g, 2:3],
                                                             psum[:, 6 + q % 2, g * EB:g * EB + NT], ALU.is_equal, ALU.mult)
                    ins.then_inc(sl, 1)

                def add(s, n):
                    v = dve.value_load(tile_of[0:1, bass.ds(n, 1)], min_val=0, max_val=T - 1)
                    o = acc[:, bass.ds(v, 1), :].rearrange("p a (h n) -> p (a h) n", h=2)
                    dve.wait_ge(mm, n + 1)
                    nc.vector.tensor_tensor(o, o, wide(s), ALU.add).then_inc(fl, 1)

                select(0, 0)
                select(1, 1)
                dve.wait_ge(ld, 32)
                with dve.Fori(0, NSB // 4) as p:
                    link.enter(p, 4)
                    for q in range(4):
                        n = p * 4 + q
                        select((q + 2) % 4, n + 2)
                        dve.wait_ge(fl, n + 2)
                        add(q % 2, n)
                    link.leave(NSB // 4)
                dve.wait_ge(fl, NSB + 2)
                for t in range(T):
                    nc.vector.tensor_tensor(acc[:, t, :], acc[:, t, :], bias[:, :], ALU.add)

    gather_block()

    with ExitStack() as ctx:
        sb = allocate(ctx)
        hh, hl = sb("h1_high", [128, KC, N], F32R), sb("h1_low", [128, KC, N], F32R)
        rows_block("gcn_", acc, hh, hl, a["L0_gnn_W_gcn"], lambda dve, link, t, rows: nc.vector.tensor_scalar(
            halves(acc[:, t, :]), rows, dinv[:, t:t + 1], None, ALU.mult))

    room.append(allocate(top, side="right")("room1", [128, T * D]))
    gn = room[1][0:NT, :].rearrange("p (t d) -> p t d", t=T)

    def propagate_block():
        with ExitStack() as ctx:
            sb = allocate(ctx)
            cf = [sb(f"p_count{s}", [NT, N]) for s in range(2)]
            ch_, cl_ = ([sb(f"p_{part}{s}", [NT, T, NT], F32R) for s in range(2)] for part in ("high", "low"))
            xh, xl = sb("p_xh", [NT, T, D], F32R), sb("p_xl", [NT, T, D], F32R)
            bias = sb("p_bias", [NT, D])
            nxt = sem("prop_next_loaded")
            ld, ch, rd, tr, hi, lo, xhi, xlo, mm, ev = (sem("prop_" + n) for n in (
                "loaded", "chain", "ready", "transposed", "high", "low", "x_high", "x_low", "product", "taken"))
            block = ctx.enter_context(nc.Block())
            groups = ((0, 4), (4, 8), (8, 10))

            def bank(j):
                i0, i1 = groups[j]
                return psum[0:NT, 4 + j, 0:(i1 - i0) * NT].rearrange("p (i n) -> p i n", i=i1 - i0)

            @block.sync
            def _(sp):
                sp.dma_start(bias[:, :], spread(a["L0_gnn_b_gcn"], NT)).then_inc(ld, 16)
                sp.wait_ge(xlo, T)
                sp.dma_start(acc, tiled(y[(R + 1) * N:(R + 2) * N, :])).then_inc(nxt, 16)
                sp.wait_ge(nxt, 16)

            @block.tensor
            def _(pe):
                def transposes(t):
                    pe.wait_ge(rd, t + 1)
                    if t:
                        pe.wait_ge(lo, 3 * t)
                    for i in range(T):
                        last = nc.tensor.transpose(psum[0:NT, 4 + i // 4, (i % 4) * NT:(i % 4 + 1) * NT],
                                                   cf[t % 2][:, i * NT:(i + 1) * NT], ident[0:NT, 0:NT])
                        if i in (3, 7, 9):
                            last.then_inc(tr, 1)

                transposes(0)
                for t in range(T):
                    if t + 1 < T:
                        transposes(t + 1)
                    pe.wait_ge(lo, 3 * t + 3)
                    if t >= 2:
                        pe.wait_ge(ev, t - 1)
                    outs = [psum[0:NT, 2 * (t % 2) + h, 0:HALF] for h in range(2)]
                    for i in range(T):
                        if t == 0:
                            pe.wait_ge(xlo, i + 1)
                        last = split_mm(outs, ch_[t % 2][:, i, :], cl_[t % 2][:, i, :],
                                        [(xh[:, i, h * HALF:(h + 1) * HALF], xl[:, i, h * HALF:(h + 1) * HALF]) for h in range(2)],
                                        i == 0, i == T - 1)
                    last.then_inc(mm, 1)

            @block.scalar
            def _(act):
                def high(t):
                    for j, (i0, i1) in enumerate(groups):
                        act.wait_ge(tr, 3 * t + j + 1)
                        nc.scalar.activation(ch_[t % 2][:, i0:i1, :], bank(j), ACT.Copy).then_inc(hi, 1)

                nc.scalar.activation(xh[:, 0, :], acc[:, 0, :], ACT.Copy).then_inc(xhi, 1)
                high(0)
                for i in range(1, T):
                    nc.scalar.activation(xh[:, i, :], acc[:, i, :], ACT.Copy).then_inc(xhi, 1)
                for t in range(1, T):
                    if t >= 2:
                        act.wait_ge(mm, t - 1)
                    high(t)

            @block.vector
            def _(dve):
                link = Chain(dve, ch)

                def ready(t):
                    link(nc.vector.tensor_copy(cf[t % 2][:, :], count[:, t, 0:N]))
                    own = cf[t % 2][:, t * NT:(t + 1) * NT]
                    nc.vector.tensor_tensor(own, own, ident[0:NT, 0:NT], ALU.add).then_inc(rd, 1)

                def low(t):
                    for j, (i0, i1) in enumerate(groups):
                        dve.wait_ge(hi, 3 * t + j + 1)
                        nc.vector.tensor_tensor(cl_[t % 2][:, i0:i1, :], bank(j), ch_[t % 2][:, i0:i1, :].bitcast(F32),
                                                ALU.subtract).then_inc(lo, 1)

                ready(0)
                ready(1)
                low(0)
                for i in range(T):
                    dve.wait_ge(xhi, i + 1)
                    nc.vector.tensor_tensor(xl[:, i, :], acc[:, i, :], xh[:, i, :].bitcast(F32), ALU.subtract).then_inc(xlo, 1)
                dve.wait_ge(ld, 16)
                for t in range(T):
                    if t + 1 < T:
                        low(t + 1)
                    if t + 2 < T:
                        dve.wait_ge(tr, 3 * t + 3)
                        ready(t + 2)
                    dve.wait_ge(mm, t + 1)
                    nc.vector.scalar_tensor_tensor(halves(gn[:, t, :]), wide(t % 2), dinv[:, t:t + 1], halves(bias[:, :]),
                                                   ALU.mult, ALU.add).then_inc(ev, 1)

    propagate_block()
    recycle()
    graph.close()

    row_parts, row_mv = (allocate(top)(f"row_{n}", [NT, T, c]) for n, c in (("parts", 12), ("mean_var", 2)))
    w = acc

    mixing = ExitStack()
    scale = allocate(mixing)("m_scale", [NT, D])
    pi = allocate(mixing)("m_pi", [NT, T, H])

    def per_head(ap):
        return ap.unsqueeze(2).broadcast_to([NT, H, DH])

    def by_head(ap):
        return ap.rearrange("p (h d) -> p h d", h=H)

    def mix_block():
        with ExitStack() as ctx:
            sb = allocate(ctx)
            w2 = sb("w2", [NT, T, D])
            tmp = [sb(f"m_tmp{s}", [NT, D]) for s in range(2)]
            temp, lg = sb("m_temp", [NT, H]), sb("m_logits", [NT, T, H])
            lt, pt = sb("m_lt", [H, N]), sb("m_pt", [H, N])
            mx, sm, sp2 = sb("m_max", [H, 1]), sb("m_sum", [H, 1]), sb("m_sum2", [H, 1])
            pn = sb("m_pin", [NT, T, H])
            ld, ch, sq, cs, nr, tr, ex, bk, dt = (sem("mix_" + n) for n in (
                "loaded", "chain", "squared", "column_sums", "norms", "transposed", "exp", "back", "dots"))
            ts = sem("mix_tiles_summed")
            lc, pc, dd = sem("mix_logits_done"), sem("mix_pi_done"), sem("mix_dots_in")
            block = ctx.enter_context(nc.Block())

            @block.sync
            def _(sp):
                sp.dma_start(temp[:, :], spread(a["L0_mix_temp"].rearrange("h a -> (h a)"), NT)).then_inc(ld, 16)

            @block.tensor
            def _(pe):
                pe.wait_ge(ts, 1)
                for h in range(2):
                    last = nc.tensor.matmul(psum[0:NT, h, 0:HALF], ones[0:NT, 0:NT], scale[:, h * HALF:(h + 1) * HALF],
                                            start=True, stop=True)
                last.then_inc(cs, 1)
                for t in range(T):
                    pe.wait_ge(lc, t + 1)
                    last = nc.tensor.transpose(psum[0:H, 2 + t // 4, (t % 4) * NT:(t % 4 + 1) * NT], lg[:, t, :], ident[0:NT, 0:NT])
                last.then_inc(tr, 1)
                pe.wait_ge(pc, 1)
                for n, m in enumerate((lt, pt)):
                    for t in range(T):
                        last = nc.tensor.transpose(psum[0:NT, 5 + n, t * H:(t + 1) * H], m[:, t * NT:(t + 1) * NT], ident[0:H, 0:H])
                last.then_inc(bk, 1)
                for t in range(T):
                    pe.wait_ge(dd, t + 1)
                    for h in range(2):
                        last = nc.tensor.matmul(psum[0:NT, h, 0:HALF], ones[0:NT, 0:NT], w2[:, t, h * HALF:(h + 1) * HALF],
                                                start=(t == 0), stop=(t == T - 1))
                last.then_inc(dt, 1)

            @block.scalar
            def _(act):
                for t in range(T):
                    nc.scalar.activation(w2[:, t, :], w[:, t, :], ACT.Square).then_inc(sq, 1)
                act.wait_ge(cs, 1)
                nc.scalar.activation(halves(scale[:, :]), wide(0), ACT.Sqrt).then_inc(nr, 1)
                act.wait_ge(ex, 1)
                nc.scalar.activation(lt[:, :], lt[:, :], ACT.Exp, bias=mx[:, :], accum_out=sm[:, :]).then_inc(nr, 1)

            @block.vector
            def _(dve):
                link = Chain(dve, ch)
                dve.wait_ge(sq, 2)
                link(nc.vector.tensor_tensor(scale[:, :], w2[:, 0, :], w2[:, 1, :], ALU.add))
                for t in range(2, T):
                    dve.wait_ge(sq, t + 1)
                    ins = nc.vector.tensor_tensor(scale[:, :], scale[:, :], w2[:, t, :], ALU.add)
                    if t + 1 < T:
                        link(ins)
                ins.then_inc(ts, 1)
                dve.wait_ge(ld, 16)
                dve.wait_ge(nr, 1)
                link(nc.vector.tensor_scalar(scale[:, :], scale[:, :], 1e-12, None, ALU.max))
                link(nc.vector.reciprocal(scale[:, :], scale[:, :]))
                link(nc.vector.tensor_tensor(scale[:, :], scale[:, :], scale[:, :], ALU.mult))
                for t in range(T):
                    x = tmp[t % 2]
                    link(nc.vector.tensor_tensor(x[:, :], w2[:, t, :], scale[:, :], ALU.mult))
                    link(nc.vector.tensor_reduce(lg[:, t, :], by_head(x[:, :]), AX.X, ALU.add))
                    nc.vector.tensor_tensor(lg[:, t, :], lg[:, t, :], temp[:, :], ALU.mult).then_inc(lc, 1)
                dve.wait_ge(tr, 1)
                link(nc.vector.tensor_copy(lt[:, 0:8 * NT].rearrange("p (a n) -> p a n", a=2), psum[0:H, 2:4, 0:4 * NT]))
                link(nc.vector.tensor_copy(lt[:, 8 * NT:N], psum[0:H, 4, 0:2 * NT]))
                link(nc.vector.tensor_reduce(mx[:, :], lt[:, :], AX.X, ALU.max))
                nc.vector.tensor_scalar(mx[:, :], mx[:, :], -1.0, None, ALU.mult).then_inc(ex, 1)
                dve.wait_ge(nr, 2)
                link(nc.vector.reciprocal(sm[:, :], sm[:, :]))
                link(nc.vector.tensor_scalar(lt[:, :], lt[:, :], sm[:, :], None, ALU.mult))
                link(nc.vector.tensor_reduce(sp2[:, :], lt[:, :], AX.X, ALU.add))
                link(nc.vector.tensor_scalar(sp2[:, :], sp2[:, :], 1e-8, None, ALU.add))
                link(nc.vector.reciprocal(sp2[:, :], sp2[:, :]))
                nc.vector.tensor_scalar(pt[:, :], lt[:, :], sp2[:, :], None, ALU.mult).then_inc(pc, 1)
                dve.wait_ge(bk, 1)
                link(nc.vector.tensor_copy(pi[:, :, :], psum[0:NT, 5, 0:T * H].rearrange("p (t h) -> p t h", t=T)))
                link(nc.vector.tensor_copy(pn[:, :, :], psum[0:NT, 6, 0:T * H].rearrange("p (t h) -> p t h", t=T)))
                for t in range(T):
                    nc.vector.tensor_tensor(by_head(w2[:, t, :]), by_head(w2[:, t, :]), per_head(pn[:, t, :]), ALU.mult).then_inc(dd, 1)
                dve.wait_ge(dt, 1)
                link(nc.vector.tensor_scalar(halves(scale[:, :]), wide(0), 1.0, None, ALU.add))
                link(nc.vector.reciprocal(scale[:, :], scale[:, :]))
                link(nc.vector.tensor_scalar(scale[:, :], scale[:, :], -1.0, None, ALU.mult))

    mix_block()

    with ExitStack() as ctx:
        sb = allocate(ctx)
        hh, hl = sb("mix_high", [128, KC, N], F32R), sb("mix_low", [128, KC, N], F32R)
        bias = sb("o_bias", [NT, D])

        def sink(dve, link, t, rows):
            g = halves(gn[:, t, :])
            link(nc.vector.tensor_tensor(g, g, rows, ALU.add))
            link(nc.vector.tensor_tensor(gn[:, t, :], gn[:, t, :], bias[:, :], ALU.add))
            link(nc.vector.tensor_tensor(gn[:, t, :], gn[:, t, :], w[:, t, :], ALU.add))
            return stats(link, gn, row_parts, row_mv, t)

        def mixed_rows(link, t):
            link(nc.vector.tensor_tensor(by_head(w[:, t, :]), by_head(w[:, t, :]), per_head(pi[:, t, :]), ALU.mult))
            return nc.vector.tensor_tensor(w[:, t, :], w[:, t, :], scale[:, :], ALU.mult)

        rows_block("wout_", w, hh, hl, a["L0_mix_w_out"], sink, loads=[(bias[:, :], spread(a["L0_mix_b_out"], NT))],
                   tile_load=lambda t: (w[:, t, :], a["x"][t * NT:(t + 1) * NT, :]),
                   store=lambda t: (scr["x1"][t * NT:(t + 1) * NT, :], gn[:, t, :]), prepare=mixed_rows)
    mixing.close()

    hidden, nrm = gn, acc
    norm_block("ln_h", hidden, lambda dve, link, t, m, r: link(
        nc.vector.tensor_scalar(hidden[:, t, :], hidden[:, t, :], m, r, ALU.subtract, ALU.mult)), ready=row_mv)

    def affine_norm(tag, src, xs, g, b, ready=None):
        with ExitStack() as ctx:
            sb = allocate(ctx)
            gain, shift = sb(tag + "gain", [NT, D]), sb(tag + "shift", [NT, D])
            gl = sem(tag + "gain_loaded")

            def then(dve, link, t, m, r):
                if t == 0:
                    dve.wait_ge(gl, 32)
                link(nc.vector.scalar_tensor_tensor(xs[:, t, :], src[:, t, :], m, gain[:, :], ALU.subtract, ALU.mult))
                link(nc.vector.scalar_tensor_tensor(xs[:, t, :], xs[:, t, :], r, shift[:, :], ALU.mult, ALU.add))

            norm_block(tag, src, then, [(gain[:, :], spread(g, NT)), (shift[:, :], spread(b, NT))], gl, ready)

    affine_norm("ln_1", hidden, nrm, a["L0_ffn_g1"], a["L0_ffn_b1"])

    keep = ExitStack()
    sbk = allocate(keep)
    unrouted = sbk("unrouted", [NT, T])
    score = sbk("score", [NT, T])
    pooled_w = sbk("pooled_w", [NT, D])
    ctxs = sbk("ctxs", [TH, 2, D])
    qt = sbk("qt", [128, KC, TOP])

    def route_block():
        with ExitStack() as ctx:
            sb = allocate(ctx)
            wr, br = sb("wr", [NT, D]), sb("br", [NT, 1])
            wm, wq = sb("r_wm", [128, KC, D]), sb("r_wq", [128, KC, D])
            bq = sb("r_bq", [128, KC])
            junk, earlier = sb("r_junk", [NT, N]), sb("r_earlier", [NT, NT])
            z, e, idx, rank, ties, before = (sb("r_" + n, [NT, T]) for n in ("z", "e", "idx", "rank", "ties", "before"))
            srow, iota = sb("srow", [NT, N]), sb("r_iota", [NT, N])
            sel = sb("sel", [NT, T, TOP])
            nselt = sb("nselt", [128, KC, TOP])
            total, pt, ptb = sb("r_total", [128, 1]), sb("r_pt", [128, KC]), sb("r_ptb", [128, KC, NT])
            ld, ldw, co, ch, zs, ex, sc, sd, rk, rd = (sem("rt_" + n) for n in (
                "loaded", "weights_loaded", "const", "chain", "z", "exp", "scores", "score_rows", "ranks", "rank_rows"))
            po, pd, sl, ns, nd, qd, pw = (sem("rt_" + n) for n in (
                "pooled", "pooled_ready", "selector", "selected", "selected_ready", "queries", "pooled_w"))
            qe, hs, ldm = sem("rt_queries_taken"), sem("rt_hidden_stored"), sem("rt_wm_loaded")
            block = ctx.enter_context(nc.Block())
            by_tile = lambda ap: ap.rearrange("(t p) -> p t", p=NT)

            @block.sync
            def _(sp):
                sp.dma_start(wr[:, :], spread(a["L0_ffn_Wr"], NT)).then_inc(ld, 16)
                sp.dma_start(br[:, :], spread(a["L0_ffn_br"], NT)).then_inc(ld, 16)
                sp.dma_start(bq[:, :], a["L0_ffn_bq"].rearrange("(k p) -> p k", p=128)).then_inc(ld, 16)
                sp.dma_start(wq[:, :, :], chunked(a["L0_ffn_Wq"])).then_inc(ldw, 16)
                sp.wait_ge(sc, 1)
                sp.dma_start(by_tile(scr["score"]), score[:, :]).then_inc(sd, 16)
                sp.wait_ge(sd, 16)
                sp.dma_start(srow[:, :], spread(scr["score"], NT)).then_inc(sd, 16)
                sp.dma_start(wm[:, :, :], chunked(a["L0_ffn_Wm"])).then_inc(ldm, 16)
                sp.dma_start(tiled(scr["hidden"]), hidden).then_inc(hs, 16)
                sp.wait_ge(rk, 1)
                sp.dma_start(by_tile(scr["rank"]), rank[:, :]).then_inc(rd, 16)
                sp.wait_ge(rd, 16)
                sp.wait_ge(hs, 16)

            @block.gpsimd
            def _(pool):
                imprecise = dict(allow_small_or_imprecise_dtypes=True)
                pool.iota(iota[:, :], pattern=[[1, N]], base=0, channel_multiplier=0, **imprecise).then_inc(co, 1)
                pool.iota(idx[:, :], pattern=[[NT, T]], base=0, channel_multiplier=1, **imprecise).then_inc(co, 1)

            @block.scalar
            def _(act):
                act.wait_ge(zs, 1)
                nc.scalar.activation(e[:, :], z[:, :], ACT.Exp, scale=-1.0).then_inc(ex, 1)

            @block.tensor
            def _(pe):
                pe.wait_ge(sc, 1)
                for k in range(KC):
                    for t in range(T):
                        nc.tensor.matmul(psum[:, 0, k:k + 1], nrm[:, t, k * 128:(k + 1) * 128], score[:, t:t + 1],
                                         start=(t == 0), stop=(t == T - 1))
                for t in range(T):
                    last = nc.tensor.matmul(psum[:, 0, KC:KC + 1], ones[0:NT, :], score[:, t:t + 1], start=(t == 0), stop=(t == T - 1))
                last.then_inc(po, 1)
                pe.wait_ge(sl, T)
                for k in range(KC):
                    if k >= 2:
                        pe.wait_ge(nd, k - 1)
                    for t in range(T):
                        last = nc.tensor.matmul(psum[:, 4 + k % 2, 0:TOP], nrm[:, t, k * 128:(k + 1) * 128], sel[:, t, :],
                                                start=(t == 0), stop=(t == T - 1))
                    last.then_inc(ns, 1)
                pe.wait_ge(nd, KC)
                pe.wait_ge(ldw, 16)
                for o in range(KC):
                    if o >= 2:
                        pe.wait_ge(qe, o - 1)
                    for k in range(KC):
                        last = nc.tensor.matmul(psum[:, 6 + o % 2, 0:TOP], wq[:, k, o * 128:(o + 1) * 128], nselt[:, k, :],
                                                start=(k == 0), stop=(k == KC - 1))
                    last.then_inc(qd, 1)
                pe.wait_ge(pd, 1)
                pe.wait_ge(ldm, 16)
                for k in range(KC):
                    for h in range(2):
                        last = nc.tensor.matmul(psum[0:NT, 2 + h, 0:HALF], ptb[:, k, :], wm[:, k, h * HALF:(h + 1) * HALF],
                                                start=(k == 0), stop=(k == KC - 1))
                last.then_inc(pw, 1)

            @block.vector
            def _(dve):
                link = Chain(dve, ch)
                dve.wait_ge(ld, 48)
                dve.wait_ge(co, 2)
                for t in range(T):
                    link(nc.vector.scalar_tensor_tensor(junk[:, 0:D], nrm[:, t, :], 1.0, wr[:, :], ALU.mult, ALU.mult, accum_out=z[:, t:t + 1]))
                nc.vector.tensor_scalar(z[:, :], z[:, :], br[:, :], None, ALU.add).then_inc(zs, 1)
                dve.wait_ge(ex, 1)
                link(nc.vector.tensor_scalar(e[:, :], e[:, :], 1.0, None, ALU.add))
                nc.vector.reciprocal(score[:, :], e[:, :]).then_inc(sc, 1)
                dve.wait_ge(sd, 32)
                link(nc.vector.tensor_scalar(earlier[:, :], iota[:, 0:NT], idx[:, 0:1], None, ALU.is_lt))
                for t in range(T):
                    own = score[:, t:t + 1]
                    if t:
                        link(nc.vector.tensor_scalar(junk[:, 0:t * NT], srow[:, 0:t * NT], own, None, ALU.is_le, ALU.add,
                                                     accum_out=before[:, t:t + 1]))
                    link(nc.vector.tensor_scalar(junk[:, t * NT:N], srow[:, t * NT:N], own, None, ALU.is_lt, ALU.add,
                                                 accum_out=rank[:, t:t + 1]))
                    link(nc.vector.scalar_tensor_tensor(junk[:, 0:NT], srow[:, t * NT:(t + 1) * NT], own, earlier[:, :],
                                                        ALU.is_equal, ALU.mult, accum_out=ties[:, t:t + 1]))
                link(nc.vector.tensor_tensor(rank[:, 1:T], rank[:, 1:T], before[:, 1:T], ALU.add))
                nc.vector.tensor_tensor(rank[:, :], rank[:, :], ties[:, :], ALU.add).then_inc(rk, 1)
                dve.wait_ge(rk, 1)
                link(nc.vector.tensor_scalar(unrouted[:, :], rank[:, :], float(TOP), None, ALU.is_ge))
                for t in range(T):
                    nc.vector.tensor_scalar(sel[:, t, :], iota[:, 0:TOP], rank[:, t:t + 1], None, ALU.is_equal).then_inc(sl, 1)
                dve.wait_ge(po, 1)
                link(nc.vector.tensor_scalar(total[:, :], psum[:, 0, KC:KC + 1], 1e-6, None, ALU.add))
                link(nc.vector.reciprocal(total[:, :], total[:, :]))
                link(nc.vector.tensor_scalar(pt[:, :], psum[:, 0, 0:KC], total[:, :], None, ALU.mult))
                nc.vector.tensor_copy(ptb[:, :, :], pt[:, :].unsqueeze(2).broadcast_to([128, KC, NT])).then_inc(pd, 1)
                for k in range(KC):
                    dve.wait_ge(ns, k + 1)
                    nc.vector.tensor_copy(nselt[:, k, :], psum[:, 4 + k % 2, 0:TOP]).then_inc(nd, 1)
                for o in range(KC):
                    dve.wait_ge(qd, o + 1)
                    nc.vector.tensor_scalar(qt[:, o, :], psum[:, 6 + o % 2, 0:TOP], bq[:, o:o + 1], None, ALU.add).then_inc(qe, 1)
                dve.wait_ge(pw, 1)
                link(nc.vector.tensor_copy(halves(pooled_w[:, :]), wide(1)))

    route_block()

    def cols_block(tag, ah, al, weight, oc, bias_dram, sink, kc=KC, then=None):
        with ExitStack() as ctx:
            sb = allocate(ctx)
            raw = [sb(f"{tag}raw{s}", [128, kc, 128]) for s in range(3)]
            wh, wl = sb(tag + "wh", [128, kc, oc * 128], F32R), sb(tag + "wl", [128, kc, oc * 128], F32R)
            bias = sb(tag + "bias", [128, oc])
            wld = sems(tag + "weights_loaded", 3)
            bl, hi, lo, mm, ev, ch = (sem(tag + n) for n in ("bias_loaded", "high", "low", "product", "taken", "chain"))
            block = ctx.enter_context(nc.Block())
            feature = lambda o: slice(o * 128, (o + 1) * 128)

            @block.sync
            def _(sp):
                for o in range(oc):
                    if o >= 3:
                        sp.wait_ge(lo, o - 2)
                    sp.dma_start(raw[o % 3][:, :, :], chunked(weight)[:, :, feature(o)]).then_inc(wld[o % 3], 16)
                    if o == 0:
                        sp.dma_start(bias[:, :], bias_dram.rearrange("(k p) -> p k", p=128)).then_inc(bl, 16)

            @block.scalar
            def _(act):
                def high(o):
                    act.wait_ge(wld[o % 3], 16 * (o // 3 + 1))
                    nc.scalar.activation(wh[:, :, feature(o)], raw[o % 3][:, :, :], ACT.Copy).then_inc(hi, 1)

                high(0)
                high(1)
                act.wait_ge(bl, 16)
                for o in range(oc):
                    if o + 2 < oc:
                        high(o + 2)
                    for c in range(3):
                        n = 3 * o + c
                        act.wait_ge(mm, n + 1)
                        sink(o, slice(COLS[c][0], COLS[c][0] + COLS[c][1]), psum[:, n % 8, 0:COLS[c][1]], bias[:, o:o + 1]).then_inc(ev, 1)

            @block.vector
            def _(dve):
                link = Chain(dve, ch)

                def low(o):
                    dve.wait_ge(hi, o + 1)
                    nc.vector.tensor_tensor(wl[:, :, feature(o)], raw[o % 3][:, :, :], wh[:, :, feature(o)].bitcast(F32),
                                            ALU.subtract).then_inc(lo, 1)

                low(0)
                low(1)
                for o in range(oc):
                    if o + 2 < oc:
                        low(o + 2)
                    for c in range(3 if then else 0):
                        dve.wait_ge(ev, 3 * o + c + 1)
                        then(link, o, slice(COLS[c][0], COLS[c][0] + COLS[c][1]))

            @block.tensor
            def _(pe):
                for n in range(oc * 3):
                    o, (c0, cn) = n // 3, COLS[n % 3]
                    if n % 3 == 0:
                        pe.wait_ge(lo, o + 1)
                    if n >= 8:
                        pe.wait_ge(ev, n - 7)
                    for k in range(kc):
                        last = split_mm([psum[:, n % 8, 0:cn]], wh[:, k, feature(o)], wl[:, k, feature(o)],
                                        [(ah[:, k, c0:c0 + cn], al[:, k, c0:c0 + cn])], k == 0, k == kc - 1)
                    last.then_inc(mm, 1)

    v = acc
    kt = room[1][:, 0:KC * N].rearrange("p (k n) -> p k n", k=KC)
    def attention_block(hh, hl, bias):
        with ExitStack() as ctx:
            sb = allocate(ctx)
            p = [sb(f"probs{s}", [TH, N]) for s in range(2)]
            pt = [sb(f"probst{s}", [NT, T, TH]) for s in range(2)]
            mx, nm, sm, rs = (sb("a_" + n, [TH, 2, 2]) for n in ("max", "negmax", "sum", "rsum"))
            wraw = [sb(f"a_raw{s}", [128, D]) for s in range(2)]
            wh, wl = sb("a_wh", [128, KC, D], F32R), sb("a_wl", [128, KC, D], F32R)
            mixed = [sb(f"a_mix{s}", [NT, D]) for s in range(2)]
            base = [m[0:NT, :] for m in wraw]
            qk, mxs, ex, tr, tc, pv, cx, ch = (sem("att_" + n) for n in (
                "scores", "max", "exp", "transposed", "copied", "context", "context_taken", "chain"))
            bl, hi, lo, gm, gb, gt = (sem("wm_" + n) for n in ("bias_loaded", "high", "low", "product", "biased", "taken"))
            wld, mst, hld = sems("wm_loaded", 2), sems("mix_stored", 2), sems("hidden_loaded", 2)
            block = ctx.enter_context(nc.Block())
            U = 2 * H
            units = [(i, h) for i in range(2) for h in range(H)]
            STEPS = 2 * T * KC
            FIRST = 2

            def steps(u, place):
                if u < FIRST:
                    return []
                s0, s1 = ((v - FIRST) * STEPS // (U - FIRST) for v in (u, u + 1))
                assert 5 <= s1 - s0 <= 6
                return [range(s0, s0 + 1), range(s0 + 1, s0 + 3), range(s0 + 3, s1)][place]

            @block.sync
            def _(sp):
                sp.dma_start(bias[:, :], spread(a["L0_ffn_bm"], NT)).then_inc(bl, 16)
                for k in range(KC):
                    if k >= 2:
                        sp.wait_ge(lo, k - 1)
                    sp.dma_start(wraw[k % 2][:, :], chunked(a["L0_ffn_Wm"])[:, k, :]).then_inc(wld[k % 2], 16)
                sp.wait_ge(lo, KC)
                for t in range(T + 2):
                    if t >= 2:
                        sp.wait_ge(gt, 2 * (t - 1))
                        sp.dma_start(scr["mix"][(t - 2) * NT:(t - 1) * NT, :], mixed[t % 2][:, :]).then_inc(mst[t % 2], 16)
                    if t < T:
                        sp.dma_start(base[t % 2], scr["hidden"][t * NT:(t + 1) * NT, :]).then_inc(hld[t % 2], 16)
                for s in range(2):
                    sp.wait_ge(mst[s], 16 * (T // 2))

            @block.tensor
            def _(pe):
                def scores(u):
                    i, h = units[u]
                    s, rows = u % 2, slice((h % 2) * DH, (h % 2 + 1) * DH)
                    if u >= 2:
                        pe.wait_ge(ex, 2 * (u - 1))
                    for c, (c0, cn) in enumerate(COLS):
                        if u >= 2 and c == 2:
                            pe.wait_ge(cx, u - 1)
                        last = nc.tensor.matmul(psum[0:TH, 3 * s + c, 0:cn], qt[rows, h // 2, i * TH:(i + 1) * TH],
                                                kt[rows, h // 2, c0:c0 + cn], start=True, stop=True)
                    last.then_inc(qk, 1)

                def transposes(u, b):
                    if b == 0:
                        pe.wait_ge(ex, 2 * (u + 1))
                    if u or b:
                        pe.wait_ge(tc, 2 * u + b)
                    for j in range(5):
                        k = 5 * b + j
                        last = nc.tensor.transpose(psum[0:NT, 6, j * TH:(j + 1) * TH], p[u % 2][:, k * NT:(k + 1) * NT], ident[0:TH, 0:TH])
                    last.then_inc(tr, 1)

                def context(u):
                    pe.wait_ge(tc, 2 * (u + 1))
                    h = units[u][1]
                    for k in range(T):
                        last = nc.tensor.matmul(psum[0:TH, 3 * (u % 2) + 2, 440:440 + DH], pt[u % 2][:, k, :], v[:, k, h * DH:(h + 1) * DH],
                                                start=(k == 0), stop=(k == T - 1))
                    last.then_inc(pv, 1)

                def mixing(u, place):
                    for step in steps(u, place):
                        half, k = divmod(step, KC)
                        t, h = divmod(half, 2)
                        if half == 0:
                            pe.wait_ge(lo, k + 1)
                        if k == 0 and half:
                            pe.wait_ge(gb, half)
                        cols = slice(t * NT, (t + 1) * NT)
                        last = split_mm([psum[0:NT, 7, 0:HALF]], hh[:, k, cols], hl[:, k, cols],
                                        [(wh[:, k, h * HALF:(h + 1) * HALF], wl[:, k, h * HALF:(h + 1) * HALF])], k == 0, k == KC - 1)
                        if k == KC - 1:
                            last.then_inc(gm, 1)

                scores(0)
                for u in range(U):
                    if u + 1 < U:
                        scores(u + 1)
                    mixing(u, 0)
                    transposes(u, 0)
                    mixing(u, 1)
                    transposes(u, 1)
                    mixing(u, 2)
                    context(u)

            @block.scalar
            def _(act):
                def high(k):
                    act.wait_ge(wld[k % 2], 16 * (k // 2 + 1))
                    nc.scalar.activation(wh[:, k, :], wraw[k % 2][:, :], ACT.Copy).then_inc(hi, 1)

                def copy(u, b):
                    act.wait_ge(tr, 2 * u + b + 1)
                    if u >= 2 and b == 0:
                        act.wait_ge(pv, u - 1)
                    nc.scalar.activation(pt[u % 2][:, 5 * b:5 * b + 5, :],
                                         psum[0:NT, 6, 0:5 * TH].rearrange("p (k n) -> p k n", k=5), ACT.Copy).then_inc(tc, 1)

                def exponentials(u):
                    s = u % 2
                    act.wait_ge(mxs, u + 1)
                    nc.scalar.activation(p[s][:, 0:832].rearrange("p (a n) -> p a n", a=2), psum[0:TH, 3 * s:3 * s + 2, 0:416], ACT.Exp,
                                         bias=nm[:, s, 0:1], scale=0.125, accum_out=sm[:, s, 0:1]).then_inc(ex, 1)
                    nc.scalar.activation(p[s][:, 832:N], psum[0:TH, 3 * s + 2, 0:418], ACT.Exp,
                                         bias=nm[:, s, 0:1], scale=0.125, accum_out=sm[:, s, 1:2]).then_inc(ex, 1)

                exponentials(0)
                for u in range(U):
                    for k in range(2 * u, min(2 * u + 2, KC)):
                        high(k)
                    copy(u, 0)
                    copy(u, 1)
                    if u + 1 < U:
                        exponentials(u + 1)

            @block.vector
            def _(dve):
                link = Chain(dve, ch)

                def maximum(u):
                    s = u % 2
                    dve.wait_ge(qk, u + 1)
                    link(nc.vector.tensor_reduce(mx[:, s, 0:1], psum[0:TH, 3 * s:3 * s + 2, 0:416], AX.XY, ALU.max))
                    link(nc.vector.tensor_reduce(mx[:, s, 1:2], psum[0:TH, 3 * s + 2, 0:418], AX.X, ALU.max))
                    link(nc.vector.tensor_tensor(mx[:, s, 0:1], mx[:, s, 0:1], mx[:, s, 1:2], ALU.max))
                    nc.vector.tensor_scalar(nm[:, s, 0:1], mx[:, s, 0:1], -0.125, None, ALU.mult).then_inc(mxs, 1)

                def take(u):
                    i, h = units[u]
                    s = u % 2
                    dve.wait_ge(ex, 2 * (u + 1))
                    link(nc.vector.tensor_tensor(rs[:, s, 0:1], sm[:, s, 0:1], sm[:, s, 1:2], ALU.add))
                    link(nc.vector.reciprocal(rs[:, s, 0:1], rs[:, s, 0:1]))
                    dve.wait_ge(pv, u + 1)
                    nc.vector.tensor_scalar(ctxs[:, i, h * DH:(h + 1) * DH], psum[0:TH, 3 * s + 2, 440:440 + DH], rs[:, s, 0:1],
                                            None, ALU.mult).then_inc(cx, 1)

                def finish_mix(u, place):
                    for step in steps(u, place):
                        if step % KC != KC - 1:
                            continue
                        t, h = divmod(step // KC, 2)
                        cols = slice(h * HALF, (h + 1) * HALF)
                        m = mixed[t % 2][:, cols]
                        if h == 0 and t >= 2:
                            dve.wait_ge(mst[t % 2], 16 * (t // 2))
                        if h == 0:
                            dve.wait_ge(hld[t % 2], 16 * (t // 2 + 1))
                        dve.wait_ge(gm, 2 * t + h + 1)
                        nc.vector.tensor_tensor(m, psum[0:NT, 7, 0:HALF], bias[:, cols], ALU.add).then_inc(gb, 1)
                        dve.wait_ge(gb, 2 * t + h + 1)
                        link(nc.vector.scalar_tensor_tensor(m, pooled_w[:, cols], score[:, t:t + 1], m, ALU.mult, ALU.add))
                        nc.vector.scalar_tensor_tensor(m, m, unrouted[:, t:t + 1], base[t % 2][:, cols], ALU.mult, ALU.add).then_inc(gt, 1)

                def low(k):
                    dve.wait_ge(hi, k + 1)
                    nc.vector.tensor_tensor(wl[:, k, :], wraw[k % 2][:, :], wh[:, k, :].bitcast(F32), ALU.subtract).then_inc(lo, 1)

                maximum(0)
                dve.wait_ge(bl, 16)
                for u in range(U):
                    for k in range(2 * u, min(2 * u + 2, KC)):
                        low(k)
                    finish_mix(u, 0)
                    if u + 1 < U:
                        maximum(u + 1)
                    finish_mix(u, 1)
                    finish_mix(u, 2)
                    take(u)

    with ExitStack() as ctx:
        sb = allocate(ctx)
        hh, hl = sb("n_high", [128, KC, N], F32R), sb("n_low", [128, KC, N], F32R)
        bias = sb("mv_bias", [NT, D])
        rows_block("wv_", nrm, hh, hl, a["L0_ffn_Wv"],
                   lambda dve, link, t, rows: nc.vector.tensor_tensor(halves(v[:, t, :]), rows, halves(bias[:, :]), ALU.add),
                   loads=[(bias[:, :], spread(a["L0_ffn_bv"], NT))])
        cols_block("wk_", hh, hl, a["L0_ffn_Wk"], KC, a["L0_ffn_bk"],
                   lambda o, cols, got, b: nc.scalar.activation(kt[:, o, cols], got, ACT.Identity, bias=b))
        attention_block(hh, hl, bias)

    hf, n2 = gn, acc

    def merge_block():
        with ExitStack() as ctx:
            sb = allocate(ctx)
            wo, bo = sb("wo", [128, KC, D]), sb("bo", [TH, D])
            ctxt, ao = sb("ctxt", [128, KC, TOP]), sb("ao", [TH, 2, D])
            aoh, aol = sb("ao_high", [TH, 2, D], F32R), sb("ao_low", [TH, 2, D], F32R)
            selt = sb("selt", [TH, 2, N], F32R)
            rrow, iotaj = sb("rank_row", [TH, N]), sb("iota_rows", [TH, 2])
            ldr, co, sl = sem("mg_ranks_loaded"), sem("mg_const"), sem("mg_selector")
            ld, ldh, tr, tc, om, oe, mm, ev, ch = (sem("mg_" + n) for n in (
                "loaded", "rows_loaded", "transposed", "copied", "out_product", "out_taken", "merged", "taken", "chain"))
            wld = sems("wo_loaded", 2)
            block = ctx.enter_context(nc.Block())

            @block.sync
            def _(sp):
                sp.dma_start(rrow[:, :], spread(scr["rank"], TH)).then_inc(ldr, 16)
                for g in range(2):
                    sp.dma_start(wo[:, 3 * g:3 * g + 3, :], chunked(a["L0_ffn_Wo"])[:, 3 * g:3 * g + 3, :]).then_inc(wld[g], 16)
                sp.dma_start(bo[:, :], spread(a["L0_ffn_bo"], TH)).then_inc(ld, 16)
                sp.dma_start(hf, tiled(scr["mix"])).then_inc(ldh, 16)

            @block.gpsimd
            def _(pool):
                pool.iota(iotaj[:, :], pattern=[[TH, 2]], base=0, channel_multiplier=1,
                          allow_small_or_imprecise_dtypes=True).then_inc(co, 1)

            @block.tensor
            def _(pe):
                for i in range(2):
                    for k in range(KC):
                        last = nc.tensor.transpose(psum[:, 4 + k // 2, (k % 2) * TOP + i * TH:(k % 2) * TOP + (i + 1) * TH],
                                                   ctxs[:, i, k * 128:(k + 1) * 128], ident[0:TH, 0:TH])
                last.then_inc(tr, 1)
                pe.wait_ge(tc, 1)
                for k in range(KC):
                    if k % 3 == 0:
                        pe.wait_ge(wld[k // 3], 16)
                    for i in range(2):
                        for h in range(2):
                            last = nc.tensor.matmul(psum[0:TH, 2 * i + h, 0:HALF], ctxt[:, k, i * TH:(i + 1) * TH],
                                                    wo[:, k, h * HALF:(h + 1) * HALF], start=(k == 0), stop=(k == KC - 1))
                last.then_inc(om, 1)
                pe.wait_ge(oe, 2)
                pe.wait_ge(sl, 2)
                for t in range(T):
                    if t >= 4:
                        pe.wait_ge(ev, t - 3)
                    for i in range(2):
                        for h in range(2):
                            for g, part in enumerate((aoh, aol)):
                                last = nc.tensor.matmul(psum[0:NT, 2 * (t % 4) + h, 0:HALF], selt[:, i, t * NT:(t + 1) * NT],
                                                        part[:, i, h * HALF:(h + 1) * HALF],
                                                        start=(i == 0 and g == 0), stop=(i == 1 and g == 1))
                    last.then_inc(mm, 1)

            @block.vector
            def _(dve):
                link = Chain(dve, ch)
                dve.wait_ge(tr, 1)
                nc.vector.tensor_copy(ctxt[:, :, :].rearrange("p (a b) n -> p a (b n)", a=3), psum[:, 4:7, 0:2 * TOP]).then_inc(tc, 1)
                dve.wait_ge(ldr, 16)
                dve.wait_ge(co, 1)
                for i in range(2):
                    nc.vector.tensor_scalar(selt[:, i, :], rrow[:, :], iotaj[:, i:i + 1], None, ALU.is_equal).then_inc(sl, 1)
                dve.wait_ge(om, 1)
                dve.wait_ge(ld, 16)
                for i in range(2):
                    link(nc.vector.tensor_tensor(halves(ao[:, i, :]), wide(i, rows=TH), halves(bo[:, :]), ALU.add))
                    link(nc.vector.tensor_copy(aoh[:, i, :], ao[:, i, :]))
                    nc.vector.tensor_tensor(aol[:, i, :], ao[:, i, :], aoh[:, i, :].bitcast(F32), ALU.subtract).then_inc(oe, 1)
                dve.wait_ge(ldh, 16)
                for t in range(T):
                    dve.wait_ge(mm, t + 1)
                    nc.vector.tensor_tensor(halves(hf[:, t, :]), halves(hf[:, t, :]), wide(t % 4), ALU.add).then_inc(ev, 1)
                    dve.wait_ge(ev, t + 1)
                    link(stats(link, hf, row_parts, row_mv, t))

    merge_block()
    keep.close()
    affine_norm("ln_2", hf, n2, a["L0_ffn_g2"], a["L0_ffn_b2"], row_mv)

    with ExitStack() as ctx:
        sb = allocate(ctx)
        fh, fl2 = sb("f_high", [128, FK, N], F32R), sb("f_low", [128, FK, N], F32R)
        with ExitStack() as c2:
            sb2 = allocate(c2)
            hh, hl = sb2("n2_high", [128, KC, N], F32R), sb2("n2_low", [128, KC, N], F32R)
            transpose_block("tr_n2", n2, hh, hl)
            f = room[0][:, 0:FK * N].rearrange("p (k n) -> p k n", k=FK)

            def split_f(link, o, cols):
                link(nc.vector.tensor_copy(fh[:, o, cols], f[:, o, cols]))
                nc.vector.tensor_tensor(fl2[:, o, cols], f[:, o, cols], fh[:, o, cols].bitcast(F32), ALU.subtract)

            cols_block("w1_", hh, hl, a["L0_ffn_W1"], FK, a["L0_ffn_bf1"],
                       lambda o, cols, got, b: nc.scalar.activation(f[:, o, cols], got, ACT.Gelu, bias=b), then=split_f)

        bias = sb("f2_bias", [NT, D])
        x1 = sb("x1", [NT, 3, D])

        def last_sink(dve, link, t, rows):
            link(nc.vector.tensor_tensor(halves(hf[:, t, :]), halves(hf[:, t, :]), rows, ALU.add))
            link(nc.vector.tensor_tensor(hf[:, t, :], hf[:, t, :], bias[:, :], ALU.add))
            return nc.vector.tensor_tensor(hf[:, t, :], hf[:, t, :], x1[:, t % 3, :], ALU.add)

        rows_block("w2_", None, fh, fl2, a["L0_ffn_W2"], last_sink, kc=FK, loads=[(bias[:, :], spread(a["L0_ffn_bf2"], NT))],
                   tile_load=lambda t: (x1[:, t % 3, :], scr["x1"][t * NT:(t + 1) * NT, :]),
                   store=lambda t: (out[t * NT:(t + 1) * NT, :], hf[:, t, :]))


def kernel(**inputs):
    import numpy as np
    import concourse.bacc as bacc
    from concourse import mybir
    from concourse.bass_utils import run_bass_kernel_spmd as run

    nc = bacc.Bacc("TRN2", target_bir_lowering=False, num_devices=1)
    arrays, a = {}, {}
    for name, value in inputs.items():
        v = np.ascontiguousarray(value)
        v = v.reshape(v.shape or (1,))
        arrays["in_" + name] = v
        a[name] = nc.dram_tensor("in_" + name, v.shape, mybir.dt.from_np(v.dtype), kind="ExternalInput").ap()
    out = nc.dram_tensor("out", (N, D), F32, kind="ExternalOutput").ap()
    scr = {name: nc.dram_tensor("scratch_" + name, shape, F32, kind="Internal").ap() for name, shape in SCRATCH.items()}
    build(nc, a, out, scr)
    r = run(nc, [arrays], core_ids=[0])
    return r.results[0]["out"]
```
